# Optimizing a Trainium2 kernel written in Bass

```python
import numpy as np
import jax
import jax.numpy as jnp

def _softmax(x, axis=-1):
    return jax.nn.softmax(x, axis=axis)

def _gelu(x):
    return jax.nn.gelu(x, approximate=True)

def _silu(x):
    return jax.nn.silu(x)

def _sigmoid(x):
    return jax.nn.sigmoid(x)

def _layernorm(x, axis=-1, eps=1e-05):
    m = jnp.mean(x, axis=axis, keepdims=True)
    v = jnp.var(x, axis=axis, keepdims=True)
    return (x - m) / jnp.sqrt(v + eps)

def _scatter_add(tgt, idx, src, axis=0):
    return tgt.at[idx].add(src)

def _segment_sum(src, seg, n):
    return jax.ops.segment_sum(src, seg, n)
kernel_name = 'mk_gnn_resnorm_d4_gnn_r16_e486f7'

def setup_inputs(seed: int=0):
    np.random.seed(seed)
    _w = jnp.asarray

    def _rec_inputs():
        import jax
        import jax.numpy as jnp
        _gk = jax.random.key(seed)
        x = -0.0008691 + 1 * jax.random.normal(jax.random.fold_in(_gk, 1), (3125, 128), jnp.float32)
        src = jax.random.randint(jax.random.fold_in(_gk, 2), (50000,), 0, 3125, jnp.int32)
        dst = jax.random.randint(jax.random.fold_in(_gk, 3), (50000,), 0, 3125, jnp.int32)
        _o = jnp.argsort(dst, stable=True)
        src = src[_o]
        dst = dst[_o]
        edge_type_9 = jax.random.randint(jax.random.fold_in(_gk, 12), (50000,), 0, 9, jnp.int32)
        return (x, src, dst, edge_type_9)
    x, src, dst, edge_type_9 = _rec_inputs()

    def _L0_gnn_setup():
        import jax, jax.numpy as jnp
        import numpy as np
        EPS = 1e-05
        N_NODES = 625

        def gcn_norm(src, dst, n):
            deg = jax.ops.segment_sum(jnp.ones(src.shape[0], jnp.float32), dst, num_segments=n)
            dinv = jnp.where(deg > 0, jax.lax.rsqrt(jnp.maximum(deg, 1.0)), 0.0)
            return dinv[src] * dinv[dst]

        def arma_conv(x, src, dst, norm, init_w, w, root_w, bias, n):
            T = root_w.shape[0]
            out = None
            for t in range(T):
                if t == 0:
                    h = jnp.einsum('nf,kfg->kng', x, init_w)
                else:
                    h = jnp.einsum('kng,kgh->knh', out, w[t - 1])
                msg = h[:, src, :] * norm[None, :, None]
                agg = jax.ops.segment_sum(jnp.swapaxes(msg, 0, 1), dst, num_segments=n)
                h = jnp.swapaxes(agg, 0, 1)
                h = h + jnp.einsum('nf,kfg->kng', x, root_w[t]) + bias[t]
                out = jax.nn.relu(h)
            return out.mean(axis=0)

        def batchnorm(x, gamma, beta):
            m = x.mean(axis=0)
            v = x.var(axis=0)
            return (x - m) * jax.lax.rsqrt(v + EPS) * gamma + beta
        key = jax.random.key(seed)
        ks = jax.random.split(key, 12)
        n, e, fin, hid, fout, K = (N_NODES, 20000, 128, 256, 128, 3)
        s = 0.05
        return {'x': jax.random.normal(ks[0], (n, fin), jnp.float32), 'edge_index': jax.random.randint(ks[1], (2, e), 0, n, jnp.int64), 'init_w1': jax.random.normal(ks[2], (K, fin, hid), jnp.float32) * s, 'w1': jax.random.normal(ks[3], (1, K, hid, hid), jnp.float32) * s, 'root_w1': jax.random.normal(ks[4], (2, K, fin, hid), jnp.float32) * s, 'b1': jax.random.normal(ks[5], (2, K, 1, hid), jnp.float32) * s, 'init_w2': jax.random.normal(ks[6], (K, hid, fout), jnp.float32) * s, 'w2': jax.random.normal(ks[7], (1, K, fout, fout), jnp.float32) * s, 'root_w2': jax.random.normal(ks[8], (2, K, hid, fout), jnp.float32) * s, 'b2': jax.random.normal(ks[9], (2, K, 1, fout), jnp.float32) * s, 'gamma1': jnp.ones((hid,), jnp.float32), 'beta1': jnp.zeros((hid,), jnp.float32), 'gamma2': jnp.ones((fout,), jnp.float32), 'beta2': jnp.zeros((fout,), jnp.float32)}
    _L0_gnn_all = _L0_gnn_setup()
    _L0_gnn_in = {k: v for k, v in _L0_gnn_all.items() if k in ('init_w1', 'w1', 'root_w1', 'b1', 'init_w2', 'w2', 'root_w2', 'b2', 'gamma1', 'beta1', 'gamma2', 'beta2')}
    del _L0_gnn_all

    def _L1_gnn_setup():
        import jax, jax.numpy as jnp
        import numpy as np
        N = 6250
        E = 100000
        D_IN = 128
        D_OUT = 128
        key = jax.random.key(seed)
        k1, k2, k3, k4 = jax.random.split(key, 4)
        x = jax.random.normal(k1, (N, D_IN), dtype=jnp.float32)
        edge_index = jax.random.randint(k2, (2, E), 0, N, dtype=jnp.int64)
        scale = jnp.sqrt(6.0 / (D_IN + D_OUT)).astype(jnp.float32)
        W = jax.random.uniform(k3, (D_IN, D_OUT), dtype=jnp.float32, minval=-scale, maxval=scale)
        b = jnp.zeros((D_OUT,), dtype=jnp.float32)
        return {'x': x, 'edge_index': edge_index, 'W': W, 'b': b}
    _L1_gnn_all = _L1_gnn_setup()
    _L1_gnn_in = {k: v for k, v in _L1_gnn_all.items() if k in ('W', 'b')}
    del _L1_gnn_all

    def _L2_gnn_setup():
        import jax, jax.numpy as jnp
        import numpy as np
        N_NODES = 3125
        EMB = 128
        N_REL = 9
        N_EDGES = 50000
        N_LAYERS = 2
        key = jax.random.key(seed)
        k1, k2, k3, k4, k5 = jax.random.split(key, 5)
        edge_index = jax.random.randint(k1, (2, N_EDGES), 0, N_NODES)
        edge_type = jax.random.randint(k2, (N_EDGES,), 0, N_REL)
        embeddings = jax.random.normal(k3, (N_NODES, EMB), dtype=jnp.float32)
        rgcn_weights = jax.random.uniform(k4, (N_LAYERS, 2 * N_REL + 1, EMB, EMB), dtype=jnp.float32) * 0.02
        rgcn_biases = jax.random.uniform(k5, (N_LAYERS, 2 * N_REL + 1, EMB), dtype=jnp.float32) * 0.02
        return {'edge_index': edge_index, 'edge_type': edge_type, 'embeddings': embeddings, 'rgcn_weights': rgcn_weights, 'rgcn_biases': rgcn_biases}
    _L2_gnn_all = _L2_gnn_setup()
    _L2_gnn_in = {k: v for k, v in _L2_gnn_all.items() if k in ('rgcn_weights', 'rgcn_biases')}
    del _L2_gnn_all

    def _L3_gnn_setup():
        import jax, jax.numpy as jnp
        import numpy as np
        NUM_NODES = 6250
        NUM_EDGES = 100000
        IN_DIM = 128
        OUT_DIM = 128
        key = jax.random.key(seed)
        k_x, k_e, k_wn, k_bn, k_ws, k_bs = jax.random.split(key, 6)
        x = jax.random.normal(k_x, (NUM_NODES, IN_DIM), dtype=jnp.float32)
        edge_index = jax.random.randint(k_e, (2, NUM_EDGES), 0, NUM_NODES, dtype=jnp.int64)
        s = 1.0 / np.sqrt(IN_DIM)
        W_neigh = jax.random.uniform(k_wn, (OUT_DIM, IN_DIM), dtype=jnp.float32, minval=-s, maxval=s)
        b_neigh = jax.random.uniform(k_bn, (OUT_DIM,), dtype=jnp.float32, minval=-s, maxval=s)
        W_self = jax.random.uniform(k_ws, (OUT_DIM, IN_DIM), dtype=jnp.float32, minval=-s, maxval=s)
        b_self = jax.random.uniform(k_bs, (OUT_DIM,), dtype=jnp.float32, minval=-s, maxval=s)
        return {'x': x, 'edge_index': edge_index, 'W_neigh': W_neigh, 'b_neigh': b_neigh, 'W_self': W_self, 'b_self': b_self}
    _L3_gnn_all = _L3_gnn_setup()
    _L3_gnn_in = {k: v for k, v in _L3_gnn_all.items() if k in ('W_neigh', 'b_neigh', 'W_self', 'b_self')}
    del _L3_gnn_all
    return {'x': x, 'src': src, 'dst': dst, 'edge_type_9': edge_type_9, 'L0_gnn_init_w1': _L0_gnn_in['init_w1'], 'L0_gnn_w1': _L0_gnn_in['w1'], 'L0_gnn_root_w1': _L0_gnn_in['root_w1'], 'L0_gnn_b1': _L0_gnn_in['b1'], 'L0_gnn_init_w2': _L0_gnn_in['init_w2'], 'L0_gnn_w2': _L0_gnn_in['w2'], 'L0_gnn_root_w2': _L0_gnn_in['root_w2'], 'L0_gnn_b2': _L0_gnn_in['b2'], 'L0_gnn_gamma1': _L0_gnn_in['gamma1'], 'L0_gnn_beta1': _L0_gnn_in['beta1'], 'L0_gnn_gamma2': _L0_gnn_in['gamma2'], 'L0_gnn_beta2': _L0_gnn_in['beta2'], 'L1_gnn_W': _L1_gnn_in['W'], 'L1_gnn_b': _L1_gnn_in['b'], 'L2_gnn_rgcn_weights': _L2_gnn_in['rgcn_weights'], 'L2_gnn_rgcn_biases': _L2_gnn_in['rgcn_biases'], 'L3_gnn_W_neigh': _L3_gnn_in['W_neigh'], 'L3_gnn_b_neigh': _L3_gnn_in['b_neigh'], 'L3_gnn_W_self': _L3_gnn_in['W_self'], 'L3_gnn_b_self': _L3_gnn_in['b_self']}

def reference(x, src, dst, edge_type_9, L0_gnn_init_w1, L0_gnn_w1, L0_gnn_root_w1, L0_gnn_b1, L0_gnn_init_w2, L0_gnn_w2, L0_gnn_root_w2, L0_gnn_b2, L0_gnn_gamma1, L0_gnn_beta1, L0_gnn_gamma2, L0_gnn_beta2, L1_gnn_W, L1_gnn_b, L2_gnn_rgcn_weights, L2_gnn_rgcn_biases, L3_gnn_W_neigh, L3_gnn_b_neigh, L3_gnn_W_self, L3_gnn_b_self):
    import jax
    import jax.numpy as jnp

    def _L0_gnn_ref(x, edge_index, init_w1, w1, root_w1, b1, init_w2, w2, root_w2, b2, gamma1, beta1, gamma2, beta2):
        import jax, jax.numpy as jnp
        import numpy as np
        EPS = 1e-05
        N_NODES = 625

        def gcn_norm(src, dst, n):
            deg = jax.ops.segment_sum(jnp.ones(src.shape[0], jnp.float32), dst, num_segments=n)
            dinv = jnp.where(deg > 0, jax.lax.rsqrt(jnp.maximum(deg, 1.0)), 0.0)
            return dinv[src] * dinv[dst]

        def arma_conv(x, src, dst, norm, init_w, w, root_w, bias, n):
            T = root_w.shape[0]
            out = None
            for t in range(T):
                if t == 0:
                    h = jnp.einsum('nf,kfg->kng', x, init_w)
                else:
                    h = jnp.einsum('kng,kgh->knh', out, w[t - 1])
                msg = h[:, src, :] * norm[None, :, None]
                agg = jax.ops.segment_sum(jnp.swapaxes(msg, 0, 1), dst, num_segments=n)
                h = jnp.swapaxes(agg, 0, 1)
                h = h + jnp.einsum('nf,kfg->kng', x, root_w[t]) + bias[t]
                out = jax.nn.relu(h)
            return out.mean(axis=0)

        def batchnorm(x, gamma, beta):
            m = x.mean(axis=0)
            v = x.var(axis=0)
            return (x - m) * jax.lax.rsqrt(v + EPS) * gamma + beta
        n = x.shape[0]
        src, dst = (edge_index[0], edge_index[1])
        norm = gcn_norm(src, dst, n)
        h = arma_conv(x, src, dst, norm, init_w1, w1, root_w1, b1, n)
        h = jax.nn.relu(batchnorm(h, gamma1, beta1))
        h = arma_conv(h, src, dst, norm, init_w2, w2, root_w2, b2, n)
        h = jax.nn.relu(batchnorm(h, gamma2, beta2))
        return h

    def _L1_gnn_ref(x, edge_index, W, b):
        import jax, jax.numpy as jnp
        import numpy as np
        N = 6250
        E = 100000
        D_IN = 128
        D_OUT = 128
        n = x.shape[0]
        loops = jnp.arange(n, dtype=edge_index.dtype)
        src = jnp.concatenate([edge_index[0], loops])
        dst = jnp.concatenate([edge_index[1], loops])
        ones = jnp.ones_like(dst, dtype=x.dtype)
        deg = jax.ops.segment_sum(ones, dst, num_segments=n)
        dinv = jnp.where(deg > 0, jax.lax.rsqrt(deg), 0.0)
        norm = dinv[src] * dinv[dst]
        h = x @ W
        msgs = h[src] * norm[:, None]
        out = jax.ops.segment_sum(msgs, dst, num_segments=n)
        return out + b

    def _L2_gnn_ref(edge_index, edge_type, embeddings, rgcn_weights, rgcn_biases):
        import jax, jax.numpy as jnp
        import numpy as np
        N_NODES = 3125
        EMB = 128
        N_REL = 9
        N_EDGES = 50000
        N_LAYERS = 2
        n = embeddings.shape[0]
        R = N_REL
        seg = jnp.concatenate([edge_type * n + edge_index[0], (edge_type + R) * n + edge_index[1]])
        srcs = jnp.concatenate([edge_index[1], edge_index[0]])
        ones = jnp.ones(seg.shape, embeddings.dtype)
        count = jax.ops.segment_sum(ones, seg, num_segments=2 * R * n).reshape(2 * R, n, 1)
        cnt = jnp.maximum(count, 1.0)
        output = embeddings
        for l in range(N_LAYERS):
            W, b = (rgcn_weights[l], rgcn_biases[l])
            agg = jax.ops.segment_sum(output[srcs], seg, num_segments=2 * R * n)
            agg = agg.reshape(2 * R, n, -1)
            hidden = output @ W[-1] + b[-1]
            for r in range(R):
                for inv in (0, 1):
                    s = r + R * inv
                    msum = agg[s] @ W[s] + count[s] * b[s]
                    hidden = 2.0 * (hidden + msum) / cnt[s]
            if l + 1 < N_LAYERS:
                hidden = jax.nn.relu(hidden)
            output = hidden
        return output

    def _L3_gnn_ref(x, edge_index, W_neigh, b_neigh, W_self, b_self):
        import jax, jax.numpy as jnp
        import numpy as np
        NUM_NODES = 6250
        NUM_EDGES = 100000
        IN_DIM = 128
        OUT_DIM = 128
        src, dst = (edge_index[0], edge_index[1])
        msgs = x[src]
        neigh = jax.ops.segment_sum(msgs, dst, num_segments=x.shape[0])
        neigh_proj = neigh @ W_neigh.T + b_neigh
        self_proj = x @ W_self.T + b_self
        return neigh_proj + self_proj
    edge_index = jnp.stack([src, dst])
    x = _layernorm(x + _L0_gnn_ref(x, edge_index, L0_gnn_init_w1, L0_gnn_w1, L0_gnn_root_w1, L0_gnn_b1, L0_gnn_init_w2, L0_gnn_w2, L0_gnn_root_w2, L0_gnn_b2, L0_gnn_gamma1, L0_gnn_beta1, L0_gnn_gamma2, L0_gnn_beta2), axis=-1)
    x = _layernorm(x + _L1_gnn_ref(x, edge_index, L1_gnn_W, L1_gnn_b), axis=-1)
    x = _layernorm(x + _L2_gnn_ref(edge_index, edge_type_9, x, L2_gnn_rgcn_weights, L2_gnn_rgcn_biases), axis=-1)
    x = _layernorm(x + _L3_gnn_ref(x, edge_index, L3_gnn_W_neigh, L3_gnn_b_neigh, L3_gnn_W_self, L3_gnn_b_self), axis=-1)
    return x

_drawn_inputs = setup_inputs


def setup_inputs(seed=0):
    import zlib

    import numpy as np

    out = dict(_drawn_inputs(seed))
    spreads = {'L0_gnn_gamma1': (1.0, 0.2),
     'L0_gnn_beta1': (0.0, 0.295),
     'L0_gnn_gamma2': (1.0, 0.2),
     'L0_gnn_beta2': (0.0, 0.1),
     'L1_gnn_b': (0.0, 0.1)}
    factors = {'L0_gnn_init_w1': 3.201,
     'L0_gnn_b2': 3.539,
     'L3_gnn_b_neigh': 4.466,
     'L3_gnn_b_self': 3.889}
    for name, (base, spread) in spreads.items():
        noise = np.random.default_rng([zlib.crc32(name.encode()), seed]).standard_normal(out[name].shape)
        drawn = base * np.exp(spread * noise) if base else spread * noise
        out[name] = jnp.asarray(drawn.astype(out[name].dtype))
    for name, factor in factors.items():
        out[name] = (out[name] * factor).astype(out[name].dtype)
    return out
```

```python
import concourse.bass as bass
from concourse import mybir
from contextlib import ExitStack

F32, BF16, FP16, I32 = mybir.dt.float32, mybir.dt.bfloat16, mybir.dt.float16, mybir.dt.int32
PE, DVE = mybir.EngineType.PE, mybir.EngineType.DVE
ALU, ACT, AX = mybir.AluOpType, mybir.ActivationFunctionType, mybir.AxisListType

P = 128
N = 3125
E = 50000
D = 128
R = 9
K = 3
HID = 256
EPS = 1e-5
NT = -(-N // P)
NP = NT * P
LAST = N - (NT - 1) * P
EP = 125
EC = E // EP
U = 16
C = -(-(E // P + NT + 1) // U) * U
S2 = 2 * R
J = 5
TURNS = NT // J
LEAD = 8


class Chip:
    pass


class Stage(ExitStack):

    def __init__(self, nc, tag):
        super().__init__()
        self.nc, self.tag = nc, tag

    def sb(self, name, shape, dt=F32):
        return self.enter_context(self.nc.sbuf_tensor(f"{name}_{self.tag}", shape, dt))

    def psum(self, name, shape, dt=F32):
        return self.enter_context(self.nc.psum_tensor(f"{name}_{self.tag}", shape, dt))

    def sems(self, *names):
        sems = [self.nc.alloc_semaphore(f"{n}_{self.tag}") for n in names]
        self.callback(self.give_back, sems)
        return sems

    def give_back(self, sems):
        for s in sems:
            self.nc.sync.sem_clear(s)
            self.nc.release_semaphore(s)

    def block(self):
        return self.enter_context(self.nc.Block())


def ts(i, n=P):
    return bass.ds(i * n, n)


def pair_free(i, j):
    return i * J + 2 + (0 if j == 0 else -1 if j == 1 else j - 1)



def load_stage(nc, k, A):
    with Stage(nc, "load") as c:
        loaded, zeroed, made = c.sems("loaded", "zeroed", "made")
        block = c.block()

        @block.sync
        def _(sp):
            sp.wait_ge(zeroed, 1)
            sp.dma_start(k.xcur[:, 0:NT - 1, :],
                         A["x"][0:(NT - 1) * P, :].rearrange("(t p) f -> p t f", p=P)).then_inc(loaded, 16)
            sp.dma_start(k.xcur[0:LAST, NT - 1, :], A["x"][(NT - 1) * P:N, :]).then_inc(loaded, 16)
            sp.wait_ge(loaded, 16 * 5)

        @block.scalar
        def _(act):
            for i, name in enumerate(("src", "dst", "edge_type_9")):
                act.dma_start(k.edges[0:EP, i, :], A[name].rearrange("(p c) -> p c", p=EP)).then_inc(loaded, 16)

        @block.vector
        def _(dve):
            nc.vector.memset(k.xcur[:, :, :], 0.0).then_inc(zeroed, 1)
            nc.vector.memset(k.onerow[:, :], 1.0)

        @block.gpsimd
        def _(gp):
            nc.gpsimd.iota(k.iota[:, :], [[1, C]], base=0, channel_multiplier=0,
                           allow_small_or_imprecise_dtypes=True)
            nc.gpsimd.iota(k.iota16[:, :], [[1, C]], base=0, channel_multiplier=0,
                           allow_small_or_imprecise_dtypes=True)
            nc.gpsimd.iota(k.diff[:, :], [[1, P]], base=0, channel_multiplier=-1,
                           allow_small_or_imprecise_dtypes=True).then_inc(made, 1)
            gp.wait_ge(made, 1)
            nc.gpsimd.tensor_scalar(k.ident[:, :], k.diff[:, :], 0.0, None, ALU.is_equal)



def rank_stage(nc, k, o):
    other = 1 - o.key
    B = 4
    W = 500
    BLOCKS = NT * EC // W
    with Stage(nc, f"rank{o.key}") as c:
        sb = c.sb
        ps = c.psum("ps", [P, 8, 512])
        ints = sb("ints", [P, 4, EC], I32)
        tile_of = sb("tile_of", [P, EC], F32)
        one_hot = sb("tile_one_hot", [P, NT, EC], BF16)
        ones = sb("ones_bf", [P, P], BF16)
        triangle = sb("triangle", [P, P], BF16)
        total = sb("column_total", [P, NT * EC], F32)
        upto = sb("edges_up_to", [P, NT * EC], F32)
        cum = sb("cum", [P, NT + 1], F32)
        size = sb("size", [P, NT], F32)
        sizei = sb("sizei", [P, NT], I32)
        first = sb("first_chunk", [P, NT + 1], F32)
        shift = sb("shift", [P, NT], F32)
        pos = sb("pos", [P, EC], F32)
        tl = sb("tile_of_chunk", [P, C], F32)
        step, counted, kept, ranked = c.sems("step", "counted", "kept", "ranked")
        block = c.block()
        flat = one_hot[:, :, :].rearrange("p b c -> p (b c)")

        @block.vector
        def _(dve):
            done = 0

            def then(inst):
                nonlocal done
                done += 1
                inst.then_inc(step, 1)
                dve.wait_ge(step, done)

            key = k.edges[0:EP, o.key, :]
            e = slice(0, EP)
            nc.vector.tensor_single_scalar(ints[e, 0, :], key, 7, ALU.arith_shift_right)
            then(nc.vector.tensor_single_scalar(ints[e, 1, :], key, P - 1, ALU.bitwise_and))
            nc.vector.tensor_copy(o.local_in[e, :], ints[e, 1, :])
            then(nc.vector.tensor_scalar(pos[e, :], k.edges[e, other, :], float(R), None, ALU.mult))
            then(nc.vector.tensor_tensor(pos[e, :], pos[e, :], k.edges[e, 2, :], ALU.add))
            then(nc.vector.tensor_scalar(pos[e, :], pos[e, :], float(P), 1.0, ALU.mult, ALU.add))
            then(nc.vector.tensor_tensor(ints[e, 2, :], pos[e, :], o.local_in[e, :], ALU.add))
            nc.vector.tensor_single_scalar(ints[e, 3, :], ints[e, 2, :], 11, ALU.arith_shift_right)
            then(nc.vector.tensor_single_scalar(ints[e, 2, :], ints[e, 2, :], 2047, ALU.bitwise_and))
            nc.vector.tensor_copy(o.high_in[e, :], ints[e, 3, :])
            nc.vector.tensor_copy(o.low_in[e, :], ints[e, 2, :])
            then(nc.vector.tensor_copy(tile_of[e, :], ints[e, 0, :]))
            nc.vector.tensor_scalar(o.group_in[e, :], tile_of[e, :], float(R), None, ALU.mult)
            nc.vector.memset(ones[:, :], 1.0)
            nc.vector.tensor_scalar(triangle[:, :], k.diff[:, :], 0.0, 1.0, ALU.is_gt, ALU.subtract)
            then(nc.vector.tensor_tensor(one_hot[e, :, :],
                                         tile_of[e, None, :].to_broadcast([EP, NT, EC]),
                                         k.iota[e, 0:NT, None].to_broadcast([EP, NT, EC]), ALU.is_equal))
            nc.vector.tensor_tensor(o.group_in[e, :], o.group_in[e, :], k.edges[e, 2, :],
                                    ALU.add).then_inc(ranked, 1)
            dve.wait_ge(kept, 1 + BLOCKS // B)
            then(nc.vector.tensor_tensor_scan(upto[:, :], total[:, :], total[:, :], 0.0, ALU.add, ALU.max))
            nc.vector.memset(cum[:, 0:1], 0.0)
            nc.vector.memset(first[:, 0:1], 0.0)
            then(nc.vector.tensor_copy(cum[:, 1:NT + 1],
                                       upto[:, :].rearrange("p (b c) -> p b c", c=EC)[:, :, EC - 1]))
            then(nc.vector.tensor_tensor(size[:, :], cum[:, 1:NT + 1], cum[:, 0:NT], ALU.subtract))
            then(nc.vector.tensor_scalar(sizei[:, :], size[:, :], float(P - 1), None, ALU.add))
            then(nc.vector.tensor_single_scalar(sizei[:, :], sizei[:, :], 7, ALU.arith_shift_right))
            then(nc.vector.tensor_copy(size[:, :], sizei[:, :]))
            then(nc.vector.tensor_tensor_scan(first[:, 1:NT + 1], size[:, :], size[:, :], 0.0, ALU.add, ALU.max))
            then(nc.vector.scalar_tensor_tensor(shift[:, :], first[:, 0:NT], float(P), cum[:, 0:NT],
                                                ALU.mult, ALU.subtract))
            then(nc.vector.tensor_tensor(upto[:, :].rearrange("p (b c) -> p b c", c=EC),
                                         upto[:, :].rearrange("p (b c) -> p b c", c=EC),
                                         shift[:, :, None].to_broadcast([P, NT, EC]), ALU.add))
            with dve.Fori(0, BLOCKS // B) as i:
                dve.wait_ge(counted, i * B + B + BLOCKS)
                for b in range(B):
                    last = nc.vector.tensor_tensor(
                        upto[0:EP, bass.ds((i * B + b) * W, W)], upto[0:EP, bass.ds((i * B + b) * W, W)],
                        ps[0:EP, 4 + b, 0:W], ALU.add)
                last.then_inc(ranked, 1)
            dve.wait_ge(ranked, 1 + BLOCKS // B)
            then(nc.vector.tensor_tensor(total[e, :], upto[e, :], flat[e, :], ALU.mult))
            then(nc.vector.tensor_reduce(pos[e, :], total[e, :].rearrange("p (b c) -> p c b", c=EC),
                                         AX.X, ALU.add))
            then(nc.vector.tensor_copy(ints[e, 0, :], pos[e, :]))
            nc.vector.tensor_single_scalar(ints[e, 1, :], ints[e, 0, :], P - 1, ALU.bitwise_and)
            then(nc.vector.tensor_single_scalar(ints[e, 2, :], ints[e, 0, :], 7, ALU.arith_shift_right))
            nc.vector.tensor_copy(o.slot_in[e, :], ints[e, 1, :])
            nc.vector.tensor_copy(o.chunk_in[e, :], ints[e, 2, :])
            then(nc.vector.memset(tl[:, :], 0.0))
            for b in range(NT):
                then(nc.vector.scalar_tensor_tensor(tl[:, :], k.iota[:, 0:C], first[:, b + 1:b + 2], tl[:, :],
                                                    ALU.is_ge, ALU.add))
            then(nc.vector.tensor_scalar_min(o.tile_of_chunk[:, :], tl[:, :], float(NT - 1)))

        @block.tensor
        def _(pe):
            pe.wait_ge(ranked, 1)
            with pe.Fori(0, BLOCKS // B) as i:
                pe.wait_ge(kept, i + 1)
                for b in range(B):
                    nc.tensor.matmul(ps[:, b, 0:W], ones[0:EP, :], flat[0:EP, bass.ds((i * B + b) * W, W)],
                                     start=True, stop=True).then_inc(counted, 1)
            with pe.Fori(0, BLOCKS // B) as i:
                pe.wait_ge(ranked, 1 + i)
                for b in range(B):
                    nc.tensor.matmul(ps[0:EP, 4 + b, 0:W], triangle[0:EP, 0:EP],
                                     flat[0:EP, bass.ds((i * B + b) * W, W)],
                                     start=True, stop=True).then_inc(counted, 1)

        @block.scalar
        def _(act):
            nc.scalar.sem_inc(kept, 1)
            with act.Fori(0, BLOCKS // B) as i:
                act.wait_ge(counted, i * B + B)
                for b in range(B):
                    last = nc.scalar.copy(total[:, bass.ds((i * B + b) * W, W)], ps[:, b, 0:W])
                last.then_inc(kept, 1)


def permute_stage(nc, k, o):
    G = NT * R
    V = 4
    with Stage(nc, f"permute{o.key}") as c:
        sb = c.sb
        ps = c.psum("ps", [P, 3, 512])
        zero = sb("zero", [1, 512], FP16)
        chunk = sb("chunk_one_hot", [P, V, C], FP16)
        slot = sb("slot_one_hot", [P, V, 2, P], FP16)
        local = sb("local_one_hot", [P, V, P], FP16)
        group = sb("group_one_hot", [P, V, G], FP16)
        codes = sb("codes", [P, C], F32)
        codei = sb("codei", [P, 2, C], I32)
        filled = sb("filled", [P, C], F32)
        other = sb("other", [P, C], F32)
        otheri = sb("otheri", [P, C], I32)
        over = sb("over", [P, C], F32)
        zeroed, column, moved, step = c.sems("zeroed", "column", "moved", "step")
        block = c.block()
        e = slice(0, EP)

        @block.vector
        def _(dve):
            nc.vector.memset(zero[:, :], 0.0).then_inc(zeroed, 1)
            with dve.Fori(0, EC // V) as i:
                for v in range(V):
                    col = bass.ds(i * V + v, 1)
                    dve.wait_ge(moved, i * V + v + 1)
                    nc.vector.tensor_scalar(chunk[e, v, :], k.iota16[e, 0:C], o.chunk_in[e, col], None,
                                            ALU.is_equal)
                    nc.vector.tensor_scalar(slot[e, v, 0, :], k.iota16[e, 0:P], o.slot_in[e, col],
                                            o.high_in[e, col], ALU.is_equal, ALU.mult)
                    nc.vector.tensor_scalar(slot[e, v, 1, :], k.iota16[e, 0:P], o.slot_in[e, col],
                                            o.low_in[e, col], ALU.is_equal, ALU.mult)
                    nc.vector.tensor_scalar(local[e, v, :], k.iota16[e, 0:P], o.local_in[e, col], None,
                                            ALU.is_equal)
                    nc.vector.tensor_scalar(group[e, v, :], k.iota16[e, 0:G], o.group_in[e, col], None,
                                            ALU.is_equal).then_inc(column, 1)
            dve.wait_ge(moved, V + EC + 1)
            done = 0

            def then(inst):
                nonlocal done
                done += 1
                inst.then_inc(step, 1)
                dve.wait_ge(step, done)

            nc.vector.tensor_copy(k.count[:, :, o.first:o.first + R],
                                  ps[:, 2, 0:G].rearrange("p (t r) -> p t r", r=R))
            then(nc.vector.tensor_scalar(codes[:, :], ps[:, 0, 0:C], 2048.0, None, ALU.mult))
            then(nc.vector.tensor_tensor(codes[:, :], codes[:, :], ps[:, 1, 0:C], ALU.add))
            nc.vector.tensor_scalar(filled[:, :], codes[:, :], 0.0, None, ALU.is_gt)
            then(nc.vector.tensor_scalar(codei[:, 0, :], codes[:, :], -1.0, 0.0, ALU.add, ALU.max))
            then(nc.vector.tensor_single_scalar(codei[:, 1, :], codei[:, 0, :], P - 1, ALU.bitwise_and))
            then(nc.vector.tensor_single_scalar(o.row[:, :], codei[:, 0, :], 7, ALU.arith_shift_right))
            then(nc.vector.tensor_scalar(codes[:, :], codei[:, 1, :], 1.0, None, ALU.add))
            then(nc.vector.tensor_tensor(codes[:, :], codes[:, :], filled[:, :], ALU.mult))
            then(nc.vector.tensor_scalar(o.local[:, :], codes[:, :], -1.0, None, ALU.add))
            then(nc.vector.tensor_scalar(otheri[:, :], o.row[:, :], 1.0 / R, None, ALU.mult))
            then(nc.vector.tensor_copy(other[:, :], otheri[:, :]))
            then(nc.vector.tensor_copy(codes[:, :], o.row[:, :]))
            then(nc.vector.scalar_tensor_tensor(codes[:, :], other[:, :], -float(R), codes[:, :],
                                                ALU.mult, ALU.add))
            then(nc.vector.tensor_scalar(over[:, :], codes[:, :], 0.0, None, ALU.is_lt))
            then(nc.vector.tensor_tensor(other[:, :], other[:, :], over[:, :], ALU.subtract))
            then(nc.vector.scalar_tensor_tensor(codes[:, :], over[:, :], float(R), codes[:, :],
                                                ALU.mult, ALU.add))
            then(nc.vector.tensor_scalar(over[:, :], codes[:, :], float(R), None, ALU.is_ge))
            then(nc.vector.tensor_tensor(o.other[:, :], other[:, :], over[:, :], ALU.add))
            then(nc.vector.scalar_tensor_tensor(o.type[:, :], over[:, :], -float(R), codes[:, :],
                                                ALU.mult, ALU.add))

        @block.tensor
        def _(pe):
            pe.wait_ge(zeroed, 1)
            for b, w in ((0, C), (1, C), (2, G)):
                last = nc.tensor.matmul(ps[:, b, 0:w], zero[0:1, 0:P], zero[0:1, 0:w], start=True, stop=False)
            last.then_inc(moved, V)
            with pe.Fori(0, EC // V) as i:
                for v in range(V):
                    pe.wait_ge(column, i * V + v + 1)
                    nc.tensor.matmul(ps[:, 0, 0:C], slot[e, v, 0, :], chunk[e, v, :], start=False, stop=False)
                    nc.tensor.matmul(ps[:, 1, 0:C], slot[e, v, 1, :], chunk[e, v, :], start=False, stop=False)
                    nc.tensor.matmul(ps[:, 2, 0:G], local[e, v, :], group[e, v, :],
                                     start=False, stop=False).then_inc(moved, 1)
            for b, w in ((0, C), (1, C), (2, G)):
                last = nc.tensor.matmul(ps[:, b, 0:w], zero[0:1, 0:P], zero[0:1, 0:w], start=False, stop=True)
            last.then_inc(moved, 1)



def chunk_tiles(nc, o, engine, first, n):
    return nc.values_load_multi_w_load_instructions(
        o.tile_of_chunk[0:1, bass.ds(first, n)], engines=(engine,), min_val=0, max_val=NT - 1,
        skip_runtime_bounds_check_because="the sort writes tiles below NT")[1]


def weight_stage(nc, k):
    with Stage(nc, "weight") as c:
        half = c.sb("two_over_count", [P, NT, S2])
        deg = c.sb("degree", [P, NT])
        has = c.sb("has_edges", [P, NT])
        roots = c.sb("roots", [P, 2, NT])
        (step, rooted, rooting) = c.sems("step", "rooted", "rooting")
        block = c.block()

        @block.vector
        def _(dve):
            done = 0

            def then(inst):
                nonlocal done
                done += 1
                inst.then_inc(step, 1)
                dve.wait_ge(step, done)

            then(nc.vector.tensor_reduce(deg[:, :], k.count[:, :, R:S2], AX.X, ALU.add))
            nc.vector.tensor_scalar(has[:, :], deg[:, :], 0.0, None, ALU.is_gt)
            nc.vector.tensor_scalar_max(roots[:, 0, :], deg[:, :], 1.0)
            nc.vector.tensor_scalar(roots[:, 1, :], deg[:, :], 1.0, None, ALU.add).then_inc(rooting, 1)
            then(nc.vector.tensor_scalar_max(half[:, :, :], k.count[:, :, :], 1.0))
            then(nc.vector.reciprocal(half[:, :, :], half[:, :, :]))
            then(nc.vector.tensor_scalar(half[:, :, :], half[:, :, :], 2.0, None, ALU.mult))
            order = [r + R * inv for r in range(R) for inv in (0, 1)]
            then(nc.vector.tensor_copy(k.factor[:, :, order[-1]], half[:, :, order[-1]]))
            for s, after in zip(order[-2::-1], order[:0:-1]):
                then(nc.vector.tensor_tensor(k.factor[:, :, s], half[:, :, s], k.factor[:, :, after], ALU.mult))
            dve.wait_ge(rooted, 1)
            nc.vector.reciprocal(k.dinv_loop[:, :], roots[:, 1, :])
            then(nc.vector.reciprocal(roots[:, 0, :], roots[:, 0, :]))
            then(nc.vector.tensor_tensor(k.dinv[:, :], roots[:, 0, :], has[:, :], ALU.mult))

        @block.scalar
        def _(act):
            act.wait_ge(rooting, 1)
            nc.scalar.activation(roots[:, :, :], roots[:, :, :], ACT.Sqrt).then_inc(rooted, 1)


def edge_factor_stage(nc, k, o):
    V = 8
    with Stage(nc, f"factor{o.key}") as c:
        pick = c.sb("pick", [P, V, P])
        turned = c.sb("turned", [P, V, P])
        types = c.sb("type_one_hot", [P, C, R])
        got = c.sb("got", [P, V, R])
        ps_turn = c.psum("ps_turn", [P, 4, 512])      
        ps_got = c.psum("ps_got", [P, 512])
        picked, flipped, copied, found, taken, step = c.sems(
            "picked", "flipped", "copied", "found", "taken", "step")
        block = c.block()

        @block.vector
        def _(dve):
            nc.vector.tensor_tensor(types[:, :, :], o.type[:, :, None].to_broadcast([P, C, R]),
                                    k.iota[:, None, 0:R].to_broadcast([P, C, R]), ALU.is_equal).then_inc(step, 1)

            def make(i, v):
                nc.vector.tensor_scalar(pick[:, v, :], k.iota[:, 0:P], o.local[:, bass.ds(i * V + v, 1)], None,
                                        ALU.is_equal).then_inc(picked, 1)

            def take(i):
                dve.wait_ge(found, i * V + 2 * V)
                dve.wait_ge(step, i + 1)
                nc.vector.tensor_tensor(got[:, :, :], ps_got[:, 0:V * R].rearrange("p (v r) -> p v r", r=R),
                                        types[:, bass.ds(i * V, V), :], ALU.mult).then_inc(taken, 1)
                dve.wait_ge(taken, i + 2)
                nc.vector.tensor_reduce(o.coef[:, bass.ds(i * V, V)], got[:, :, :], AX.X, ALU.add).then_inc(step, 1)

            nc.vector.sem_inc(taken, 1)
            for v in range(V):
                make(0, v)
            with dve.Fori(0, C // V - 1) as i:
                for v in range(V):
                    dve.wait_ge(flipped, i * V + v + 1)
                    make(i + 1, v)
                take(i)
            take(C // V - 1)

        @block.tensor
        def _(pe):
            nc.tensor.sem_inc(found, V)
            with pe.Fori(0, C // V) as i:
                tiles = chunk_tiles(nc, o, PE, i * V, V)
                for v in range(V + 2):
                    if v < V:
                        pe.wait_ge(picked, i * V + v + 1)
                        pe.wait_ge(copied, i * V + v + 1)
                        nc.tensor.transpose(ps_turn[:, v % 4, 0:P], pick[:, v, :], k.ident[:, :]).then_inc(flipped, 1)
                    if v == 1:
                        pe.wait_ge(taken, i + 1)
                    if v >= 2:
                        pe.wait_ge(copied, i * V + v + 3)
                        nc.tensor.matmul(ps_got[:, R * v - 2 * R:R * v - R], turned[:, v - 2, :],
                                         k.factor[:, bass.ds(tiles[v - 2], 1), o.first:o.first + R],
                                         start=True, stop=True).then_inc(found, 1)

        @block.scalar
        def _(act):
            nc.scalar.sem_inc(copied, 4)
            with act.Fori(0, C // V) as i:
                for v in range(V):
                    act.wait_ge(flipped, i * V + v + 1)
                    act.wait_ge(found, i * V + v + 1)
                    nc.scalar.copy(turned[:, v, :], ps_turn[:, v % 4, 0:P]).then_inc(copied, 1)



def edge_sum_stage(nc, k, tag, o, rows, table, width, acc, factors=None):
    BANKS = 1 if width <= 512 else 2
    PIECES = BANKS
    W = width // PIECES
    RING = 4
    PLACES = U if BANKS == 1 else U // 2
    H = U // 2
    with Stage(nc, tag) as c:
        got = c.sb("gathered", [P, PLACES, width])
        select = c.sb("select", [P, U, P])
        index = c.sb("index", [P, U], I32)
        ps = c.psum("ps", [P, RING * BANKS, 512])
        arrived, before = k.arrived, list(k.arrivals)
        for p in range(PLACES):
            k.arrivals[p] += C // PLACES
        indexed, selected, multiplied, added = c.sems("indexed", "selected", "multiplied", "added")
        block = c.block()

        @block.gpsimd
        def _(gp):
            with gp.Fori(0, C // U) as i:
                for u in range(U):
                    if u % H == 0:
                        gp.wait_ge(multiplied, i * U + u + H)
                        nc.gpsimd.tensor_copy(index[:, u:u + H], rows[:, bass.ds(i * U + u, H)]).then_inc(indexed, 1)
                        gp.wait_ge(indexed, i * 2 + u // H + 1)
                        nc.gpsimd.nop(nofuse=True)
                    if u % 4 == 0:
                        gp.wait_ge(multiplied, i * U + u + 4 + U - PLACES)
                        nc.gpsimd.nop(nofuse=True)
                    nc.gpsimd.indirect_dma_start(
                        got[:, u % PLACES, :], None, table,
                        bass.IndirectOffsetOnAxis(ap=index[:, u:u + 1], axis=0)).then_inc(arrived[u % PLACES], 16)

        @block.tensor
        def _(pe):
            nc.tensor.sem_inc(multiplied, U)
            with pe.Fori(0, C // U) as i:
                for u in range(U):
                    pe.wait_ge(arrived[u % PLACES],
                               (i * (U // PLACES) + u // PLACES + 1 + before[u % PLACES]) * 16)
                    pe.wait_ge(selected, i * U + u + 1)
                    pe.wait_ge(added, i * U + u + 1)
                    for b in range(PIECES):
                        last = nc.tensor.matmul(ps[:, (u % RING) * BANKS + b, 0:W], select[:, u, :],
                                                got[:, u % PLACES, b * W:b * W + W], start=True, stop=True)
                    last.then_inc(multiplied, 1)

        @block.vector
        def _(dve):
            nc.vector.sem_inc(added, RING)

            def make(n, u):
                dve.wait_ge(multiplied, n + 1)
                if factors is None:
                    nc.vector.tensor_scalar(select[:, u, :], k.iota[:, 0:P], o.local[:, bass.ds(n, 1)],
                                            None, ALU.is_equal).then_inc(selected, 1)
                else:
                    nc.vector.tensor_scalar(select[:, u, :], k.iota[:, 0:P], o.local[:, bass.ds(n, 1)],
                                            factors[:, bass.ds(n, 1)], ALU.is_equal, ALU.mult).then_inc(selected, 1)

            def turn(i, ahead):
                tiles = chunk_tiles(nc, o, DVE, i * U, U)
                for u in range(U):
                    if u < ahead:
                        make(i * U + u + LEAD, (u + LEAD) % U)
                    dve.wait_ge(multiplied, i * U + u + 1 + U)
                    dve.wait_ge(added, i * U + u + RING)
                    row = acc[:, bass.ds(tiles[u], 1), 0:width]
                    part = ps[:, (u % RING) * BANKS:(u % RING + 1) * BANKS, 0:W]
                    nc.vector.tensor_tensor(row.rearrange("p a (b w) -> p (a b) w", w=W),
                                            row.rearrange("p a (b w) -> p (a b) w", w=W), part,
                                            ALU.add).then_inc(added, 1)

            for u in range(LEAD):
                make(u, u)
            with dve.Fori(0, C // U - 1) as i:
                turn(i, U)
            turn(C // U - 1, LEAD)



def piece(first, width, terms, bias=None, target=None):
    return first, width, terms, bias, target


def table_stage(nc, k, tag, pieces, tables, width, scale=None):
    M = len(pieces)
    feeds = []
    for p in pieces:
        for turned, _ in p[2]:
            if not any(turned is f for f in feeds):
                feeds.append(turned)
    with Stage(nc, tag) as c:
        fed = c.sb("fed", [P, J, len(feeds), P])
        (copied,) = c.sems("copied")
        rows = c.sb("rows", [P, J, width])
        ps = c.psum("ps", [P, J, 512])
        stored = c.sems(*(f"stored{j}" for j in range(J)))
        multiplied, drained = c.sems("multiplied", "drained")
        block = c.block()

        @block.tensor
        def _(pe):
            nc.tensor.sem_inc(multiplied, M * J)
            with pe.Fori(0, TURNS) as i:
                for m in range(M * J):
                    j, (first, w, terms, bias, target) = m // M, pieces[m % M]
                    if m % M == 0:
                        pe.wait_ge(copied, (i * J + j + 1) * len(feeds))
                    pe.wait_ge(drained, i * (M * J) + m + 1)
                    for n, (turned, weights) in enumerate(terms):
                        (q,) = (q for q, f in enumerate(feeds) if f is turned)
                        last = nc.tensor.matmul(ps[:, m % J, 0:w], fed[:, j, q, :], weights,
                                                start=(n == 0), stop=(n == len(terms) - 1))
                    last.then_inc(multiplied, 1)

        def feed(engine, copy):
            with engine.Fori(0, TURNS) as i:
                for j in range(J):
                    engine.wait_ge(multiplied, i * (M * J) + M * j + M)
                    for q, turned in enumerate(feeds):
                        copy(fed[:, j, q, :], turned[:, bass.ds((i * J + j) * P, P)]).then_inc(copied, 1)

        def drain_turn(engine, i, first_turn):
            for m in range(M * J):
                j, (first, w, terms, bias, target) = m // M, pieces[m % M]
                if m % M == 0 and not first_turn:
                    engine.wait_ge(stored[j], i * 16 * len(tables))
                engine.wait_ge(multiplied, i * (M * J) + m + 1 + M * J)
                if scale is not None:
                    nc.scalar.nop(nofuse=True)
                to = rows[:, j, first:first + w] if target is None else \
                    target[:, bass.ds(i * J + j, 1), 0:w].rearrange("p a f -> p (a f)")
                if scale is not None:
                    last = nc.scalar.activation(to, ps[:, m % J, 0:w], ACT.Copy, scale=scale[:, bass.ds(i * J + j, 1)])
                elif bias is None:
                    last = nc.vector.tensor_copy(to, ps[:, m % J, 0:w])
                else:
                    last = nc.vector.tensor_tensor(to, ps[:, m % J, 0:w], bias, ALU.add)
                last.then_inc(drained, 1)

        def drain(engine):
            engine.sem_inc(drained, J)
            drain_turn(engine, 0, True)
            with engine.Fori(1, TURNS) as i:
                drain_turn(engine, i, False)

        if scale is not None:
            @block.scalar
            def _(act):
                drain(act)

            @block.vector
            def _(dve):
                feed(dve, nc.vector.tensor_copy)
        else:
            @block.vector
            def _(dve):
                drain(dve)

            @block.scalar
            def _(act):
                feed(act, nc.scalar.copy)

        @block.sync
        def _(sp):
            with sp.Fori(0, TURNS) as i:
                for j in range(J):
                    sp.wait_ge(drained, i * (M * J) + M * j + M + J)
                    for table, first, w in tables:
                        sp.dma_start(table[bass.ds((i * J + j) * P, P), :],
                                     rows[:, j, first:first + w]).then_inc(stored[j], 16)
            for j in range(J):
                sp.wait_ge(stored[j], 16 * TURNS * len(tables))


def combine_stage(nc, k, tag, acc, width, terms, bias, mean):
    PIECES = -(-width // 512)
    W = width // PIECES
    M = PIECES
    with Stage(nc, tag) as c:
        ps = c.psum("ps", [P, J, 512])
        fed = c.sb("fed", [P, J, len(terms), P])
        multiplied, drained, biased, relued, copied = c.sems("multiplied", "drained", "biased", "relued", "copied")
        block = c.block()

        @block.gpsimd
        def _(gp):
            with gp.Fori(0, TURNS) as i:
                for j in range(J):
                    gp.wait_ge(multiplied, i * (M * J) + M * j + M)
                    for q, (turned, _) in enumerate(terms):
                        nc.gpsimd.tensor_copy(fed[:, j, q, :], turned[:, bass.ds((i * J + j) * P, P)]).then_inc(copied, 1)

        @block.tensor
        def _(pe):
            nc.tensor.sem_inc(multiplied, M * J)
            with pe.Fori(0, TURNS) as i:
                for m in range(M * J):
                    j, b = divmod(m, M)
                    if b == 0:
                        pe.wait_ge(copied, (i * J + j + 1) * len(terms))
                    pe.wait_ge(drained, i * (M * J) + m + 1)
                    for n, (_, weights) in enumerate(terms):
                        last = nc.tensor.matmul(ps[:, m % J, 0:W], fed[:, j, n, :], weights[:, b * W:b * W + W],
                                                start=(n == 0), stop=(n == len(terms) - 1))
                    last.then_inc(multiplied, 1)

        @block.vector
        def _(dve):
            nc.vector.sem_inc(drained, J)
            with dve.Fori(0, TURNS) as i:
                for m in range(M * J):
                    j, b = divmod(m, M)
                    part = acc[:, bass.ds(i * J + j, 1), b * W:b * W + W].rearrange("p a f -> p (a f)")
                    dve.wait_ge(multiplied, i * (M * J) + m + 1 + M * J)
                    nc.vector.scalar_tensor_tensor(part, part, k.dinv[:, bass.ds(i * J + j, 1)], ps[:, m % J, 0:W],
                                                   ALU.mult, ALU.add).then_inc(drained, 1)
                    dve.wait_ge(drained, i * (M * J) + m + 1 + J)
                    nc.vector.tensor_tensor(part, part, bias[:, b * W:b * W + W], ALU.add).then_inc(biased, 1)
            if mean:
                F = width // K
                for n in range(1, K):
                    dve.wait_ge(relued, TURNS if n == 1 else TURNS)
                    if n > 1:
                        dve.wait_ge(biased, TURNS * M * J + 1)
                    nc.vector.tensor_tensor(acc[:, :, 0:F], acc[:, :, 0:F], acc[:, :, n * F:n * F + F],
                                            ALU.add).then_inc(biased, 1)

        @block.scalar
        def _(act):
            with act.Fori(0, TURNS) as i:
                for j in range(J):
                    act.wait_ge(biased, i * (M * J) + M * j + M)
                    nc.scalar.nop(nofuse=True)
                    part = acc[:, bass.ds(i * J + j, 1), 0:width]
                    last = nc.scalar.activation(part, part, ACT.Relu, scale=1.0 / K if mean else 1.0)
                last.then_inc(relued, 1)


def turn_stage(nc, k, tag, source, target, blocks=1, scale=None, relu=False):
    M = blocks
    with Stage(nc, tag) as c:
        fed = c.sb("fed", [P, J, M * P])
        ps = c.psum("ps", [P, J, 512])
        turned, copied, made = c.sems("turned", "copied", "made")
        block = c.block()

        @block.vector
        def _(dve):
            with dve.Fori(0, TURNS) as i:
                for j in range(J):
                    dve.wait_ge(turned, i * (M * J) + M * j + M)
                    part = source[:, bass.ds(i * J + j, 1), 0:M * P].rearrange("p a f -> p (a f)")
                    if scale is None:
                        last = nc.vector.tensor_copy(fed[:, j, :], part)
                    else:
                        last = nc.vector.tensor_scalar(fed[:, j, :], part, scale[:, bass.ds(i * J + j, 1)], None, ALU.mult)
                    last.then_inc(made, 1)

        @block.tensor
        def _(pe):
            nc.tensor.sem_inc(turned, M * J)
            with pe.Fori(0, TURNS) as i:
                for m in range(M * J):
                    j, b = divmod(m, M)
                    if b == 0:
                        pe.wait_ge(made, i * J + j + 1)
                    pe.wait_ge(copied, i * (M * J) + m + 1)
                    nc.tensor.transpose(ps[:, m % J, 0:P], fed[:, j, b * P:b * P + P], k.ident[:, :]).then_inc(turned, 1)

        @block.scalar
        def _(act):
            nc.scalar.sem_inc(copied, J)
            with act.Fori(0, TURNS) as i:
                for m in range(M * J):
                    j, b = divmod(m, M)
                    act.wait_ge(turned, i * (M * J) + m + 1 + M * J)
                    nc.scalar.nop(nofuse=True)
                    nc.scalar.activation(target[:, b, bass.ds((i * J + j) * P, P)], ps[:, m % J, 0:P],
                                         ACT.Relu if relu else ACT.Copy).then_inc(copied, 1)


def turn_back_stage(nc, k, tag, source):
    with Stage(nc, tag) as c:
        fed = c.sb("fed", [P, J, P])
        ps = c.psum("ps", [P, J, 512])
        turned, added, copied = c.sems("turned", "added", "copied")
        block = c.block()

        @block.scalar
        def _(act):
            with act.Fori(0, TURNS) as i:
                for j in range(J):
                    act.wait_ge(turned, i * J + j + 1)
                    nc.scalar.copy(fed[:, j, :], source[:, bass.ds((i * J + j) * P, P)]).then_inc(copied, 1)

        @block.tensor
        def _(pe):
            nc.tensor.sem_inc(turned, J)
            with pe.Fori(0, TURNS) as i:
                for j in range(J):
                    pe.wait_ge(copied, i * J + j + 1)
                    pe.wait_ge(added, i * J + j + 1)
                    nc.tensor.transpose(ps[:, j, 0:P], fed[:, j, :], k.ident[:, :]).then_inc(turned, 1)

        @block.vector
        def _(dve):
            nc.vector.sem_inc(added, J)
            with dve.Fori(0, TURNS) as i:
                for j in range(J):
                    part = k.xcur[:, bass.ds(i * J + j, 1), :].rearrange("p a f -> p (a f)")
                    dve.wait_ge(turned, i * J + j + 1 + J)
                    nc.vector.tensor_tensor(part, part, ps[:, j, 0:P], ALU.add).then_inc(added, 1)


def layer_norm_stage(nc, k, tag, addend=None, scale=None, bias=None):
    with Stage(nc, tag) as c:
        stats = c.sb("stats", [P, NT, 6])
        mean = c.sb("mean", [P, NT, 2])
        root = c.sb("root", [P, NT])
        step, rooting, rooted = c.sems("step", "rooting", "rooted")
        block = c.block()

        @block.vector
        def _(dve):
            done = 0

            def then(inst):
                nonlocal done
                done += 1
                inst.then_inc(step, 1)
                dve.wait_ge(step, done)

            if addend is not None:
                if scale is not None:
                    then(nc.vector.tensor_tensor(addend, addend, scale[:, :, None].to_broadcast([P, NT, D]), ALU.mult))
                then(nc.vector.tensor_tensor(k.xcur[:, :, :], k.xcur[:, :, :], addend, ALU.add))
            if bias is not None:
                then(nc.vector.tensor_tensor(k.xcur[:, :, :], k.xcur[:, :, :],
                                             bias[:, None, :].to_broadcast([P, NT, D]), ALU.add))
            for t in range(NT):
                last = nc.vector.bn_stats(stats[:, t, :], k.xcur[:, t, :])
            then(last)
            for t in range(NT):
                last = nc.vector.bn_aggr(mean[:, t, :], stats[:, t, :])
            then(last)
            nc.vector.tensor_scalar(root[:, :], mean[:, :, 1], EPS, None, ALU.add).then_inc(rooting, 1)
            dve.wait_ge(rooted, 1)
            then(nc.vector.reciprocal(root[:, :], root[:, :]))
            then(nc.vector.tensor_tensor(k.xcur[:, :, :], k.xcur[:, :, :],
                                         mean[:, :, 0:1].to_broadcast([P, NT, D]), ALU.subtract))
            then(nc.vector.tensor_tensor(k.xcur[:, :, :], k.xcur[:, :, :],
                                         root[:, :, None].to_broadcast([P, NT, D]), ALU.mult))

        @block.scalar
        def _(act):
            act.wait_ge(rooting, 1)
            nc.scalar.activation(root[:, :], root[:, :], ACT.Sqrt).then_inc(rooted, 1)


def batch_norm_stage(nc, k, tag, h, blocks, gamma, beta):
    with Stage(nc, tag) as c:
        mean = c.sb("mean", [P, blocks])
        var = c.sb("var", [P, blocks])
        root = c.sb("root", [P, blocks])
        spare = c.sb("squares", [P, NP])
        params = c.sb("params", [P, 2, blocks])
        loaded, step, centred, rooted, scaled, done_act = c.sems(
            "loaded", "step", "centred", "rooted", "scaled", "done_act")
        block = c.block()

        @block.sync
        def _(sp):
            with nc.allow_non_contiguous_dma(reason="one value per partition"):
                for n, a in enumerate((gamma, beta)):
                    sp.dma_start(params[:, n, :], a.rearrange("(b p) -> p b", p=P)).then_inc(loaded, 16)

        @block.vector
        def _(dve):
            done = 0

            def then(inst):
                nonlocal done
                done += 1
                inst.then_inc(step, 1)
                dve.wait_ge(step, done)

            then(nc.vector.tensor_reduce(mean[:, :], h[:, :, 0:N], AX.X, ALU.add))
            nc.vector.tensor_scalar(mean[:, :], mean[:, :], -1.0 / N, None, ALU.mult).then_inc(centred, 1)
            dve.wait_ge(centred, 1)
            dve.wait_ge(rooted, 1)
            then(nc.vector.reciprocal(root[:, :], root[:, :]))
            dve.wait_ge(loaded, 32)
            then(nc.vector.tensor_tensor(root[:, :], root[:, :], params[:, 0, :], ALU.mult))
            then(nc.vector.tensor_tensor(mean[:, :], mean[:, :], root[:, :], ALU.mult))
            nc.vector.tensor_tensor(mean[:, :], mean[:, :], params[:, 1, :], ALU.add).then_inc(scaled, 1)

        @block.scalar
        def _(act):
            act.wait_ge(centred, 1)
            for b in range(blocks):
                if b:
                    act.wait_ge(done_act, b)
                nc.scalar.activation(spare[:, 0:N], h[:, b, 0:N], ACT.Square, bias=mean[:, b:b + 1],
                                     accum_out=var[:, b:b + 1]).then_inc(done_act, 1)
            act.wait_ge(done_act, blocks)
            nc.scalar.activation(var[:, :], var[:, :], ACT.Copy, scale=1.0 / N, bias=EPS).then_inc(done_act, 1)
            act.wait_ge(done_act, blocks + 1)
            nc.scalar.activation(root[:, :], var[:, :], ACT.Sqrt).then_inc(rooted, 1)
            act.wait_ge(scaled, 1)
            for b in range(blocks):
                nc.scalar.activation(h[:, b, :], h[:, b, :], ACT.Relu, bias=mean[:, b:b + 1], scale=root[:, b:b + 1])


def feature_stage(nc, k, tag, out, terms, bias):
    W = 400
    PARTS = NP // W
    B = out.shape[1]
    with Stage(nc, tag) as c:
        ps = c.psum("ps", [P, 8, 512])
        multiplied, drained = c.sems("multiplied", "drained")
        block = c.block()

        @block.tensor
        def _(pe):
            for b in range(B):
                for n in range(PARTS):
                    if b:
                        pe.wait_ge(drained, (b - 1) * PARTS + n + 1)
                    for t, (weights, turned) in enumerate(terms):
                        last = nc.tensor.matmul(ps[:, n, 0:W], weights[:, b * P:b * P + P], turned[:, n * W:n * W + W],
                                                start=(t == 0), stop=(t == len(terms) - 1))
                    last.then_inc(multiplied, 1)

        @block.scalar
        def _(act):
            for b in range(B):
                for n in range(PARTS):
                    act.wait_ge(multiplied, b * PARTS + n + 1)
                    nc.scalar.activation(out[:, b, n * W:n * W + W], ps[:, n, 0:W], ACT.Relu,
                                         bias=bias[:, b:b + 1]).then_inc(drained, 1)


def load_weights_stage(nc, k, tag, loads, zero=None):
    with Stage(nc, tag) as c:
        (loaded,) = c.sems("loaded")
        block = c.block()

        @block.sync
        def _(sp):
            with nc.allow_non_contiguous_dma(reason="weights and biases, small"):
                for to, source in loads:
                    sp.dma_start(to, source).then_inc(loaded, 16)
            if loads:
                sp.wait_ge(loaded, 16 * len(loads))

        if zero is not None:
            @block.vector
            def _(dve):
                nc.vector.memset(zero, 0.0)


def setup(nc, c):
    k = Chip()

    def sb(name, shape, dt=F32):
        return c.enter_context(nc.sbuf_tensor(name, shape, dt))

    k.xcur = sb("xcur", [P, NT, D])
    k.xT = sb("xT", [P, NP])
    k.iota = sb("iota", [P, C])
    k.iota16 = sb("iota16", [P, C], FP16)
    k.diff = sb("diff", [P, P])
    k.ident = sb("ident", [P, P])
    k.onerow = sb("onerow", [1, P])
    k.count = sb("count", [P, NT, S2])
    k.factor = sb("factor", [P, NT, S2])
    k.dinv = sb("dinv", [P, NT])
    k.dinv_loop = sb("dinv_loop", [P, NT])
    k.arrived = [nc.alloc_semaphore(f"gathered{u}") for u in range(U)]
    k.arrivals = [0] * U
    k.orders = []
    for key in (0, 1):
        o = Chip()
        o.key = key
        o.first = R * key
        o.row = sb(f"row{key}", [P, C], I32)
        o.other = sb(f"other{key}", [P, C], I32)
        o.local = sb(f"local{key}", [P, C])
        o.type = sb(f"type{key}", [P, C])
        o.coef = sb(f"coef{key}", [P, C])
        o.tile_of_chunk = sb(f"tile_of_chunk{key}", [P, C], I32)
        k.orders.append(o)
    return k


def prepare(nc, k, A):
    with ExitStack() as c:
        def sb(name, shape, dt=F32):
            return c.enter_context(nc.sbuf_tensor(name, shape, dt))

        k.edges = sb("edges", [P, 3, EC], I32)
        load_stage(nc, k, A)
        for o in k.orders:
            with ExitStack() as d:
                o.local_in, o.high_in, o.low_in, o.group_in, o.slot_in, o.chunk_in = (
                    d.enter_context(nc.sbuf_tensor(f"{name}{o.key}", [P, EC], F32))
                    for name in ("local_in", "high_in", "low_in", "group_in", "slot_in", "chunk_in"))
                rank_stage(nc, k, o)
                permute_stage(nc, k, o)
        weight_stage(nc, k)
        for o in k.orders:
            edge_factor_stage(nc, k, o)



def arma_layer(nc, k, A, dram):
    by_dst = k.orders[1]

    with Stage(nc, "arma1") as c:
        ax = c.sb("ax", [P, NT, D])
        out1T = c.sb("out1T", [P, K * HID // P, NP])
        axT = c.sb("axT", [P, 1, NP])
        init_w = c.sb("init_w", [P, K, HID])
        root_w = c.sb("root_w", [P, K, HID])
        w = c.sb("w", [P, K, HID // P, HID])
        bias = c.sb("bias", [P, K * HID // P])
        load_weights_stage(nc, k, "arma1_load", [
            (init_w[:, :, :], A["L0_gnn_init_w1"].rearrange("k f g -> f k g")),
            (root_w[:, :, :], A["L0_gnn_root_w1"][0].rearrange("k f g -> f k g")),
            (w[:, :, :, :].rearrange("p k b h -> p (k b) h"),
             A["L0_gnn_w1"][0].rearrange("k (b p) h -> p (k b) h", p=P)),
            (bias[:, :], A["L0_gnn_b1"][0].rearrange("k o (b p) -> p (k o b)", p=P))], zero=ax[:, :, :])
        scaled_x_stage(nc, k, dram["x_scaled"])
        edge_sum_stage(nc, k, "sum_x", by_dst, by_dst.other, dram["x_scaled"][:, :], D, ax)
        turn_stage(nc, k, "turn_ax", ax, axT, scale=k.dinv)
        feature_stage(nc, k, "arma1_out", out1T,
                      [(init_w[:, :, :].rearrange("p k g -> p (k g)"), axT[:, 0, :]),
                       (root_w[:, :, :].rearrange("p k g -> p (k g)"), k.xT[:, :])], bias)
        table_stage(nc, k, "arma1_table",
                    [piece(s * HID, HID, [(out1T[:, s * 2 + b, :], w[:, s, b, :]) for b in range(HID // P)])
                     for s in range(K)], [(dram["arma1"], 0, K * HID)], K * HID, scale=k.dinv)

    with Stage(nc, "arma2") as c2:
        hT = c2.sb("hT", [P, HID // P, NP])
        with Stage(nc, "arma1_end") as c:
            acc = c.sb("acc", [P, NT, K * HID])
            root_w = c.sb("root_w", [P, K, HID])
            bias = c.sb("bias", [P, K * HID])
            load_weights_stage(nc, k, "arma1_end_load", [
                (root_w[:, :, :], A["L0_gnn_root_w1"][1].rearrange("k f g -> f k g")),
                (bias[:, :], A["L0_gnn_b1"][1].rearrange("k o g -> o (k g)").to_broadcast([P, K * HID]))],
                zero=acc[:, :, :])
            edge_sum_stage(nc, k, "sum_arma1", by_dst, by_dst.other, dram["arma1"][:, :], K * HID, acc)
            combine_stage(nc, k, "arma1_combine", acc, K * HID,
                          [(k.xT[:, :], root_w[:, :, :].rearrange("p k g -> p (k g)"))], bias, mean=True)
            turn_stage(nc, k, "turn_h", acc, hT, blocks=HID // P)
        batch_norm_stage(nc, k, "norm_h", hT, HID // P, A["L0_gnn_gamma1"], A["L0_gnn_beta1"])

        G = HID // P
        init_w = c2.sb("init_w", [P, G, K, D])
        root_w = c2.sb("root_w", [P, 2, G, K, D])
        w = c2.sb("w", [P, K, D])
        bias = c2.sb("bias", [P, 2, K * D])
        acc = c2.sb("acc", [P, NT, K * D])
        load_weights_stage(nc, k, "arma2_load", [
            *((init_w[:, b, :, :], A["L0_gnn_init_w2"][:, b * P:b * P + P, :].rearrange("k f g -> f k g"))
              for b in range(G)),
            *((root_w[:, t, b, :, :], A["L0_gnn_root_w2"][t, :, b * P:b * P + P, :].rearrange("k f g -> f k g"))
              for t in (0, 1) for b in range(G)),
            (w[:, :, :], A["L0_gnn_w2"][0].rearrange("k f g -> f k g")),
            *((bias[:, t, :], A["L0_gnn_b2"][t].rearrange("k o g -> o (k g)").to_broadcast([P, K * D]))
              for t in (0, 1))], zero=acc[:, :, :])

        def flat(weights):
            return weights.rearrange("p k g -> p (k g)")

        roots = [[(hT[:, b, :], flat(root_w[:, t, b, :, :])) for b in range(G)] for t in (0, 1)]
        table_stage(nc, k, "arma2_table0",
                    [piece(0, K * D, [(hT[:, b, :], flat(init_w[:, b, :, :])) for b in range(G)])],
                    [(dram["arma2"], 0, K * D)], K * D, scale=k.dinv)
        edge_sum_stage(nc, k, "sum_arma2", by_dst, by_dst.other, dram["arma2"][:, :], K * D, acc)
        combine_stage(nc, k, "arma2_combine0", acc, K * D, roots[0], bias[:, 0, :], mean=False)
        with Stage(nc, "arma2_mid") as c:
            outT = c.sb("outT", [P, K, NP])
            turn_stage(nc, k, "turn_out", acc, outT, blocks=K)
            table_stage(nc, k, "arma2_table1",
                        [piece(s * D, D, [(outT[:, s, :], w[:, s, :])]) for s in range(K)],
                        [(dram["arma2"], 0, K * D)], K * D, scale=k.dinv)
        load_weights_stage(nc, k, "arma2_clear", [], zero=acc[:, :, :])
        edge_sum_stage(nc, k, "sum_arma3", by_dst, by_dst.other, dram["arma2"][:, :], K * D, acc)
        combine_stage(nc, k, "arma2_combine1", acc, K * D, roots[1], bias[:, 1, :], mean=True)
        h2T = c2.sb("h2T", [P, 1, NP])
        turn_stage(nc, k, "turn_h2", acc, h2T)
        batch_norm_stage(nc, k, "norm_h2", h2T, 1, A["L0_gnn_gamma2"], A["L0_gnn_beta2"])
        turn_back_stage(nc, k, "arma_back", h2T[:, 0, :])
    layer_norm_stage(nc, k, "norm0")
    turn_stage(nc, k, "turn0", k.xcur, k.xT[:, None, :])


def scaled_x_stage(nc, k, table):
    with Stage(nc, "scaled_x") as c:
        rows = c.sb("rows", [P, NT, D])
        ps = c.psum("ps", [P, J, 512])
        made, stored, turned, copied = c.sems("made", "stored", "turned", "copied")
        block = c.block()

        @block.vector
        def _(dve):
            nc.vector.tensor_tensor(rows[:, :, :], k.xcur[:, :, :], k.dinv[:, :, None].to_broadcast([P, NT, D]),
                                    ALU.mult).then_inc(made, 1)

        @block.sync
        def _(sp):
            sp.wait_ge(made, 1)
            sp.dma_start(table.rearrange("(t p) f -> p t f", p=P), rows[:, :, :]).then_inc(stored, 16)
            sp.wait_ge(stored, 16)
    turn_stage(nc, k, "turn_x", k.xcur, k.xT[:, None, :])


def gcn_layer(nc, k, A, dram):
    xT = k.xT[:, :]
    by_dst = k.orders[1]
    with Stage(nc, "gcn") as c:
        w = c.sb("w", [P, D])
        bias = c.sb("bias", [P, D])
        acc = c.sb("acc", [P, NT, D])
        load_weights_stage(nc, k, "gcn_load", [
            (w[:, :], A["L1_gnn_W"]), (bias[:, :], A["L1_gnn_b"][None, :].to_broadcast([P, D]))])
        table_stage(nc, k, "gcn_table", [piece(0, D, [(xT, w[:, :])]),
                                         piece(0, D, [(xT, w[:, :])], target=acc)],
                    [(dram["narrow"], 0, D)], D, scale=k.dinv_loop)
        edge_sum_stage(nc, k, "sum_gcn", by_dst, by_dst.other, dram["narrow"][:, :], D, acc)
        layer_norm_stage(nc, k, "norm1", acc[:, :, :], scale=k.dinv_loop, bias=bias)
    turn_stage(nc, k, "turn1", k.xcur, k.xT[:, None, :])


def rgcn_layer(nc, k, A, dram):
    xT = k.xT[:, :]
    S = S2 + 1
    with Stage(nc, "rgcn") as c:
        acc = c.sb("acc", [P, NT, D])
        for layer in (0, 1):
            with Stage(nc, f"rgcn{layer}") as d:
                w = d.sb("w", [P, S, D])
                bias = d.sb("bias", [P, S, D])
                load_weights_stage(nc, k, f"rgcn_load{layer}", [
                    (w[:, :, :], A["L2_gnn_rgcn_weights"][layer].rearrange("s f g -> f s g")),
                    (bias[:, :, :].rearrange("p s g -> p (s g)"),
                     A["L2_gnn_rgcn_biases"][layer:layer + 1].rearrange("o s g -> o (s g)").to_broadcast([P, S * D]))])
                pieces = []
                for s in range(0, S2, 4):
                    n = min(4, S2 - s)
                    pieces.append(piece(s * D, n * D, [(xT, w[:, s:s + n, :].rearrange("p s g -> p (s g)"))],
                                        bias=bias[:, s:s + n, :].rearrange("p s g -> p (s g)")))
                pieces.append(piece(0, D, [(xT, w[:, S2, :])], bias=bias[:, S2, :], target=acc))
                table_stage(nc, k, f"rgcn_table{layer}", pieces,
                            [(dram["by_src"], 0, R * D), (dram["by_dst"], R * D, R * D)], S2 * D)
            root_scale_stage(nc, k, f"root{layer}", acc)
            for o, name in zip(k.orders, ("by_src", "by_dst")):
                edge_sum_stage(nc, k, f"sum_rgcn{layer}_{name}", o, o.row,
                               dram[name].rearrange("n (r f) -> (n r) f", f=D), D, acc, factors=o.coef)
            if layer == 0:
                turn_stage(nc, k, "turn_rgcn", acc, k.xT[:, None, :], relu=True)
        layer_norm_stage(nc, k, "norm2", acc[:, :, :])
    turn_stage(nc, k, "turn2", k.xcur, k.xT[:, None, :])


def root_scale_stage(nc, k, tag, acc):
    with Stage(nc, tag) as c:
        block = c.block()

        @block.vector
        def _(dve):
            nc.vector.tensor_tensor(acc[:, :, :], acc[:, :, :], k.factor[:, :, 0:1].to_broadcast([P, NT, D]), ALU.mult)


def neighbour_layer(nc, k, A, dram):
    xT = k.xT[:, :]
    by_dst = k.orders[1]
    with Stage(nc, "neighbour") as c:
        w = c.sb("w", [P, 2, D])
        wT = c.sb("wT", [P, 2, D])
        bias = c.sb("bias", [P, 2, D])
        acc = c.sb("acc", [P, NT, D])
        load_weights_stage(nc, k, "neighbour_load", [
            (w[:, 0, :], A["L3_gnn_W_neigh"]), (w[:, 1, :], A["L3_gnn_W_self"]),
            (bias[:, 0, :], A["L3_gnn_b_neigh"][None, :].to_broadcast([P, D])),
            (bias[:, 1, :], A["L3_gnn_b_self"][None, :].to_broadcast([P, D]))])
        with Stage(nc, "neighbour_turn") as d:
            ps = d.psum("ps", [P, 2, 512])
            (turned,) = d.sems("turned")
            block = d.block()

            @block.tensor
            def _(pe):
                for n in (0, 1):
                    last = nc.tensor.transpose(ps[:, n, 0:D], w[:, n, :], k.ident[:, :])
                last.then_inc(turned, 1)

            @block.vector
            def _(dve):
                nc.vector.tensor_tensor(bias[:, 0, :], bias[:, 0, :], bias[:, 1, :], ALU.add)
                dve.wait_ge(turned, 1)
                nc.vector.tensor_copy(wT[:, :, :], ps[:, :, 0:D])
        table_stage(nc, k, "neighbour_table", [piece(0, D, [(xT, wT[:, 0, :])]),
                                               piece(0, D, [(xT, wT[:, 1, :])], bias=bias[:, 0, :], target=acc)],
                    [(dram["narrow"], 0, D)], D)
        edge_sum_stage(nc, k, "sum_neighbour", by_dst, by_dst.other, dram["narrow"][:, :], D, acc)
        layer_norm_stage(nc, k, "norm3", acc[:, :, :])


def store_stage(nc, k, out):
    with Stage(nc, "store") as c:
        (stored,) = c.sems("stored")
        block = c.block()

        @block.sync
        def _(sp):
            sp.dma_start(out[0:(NT - 1) * P, :].rearrange("(t p) f -> p t f", p=P),
                         k.xcur[:, 0:NT - 1, :]).then_inc(stored, 16)
            sp.dma_start(out[(NT - 1) * P:N, :], k.xcur[0:LAST, NT - 1, :]).then_inc(stored, 16)
            sp.wait_ge(stored, 32)


def gnn_kernel(nc, A, out):
    dram = {name: nc.dram_tensor(name, (NP, width), F32, kind="Internal").ap()
            for name, width in (("x_scaled", D), ("arma1", K * HID), ("arma2", K * D), ("narrow", D),
                                ("by_src", R * D), ("by_dst", R * D))}
    with ExitStack() as c:
        k = setup(nc, c)
        prepare(nc, k, A)
        arma_layer(nc, k, A, dram)
        gcn_layer(nc, k, A, dram)
        rgcn_layer(nc, k, A, dram)
        neighbour_layer(nc, k, A, dram)
        store_stage(nc, k, out)


NAMES = ["x", "src", "dst", "edge_type_9",
         "L0_gnn_init_w1", "L0_gnn_w1", "L0_gnn_root_w1", "L0_gnn_b1",
         "L0_gnn_init_w2", "L0_gnn_w2", "L0_gnn_root_w2", "L0_gnn_b2",
         "L0_gnn_gamma1", "L0_gnn_beta1", "L0_gnn_gamma2", "L0_gnn_beta2",
         "L1_gnn_W", "L1_gnn_b", "L2_gnn_rgcn_weights", "L2_gnn_rgcn_biases",
         "L3_gnn_W_neigh", "L3_gnn_b_neigh", "L3_gnn_W_self", "L3_gnn_b_self"]


def kernel(**inputs):
    import numpy as np
    import concourse.bacc as bacc
    from concourse.bass_utils import run_bass_kernel_spmd

    nc = bacc.Bacc("TRN2", target_bir_lowering=False, num_devices=1)
    arrays, args = {}, {}
    for name in NAMES:
        a = np.ascontiguousarray(inputs[name])
        arrays[f"in_{name}"] = a
        args[name] = nc.dram_tensor(f"in_{name}", a.shape, mybir.dt.from_np(a.dtype), kind="ExternalInput").ap()
    out = nc.dram_tensor("out_0", (N, D), F32, kind="ExternalOutput").ap()
    gnn_kernel(nc, args, out)
    return run_bass_kernel_spmd(nc, [arrays], core_ids=[0]).results[0]["out_0"]
```

```python
import concourse.bass as bass
from concourse import mybir
from contextlib import ExitStack

F32, BF16, FP16, I32 = mybir.dt.float32, mybir.dt.bfloat16, mybir.dt.float16, mybir.dt.int32
PE, DVE = mybir.EngineType.PE, mybir.EngineType.DVE
ALU, ACT, AX = mybir.AluOpType, mybir.ActivationFunctionType, mybir.AxisListType

P = 128
N = 3125
E = 50000
D = 128
R = 9
K = 3
HID = 256
EPS = 1e-5
NT = -(-N // P)
NP = NT * P
LAST = N - (NT - 1) * P
EP = 125
EC = E // EP
U = 16
C = -(-(E // P + NT + 1) // U) * U
S2 = 2 * R
J = 5
TURNS = NT // J
TURNS_OF_CHUNKS = C // U
LAG = 2
LEAD = 8


class Chip:
    pass


class Stage(ExitStack):

    def __init__(self, nc, tag):
        super().__init__()
        self.nc, self.tag = nc, tag

    def sb(self, name, shape, dt=F32):
        return self.enter_context(self.nc.sbuf_tensor(f"{name}_{self.tag}", shape, dt))

    def psum(self, name, shape, dt=F32):
        return self.enter_context(self.nc.psum_tensor(f"{name}_{self.tag}", shape, dt))

    def sems(self, *names):
        sems = [self.nc.alloc_semaphore(f"{n}_{self.tag}") for n in names]
        self.callback(self.give_back, sems)
        return sems

    def give_back(self, sems):
        for s in sems:
            self.nc.sync.sem_clear(s)
            self.nc.release_semaphore(s)

    def block(self):
        return self.enter_context(self.nc.Block())


def ts(i, n=P):
    return bass.ds(i * n, n)


def pair_free(i, j):
    return i * J + 2 + (0 if j == 0 else -1 if j == 1 else j - 1)



def load_stage(nc, k, A):
    with Stage(nc, "load") as c:
        loaded, zeroed, made = c.sems("loaded", "zeroed", "made")
        block = c.block()

        @block.sync
        def _(sp):
            sp.wait_ge(zeroed, 1)
            sp.dma_start(k.xcur[:, 0:NT - 1, :],
                         A["x"][0:(NT - 1) * P, :].rearrange("(t p) f -> p t f", p=P)).then_inc(loaded, 16)
            sp.dma_start(k.xcur[0:LAST, NT - 1, :], A["x"][(NT - 1) * P:N, :]).then_inc(loaded, 16)
            sp.wait_ge(loaded, 16 * 5)

        @block.scalar
        def _(act):
            for i, name in enumerate(("src", "dst", "edge_type_9")):
                act.dma_start(k.edges[0:EP, i, :], A[name].rearrange("(p c) -> p c", p=EP)).then_inc(loaded, 16)

        @block.vector
        def _(dve):
            nc.vector.memset(k.xcur[:, :, :], 0.0).then_inc(zeroed, 1)
            nc.vector.memset(k.one[:, :], 1.0)

        @block.gpsimd
        def _(gp):
            nc.gpsimd.iota(k.iota[:, :], [[1, C]], base=0, channel_multiplier=0,
                           allow_small_or_imprecise_dtypes=True)
            nc.gpsimd.iota(k.iota16[:, :], [[1, C]], base=0, channel_multiplier=0,
                           allow_small_or_imprecise_dtypes=True)
            nc.gpsimd.iota(k.diff[:, :], [[1, P]], base=0, channel_multiplier=-1,
                           allow_small_or_imprecise_dtypes=True).then_inc(made, 1)
            gp.wait_ge(made, 1)
            nc.gpsimd.tensor_scalar(k.ident[:, :], k.diff[:, :], 0.0, None, ALU.is_equal)



def rank_stage(nc, k, o):
    other = 1 - o.key
    B = 4
    W = 500
    BLOCKS = NT * EC // W
    with Stage(nc, f"rank{o.key}") as c:
        sb = c.sb
        ps = c.psum("ps", [P, 8, 512])
        ints = sb("ints", [P, 4, EC], I32)
        tile_of = sb("tile_of", [P, EC], F32)
        one_hot = sb("tile_one_hot", [P, NT, EC], BF16)
        ones = sb("ones_bf", [P, P], BF16)
        triangle = sb("triangle", [P, P], BF16)
        total = sb("column_total", [P, NT * EC], F32)
        upto = sb("edges_up_to", [P, NT * EC], F32)
        cum = sb("cum", [P, NT + 1], F32)
        size = sb("size", [P, NT], F32)
        sizei = sb("sizei", [P, NT], I32)
        first = sb("first_chunk", [P, NT + 1], F32)
        shift = sb("shift", [P, NT], F32)
        pos = sb("pos", [P, EC], F32)
        tl = sb("tile_of_chunk", [P, C], F32)
        step, counted, kept, ranked = c.sems("step", "counted", "kept", "ranked")
        block = c.block()
        flat = one_hot[:, :, :].rearrange("p b c -> p (b c)")

        @block.vector
        def _(dve):
            done = 0

            def then(inst):
                nonlocal done
                done += 1
                inst.then_inc(step, 1)
                dve.wait_ge(step, done)

            key = k.edges[0:EP, o.key, :]
            e = slice(0, EP)
            nc.vector.tensor_single_scalar(ints[e, 0, :], key, 7, ALU.arith_shift_right)
            then(nc.vector.tensor_single_scalar(ints[e, 1, :], key, P - 1, ALU.bitwise_and))
            nc.vector.tensor_copy(o.local_in[e, :], ints[e, 1, :])
            nc.vector.tensor_scalar(o.minus_local_in[e, :], ints[e, 1, :], -1.0, None, ALU.mult)
            then(nc.vector.tensor_scalar(pos[e, :], k.edges[e, other, :], float(R), None, ALU.mult))
            then(nc.vector.tensor_tensor(pos[e, :], pos[e, :], k.edges[e, 2, :], ALU.add))
            then(nc.vector.tensor_scalar(pos[e, :], pos[e, :], float(P), 1.0, ALU.mult, ALU.add))
            then(nc.vector.tensor_tensor(ints[e, 2, :], pos[e, :], o.local_in[e, :], ALU.add))
            nc.vector.tensor_single_scalar(ints[e, 3, :], ints[e, 2, :], 11, ALU.arith_shift_right)
            then(nc.vector.tensor_single_scalar(ints[e, 2, :], ints[e, 2, :], 2047, ALU.bitwise_and))
            nc.vector.tensor_copy(o.high_in[e, :], ints[e, 3, :])
            nc.vector.tensor_copy(o.low_in[e, :], ints[e, 2, :])
            then(nc.vector.tensor_copy(tile_of[e, :], ints[e, 0, :]))
            nc.vector.tensor_scalar(o.group_in[e, :], tile_of[e, :], float(R), None, ALU.mult)
            nc.vector.memset(ones[:, :], 1.0)
            nc.vector.tensor_scalar(triangle[:, :], k.diff[:, :], 0.0, 1.0, ALU.is_gt, ALU.subtract)
            then(nc.vector.tensor_tensor(one_hot[e, :, :],
                                         tile_of[e, None, :].to_broadcast([EP, NT, EC]),
                                         k.iota[e, 0:NT, None].to_broadcast([EP, NT, EC]), ALU.is_equal))
            nc.vector.tensor_tensor(o.group_in[e, :], o.group_in[e, :], k.edges[e, 2, :],
                                    ALU.add).then_inc(ranked, 1)
            dve.wait_ge(kept, 1 + BLOCKS // B)
            then(nc.vector.tensor_tensor_scan(upto[:, :], total[:, :], total[:, :], 0.0, ALU.add, ALU.max))
            nc.vector.memset(cum[:, 0:1], 0.0)
            nc.vector.memset(first[:, 0:1], 0.0)
            then(nc.vector.tensor_copy(cum[:, 1:NT + 1],
                                       upto[:, :].rearrange("p (b c) -> p b c", c=EC)[:, :, EC - 1]))
            then(nc.vector.tensor_tensor(size[:, :], cum[:, 1:NT + 1], cum[:, 0:NT], ALU.subtract))
            then(nc.vector.tensor_scalar(sizei[:, :], size[:, :], float(P - 1), None, ALU.add))
            then(nc.vector.tensor_single_scalar(sizei[:, :], sizei[:, :], 7, ALU.arith_shift_right))
            then(nc.vector.tensor_copy(size[:, :], sizei[:, :]))
            then(nc.vector.tensor_tensor_scan(first[:, 1:NT + 1], size[:, :], size[:, :], 0.0, ALU.add, ALU.max))
            then(nc.vector.scalar_tensor_tensor(shift[:, :], first[:, 0:NT], float(P), cum[:, 0:NT],
                                                ALU.mult, ALU.subtract))
            then(nc.vector.tensor_tensor(upto[:, :].rearrange("p (b c) -> p b c", c=EC),
                                         upto[:, :].rearrange("p (b c) -> p b c", c=EC),
                                         shift[:, :, None].to_broadcast([P, NT, EC]), ALU.add))
            with dve.Fori(0, BLOCKS // B) as i:
                dve.wait_ge(counted, i * B + B + BLOCKS)
                for b in range(B):
                    last = nc.vector.tensor_tensor(
                        upto[0:EP, bass.ds((i * B + b) * W, W)], upto[0:EP, bass.ds((i * B + b) * W, W)],
                        ps[0:EP, 4 + b, 0:W], ALU.add)
                last.then_inc(ranked, 1)
            dve.wait_ge(ranked, 1 + BLOCKS // B)
            then(nc.vector.tensor_tensor(total[e, :], upto[e, :], flat[e, :], ALU.mult))
            then(nc.vector.tensor_reduce(pos[e, :], total[e, :].rearrange("p (b c) -> p c b", c=EC),
                                         AX.X, ALU.add))
            then(nc.vector.tensor_copy(ints[e, 0, :], pos[e, :]))
            nc.vector.tensor_single_scalar(ints[e, 1, :], ints[e, 0, :], P - 1, ALU.bitwise_and)
            then(nc.vector.tensor_single_scalar(ints[e, 2, :], ints[e, 0, :], 7, ALU.arith_shift_right))
            nc.vector.tensor_copy(o.slot_in[e, :], ints[e, 1, :])
            nc.vector.tensor_copy(o.chunk_in[e, :], ints[e, 2, :])
            then(nc.vector.memset(tl[:, :], 0.0))
            for b in range(NT):
                then(nc.vector.scalar_tensor_tensor(tl[:, :], k.iota[:, 0:C], first[:, b + 1:b + 2], tl[:, :],
                                                    ALU.is_ge, ALU.add))
            then(nc.vector.tensor_scalar_min(o.tile_of_chunk[:, :], tl[:, :], float(NT - 1)))

        @block.tensor
        def _(pe):
            pe.wait_ge(ranked, 1)
            with pe.Fori(0, BLOCKS // B) as i:
                pe.wait_ge(kept, i + 1)
                for b in range(B):
                    nc.tensor.matmul(ps[:, b, 0:W], ones[0:EP, :], flat[0:EP, bass.ds((i * B + b) * W, W)],
                                     start=True, stop=True).then_inc(counted, 1)
            with pe.Fori(0, BLOCKS // B) as i:
                pe.wait_ge(ranked, 1 + i)
                for b in range(B):
                    nc.tensor.matmul(ps[0:EP, 4 + b, 0:W], triangle[0:EP, 0:EP],
                                     flat[0:EP, bass.ds((i * B + b) * W, W)],
                                     start=True, stop=True).then_inc(counted, 1)

        @block.scalar
        def _(act):
            nc.scalar.sem_inc(kept, 1)
            with act.Fori(0, BLOCKS // B) as i:
                act.wait_ge(counted, i * B + B)
                for b in range(B):
                    last = nc.scalar.copy(total[:, bass.ds((i * B + b) * W, W)], ps[:, b, 0:W])
                last.then_inc(kept, 1)


class Job:

    def __init__(self, turns):
        self.turns = turns

    def vector_close(self, dve, i):
        pass


def run_job_stage(nc, tag, job):
    with Stage(nc, tag) as c:
        block = c.block()

        @block.vector
        def _(dve):
            with dve.Fori(0, job.turns) as i:
                for u in range(U):
                    job.vector(dve, i, u)

        @block.scalar
        def _(act):
            with act.Fori(0, job.turns) as i:
                for u in range(U):
                    job.scalar(act, i, u)

        @block.tensor
        def _(pe):
            with pe.Fori(0, job.turns) as i:
                for u in range(U):
                    job.tensor(pe, i, u)


class Permute(Job):

    G = NT * R
    V = 4

    def __init__(self, nc, c, k, o):
        super().__init__(EC // U)
        self.nc, self.k, self.o = nc, k, o
        self.ps = c.psum("ps", [P, 3, 512])
        self.zero = c.sb("zero", [1, 512], FP16)
        self.chunk = c.sb("chunk_one_hot", [P, self.V, C], FP16)
        self.slot = c.sb("slot_one_hot", [P, self.V, 2, P], FP16)
        self.group = c.sb("group_one_hot", [P, self.V, self.G], FP16)
        self.far = c.sb("distance", [P, self.V, P], FP16)
        self.local = c.sb("local_one_hot", [P, self.V, P], FP16)
        self.zeroed, self.column, self.measured, self.located, self.moved = c.sems(
            "zeroed", "column", "measured", "located", "moved")

    def start_stage(self):
        nc = self.nc
        with Stage(nc, f"permute_start{self.o.key}") as c:
            block = c.block()

            @block.vector
            def _(dve):
                nc.vector.memset(self.zero[:, :], 0.0).then_inc(self.zeroed, 1)

            @block.tensor
            def _(pe):
                pe.wait_ge(self.zeroed, 1)
                for b, w in ((0, C), (1, C), (2, self.G)):
                    last = nc.tensor.matmul(self.ps[:, b, 0:w], self.zero[0:1, 0:P], self.zero[0:1, 0:w],
                                            start=True, stop=False)
                last.then_inc(self.moved, self.V)

    def vector(self, dve, i, u):
        nc, k, o, e = self.nc, self.k, self.o, slice(0, EP)
        n, v = i * U + u, u % self.V
        col = bass.ds(n, 1)
        dve.wait_ge(self.moved, n + 1)
        nc.vector.tensor_scalar(self.chunk[e, v, :], k.iota16[e, 0:C], o.chunk_in[e, col], None, ALU.is_equal)
        nc.vector.tensor_scalar(self.slot[e, v, 0, :], k.iota16[e, 0:P], o.slot_in[e, col],
                                o.high_in[e, col], ALU.is_equal, ALU.mult)
        nc.vector.tensor_scalar(self.slot[e, v, 1, :], k.iota16[e, 0:P], o.slot_in[e, col],
                                o.low_in[e, col], ALU.is_equal, ALU.mult)
        nc.vector.tensor_scalar(self.group[e, v, :], k.iota16[e, 0:self.G], o.group_in[e, col], None,
                                ALU.is_equal).then_inc(self.column, 1)

    def scalar(self, act, i, u):
        nc, k, o, e = self.nc, self.k, self.o, slice(0, EP)
        n, v = i * U + u, u % self.V
        act.wait_ge(self.moved, n + 1)
        nc.scalar.nop(nofuse=True)
        nc.scalar.activation(self.far[e, v, :], k.iota16[e, 0:P], ACT.Abs,
                             bias=o.minus_local_in[e, bass.ds(n, 1)]).then_inc(self.measured, 1)
        act.wait_ge(self.measured, n + 1)
        nc.scalar.nop(nofuse=True)
        nc.scalar.activation(self.local[e, v, :], self.far[e, v, :], ACT.Relu, bias=k.one[e, :],
                             scale=-1.0).then_inc(self.located, 1)

    def tensor(self, pe, i, u):
        nc, e = self.nc, slice(0, EP)
        n, v = i * U + u, u % self.V
        pe.wait_ge(self.column, n + 1)
        nc.tensor.matmul(self.ps[:, 0, 0:C], self.slot[e, v, 0, :], self.chunk[e, v, :], start=False, stop=False)
        nc.tensor.matmul(self.ps[:, 1, 0:C], self.slot[e, v, 1, :], self.chunk[e, v, :], start=False, stop=False)
        pe.wait_ge(self.located, n + 1)
        nc.tensor.matmul(self.ps[:, 2, 0:self.G], self.local[e, v, :], self.group[e, v, :],
                         start=False, stop=False).then_inc(self.moved, 1)

    def end_stage(self):
        nc, k, o, ps, G = self.nc, self.k, self.o, self.ps, self.G
        with Stage(nc, f"permute_end{o.key}") as c:
            codes = c.sb("codes", [P, C])
            codei = c.sb("codei", [P, 2, C], I32)
            filled = c.sb("filled", [P, C])
            other = c.sb("other", [P, C])
            otheri = c.sb("otheri", [P, C], I32)
            over = c.sb("over", [P, C])
            closed, step = c.sems("closed", "step")
            block = c.block()

            @block.tensor
            def _(pe):
                for b, w in ((0, C), (1, C), (2, G)):
                    last = nc.tensor.matmul(ps[:, b, 0:w], self.zero[0:1, 0:P], self.zero[0:1, 0:w],
                                            start=False, stop=True)
                last.then_inc(closed, 1)

            @block.vector
            def _(dve):
                dve.wait_ge(closed, 1)
                done = 0

                def then(inst):
                    nonlocal done
                    done += 1
                    inst.then_inc(step, 1)
                    dve.wait_ge(step, done)

                nc.vector.tensor_copy(k.count[:, :, o.first:o.first + R],
                                      ps[:, 2, 0:G].rearrange("p (t r) -> p t r", r=R))
                then(nc.vector.tensor_scalar(codes[:, :], ps[:, 0, 0:C], 2048.0, None, ALU.mult))
                then(nc.vector.tensor_tensor(codes[:, :], codes[:, :], ps[:, 1, 0:C], ALU.add))
                nc.vector.tensor_scalar(filled[:, :], codes[:, :], 0.0, None, ALU.is_gt)
                then(nc.vector.tensor_scalar(codei[:, 0, :], codes[:, :], -1.0, 0.0, ALU.add, ALU.max))
                then(nc.vector.tensor_single_scalar(codei[:, 1, :], codei[:, 0, :], P - 1, ALU.bitwise_and))
                then(nc.vector.tensor_single_scalar(o.row[:, :], codei[:, 0, :], 7, ALU.arith_shift_right))
                then(nc.vector.tensor_scalar(codes[:, :], codei[:, 1, :], 1.0, None, ALU.add))
                then(nc.vector.tensor_tensor(codes[:, :], codes[:, :], filled[:, :], ALU.mult))
                if o.key:
                    nc.vector.tensor_scalar(o.minus_local[:, :], codes[:, :], -1.0, 1.0, ALU.mult, ALU.add)
                then(nc.vector.tensor_scalar(o.local[:, :], codes[:, :], -1.0, None, ALU.add))
                then(nc.vector.tensor_scalar(otheri[:, :], o.row[:, :], 1.0 / R, None, ALU.mult))
                then(nc.vector.tensor_copy(other[:, :], otheri[:, :]))
                then(nc.vector.tensor_copy(codes[:, :], o.row[:, :]))
                then(nc.vector.scalar_tensor_tensor(codes[:, :], other[:, :], -float(R), codes[:, :],
                                                    ALU.mult, ALU.add))
                then(nc.vector.tensor_scalar(over[:, :], codes[:, :], 0.0, None, ALU.is_lt))
                then(nc.vector.tensor_tensor(other[:, :], other[:, :], over[:, :], ALU.subtract))
                then(nc.vector.scalar_tensor_tensor(codes[:, :], over[:, :], float(R), codes[:, :],
                                                    ALU.mult, ALU.add))
                then(nc.vector.tensor_scalar(over[:, :], codes[:, :], float(R), None, ALU.is_ge))
                if o.key:
                    then(nc.vector.tensor_tensor(o.other[:, :], other[:, :], over[:, :], ALU.add))
                then(nc.vector.scalar_tensor_tensor(o.type[:, :], over[:, :], -float(R), codes[:, :],
                                                    ALU.mult, ALU.add))



def chunk_tiles(nc, o, engine, first, n):
    return nc.values_load_multi_w_load_instructions(
        o.tile_of_chunk[0:1, bass.ds(first, n)], engines=(engine,), min_val=0, max_val=NT - 1,
        skip_runtime_bounds_check_because="the sort writes tiles below NT")[1]


def degree_stage(nc, k):
    with Stage(nc, "degree") as c:
        deg = c.sb("degree", [P, NT])
        has = c.sb("has_edges", [P, NT])
        roots = c.sb("roots", [P, 2, NT])
        step, rooted, rooting = c.sems("step", "rooted", "rooting")
        block = c.block()

        @block.vector
        def _(dve):
            nc.vector.tensor_reduce(deg[:, :], k.count[:, :, R:S2], AX.X, ALU.add).then_inc(step, 1)
            dve.wait_ge(step, 1)
            nc.vector.tensor_scalar(has[:, :], deg[:, :], 0.0, None, ALU.is_gt)
            nc.vector.tensor_scalar_max(roots[:, 0, :], deg[:, :], 1.0)
            nc.vector.tensor_scalar(roots[:, 1, :], deg[:, :], 1.0, None, ALU.add).then_inc(rooting, 1)
            dve.wait_ge(rooted, 1)
            nc.vector.reciprocal(k.dinv_loop[:, :], roots[:, 1, :])
            nc.vector.reciprocal(roots[:, 0, :], roots[:, 0, :]).then_inc(step, 1)
            dve.wait_ge(step, 2)
            nc.vector.tensor_tensor(k.dinv[:, :], roots[:, 0, :], has[:, :], ALU.mult)

        @block.scalar
        def _(act):
            act.wait_ge(rooting, 1)
            nc.scalar.activation(roots[:, :, :], roots[:, :, :], ACT.Sqrt).then_inc(rooted, 1)


def factor_stage(nc, k):
    with Stage(nc, "factor") as c:
        half = c.sb("two_over_count", [P, NT, S2])
        (step,) = c.sems("step")
        block = c.block()

        @block.vector
        def _(dve):
            done = 0

            def then(inst):
                nonlocal done
                done += 1
                inst.then_inc(step, 1)
                dve.wait_ge(step, done)

            then(nc.vector.tensor_scalar_max(half[:, :, :], k.count[:, :, :], 1.0))
            then(nc.vector.reciprocal(half[:, :, :], half[:, :, :]))
            then(nc.vector.tensor_scalar(half[:, :, :], half[:, :, :], 2.0, None, ALU.mult))
            order = [r + R * inv for r in range(R) for inv in (0, 1)]
            then(nc.vector.tensor_copy(k.factor[:, :, order[-1]], half[:, :, order[-1]]))
            for s, after in zip(order[-2::-1], order[:0:-1]):
                then(nc.vector.tensor_tensor(k.factor[:, :, s], half[:, :, s], k.factor[:, :, after], ALU.mult))


def late(u):
    return range(max(u - LAG, 0), u + 1) if u == U - 1 else range(u - LAG, u - LAG + 1) if u >= LAG else ()


class EdgeFactors(Job):

    V = 8

    def __init__(self, nc, c, k, o):
        super().__init__(C // U)
        self.nc, self.k, self.o = nc, k, o
        self.pick = c.sb(f"pick{o.key}", [P, self.V, P])
        self.turned = c.sb(f"turned{o.key}", [P, self.V, P])
        self.type_hot = c.sb(f"type_one_hot{o.key}", [P, C, R])
        self.got = c.sb(f"got{o.key}", [P, U, R])
        self.ps_turn = c.psum(f"ps_turn{o.key}", [P, 2, 512])
        self.ps_got = c.psum(f"ps_got{o.key}", [P, 512])
        self.picked, self.flipped, self.copied, self.found, self.taken, self.step = c.sems(
            *(f"{n}{o.key}" for n in ("picked", "flipped", "copied", "found", "taken", "step")))

    def start_stage(self):
        nc, k, o, V = self.nc, self.k, self.o, self.V
        with Stage(nc, f"factor_start{o.key}") as c:
            block = c.block()

            @block.vector
            def _(dve):
                nc.vector.tensor_tensor(self.type_hot[:, :, :], o.type[:, :, None].to_broadcast([P, C, R]),
                                        k.iota[:, None, 0:R].to_broadcast([P, C, R]),
                                        ALU.is_equal).then_inc(self.step, 1)
                nc.vector.sem_inc(self.taken, 1)

            @block.tensor
            def _(pe):
                nc.tensor.sem_inc(self.flipped, V)
                nc.tensor.sem_inc(self.found, V)

            @block.scalar
            def _(act):
                nc.scalar.sem_inc(self.copied, 2)

    def vector(self, dve, i, u):
        nc, k, o, V = self.nc, self.k, self.o, self.V
        n, v = i * U + u, u % V
        dve.wait_ge(self.flipped, n + 1)
        nc.vector.tensor_scalar(self.pick[:, v, :], k.iota[:, 0:P], o.local[:, bass.ds(n, 1)], None,
                                ALU.is_equal).then_inc(self.picked, 1)

    def vector_close(self, dve, i):
        nc, o, V = self.nc, self.o, self.V
        dve.wait_ge(self.found, i * U + U + V)
        dve.wait_ge(self.step, i + 1)
        nc.vector.tensor_tensor(self.got[:, :, :], self.ps_got[:, 0:U * R].rearrange("p (v r) -> p v r", r=R),
                                self.type_hot[:, bass.ds(i * U, U), :], ALU.mult).then_inc(self.taken, 1)
        dve.wait_ge(self.taken, i + 2)
        nc.vector.tensor_reduce(o.coef[:, bass.ds(i * U, U)], self.got[:, :, :], AX.X,
                                ALU.add).then_inc(self.step, 1)

    def tensor(self, pe, i, u):
        nc, k, o, V = self.nc, self.k, self.o, self.V
        if u % V == 0:
            self.tiles = (self.tiles if u else []) + list(chunk_tiles(nc, o, PE, i * U + u, V))
        n = i * U + u
        pe.wait_ge(self.picked, n + 1)
        pe.wait_ge(self.copied, n + 1)
        nc.tensor.transpose(self.ps_turn[:, u % 2, 0:P], self.pick[:, u % V, :], k.ident[:, :]).then_inc(self.flipped, 1)
        for w in late(u):
            if w == 0:
                pe.wait_ge(self.taken, i + 1)
            pe.wait_ge(self.copied, i * U + w + 1 + 2)
            nc.tensor.matmul(self.ps_got[:, R * w:R * w + R], self.turned[:, w % V, :],
                             k.factor[:, bass.ds(self.tiles[w], 1), o.first:o.first + R],
                             start=True, stop=True).then_inc(self.found, 1)

    def scalar(self, act, i, u):
        nc, V = self.nc, self.V
        n = i * U + u
        act.wait_ge(self.flipped, n + 1 + V)
        act.wait_ge(self.found, n + 1)
        nc.scalar.copy(self.turned[:, u % V, :], self.ps_turn[:, u % 2, 0:P]).then_inc(self.copied, 1)



def edge_sum_stage(nc, k, tag, o, rows, table, width, acc, factors=None, jobs=(),
                   zero=False, loads=(), scalar_makes=0):
    def by_scalar(u):
        return scalar_makes and u % scalar_makes == scalar_makes - 1

    BANKS = 1 if width <= 512 else 2
    PIECES = BANKS
    W = width // PIECES
    RING = 4
    PLACES = U if BANKS == 1 else U // 2
    Q = U // 4
    with Stage(nc, tag) as c:
        got = c.sb("gathered", [P, PLACES, width])
        select = c.sb("select", [P, U, P])
        index = c.sb("index", [P, U], I32)
        ps = c.psum("ps", [P, RING * BANKS, 512])
        arrived, before = k.arrived, list(k.arrivals)
        for p in range(PLACES):
            k.arrivals[p] += C // PLACES
        far = c.sb("distance", [P, U // scalar_makes, P], FP16) if scalar_makes else None
        indexed, selected, multiplied, added, loaded, measured, selected_too = c.sems(
            "indexed", "selected", "multiplied", "added", "loaded", "measured", "selected_too")
        block = c.block()
        made = [u for u in range(U) if by_scalar(u)]
        own = [u for u in range(U) if not by_scalar(u)]

        if loads:
            @block.sync
            def _(sp):
                with nc.allow_non_contiguous_dma(reason="weights and biases, small"):
                    for to, source in loads:
                        sp.dma_start(to, source).then_inc(loaded, 16)
                sp.wait_ge(loaded, 16 * len(loads))

        @block.gpsimd
        def _(gp):
            with gp.Fori(0, C // U) as i:
                for u in range(U):
                    if u % Q == 0:
                        gp.wait_ge(indexed, i * 4 + u // Q + 1)
                        gp.wait_ge(multiplied, i * U + u + Q + U - PLACES)
                        nc.gpsimd.nop(nofuse=True)
                    nc.gpsimd.indirect_dma_start(
                        got[:, u % PLACES, :], None, table,
                        bass.IndirectOffsetOnAxis(ap=index[:, u:u + 1], axis=0)).then_inc(arrived[u % PLACES], 16)

        @block.tensor
        def _(pe):
            nc.tensor.sem_inc(multiplied, U)
            def turn(i, last_turn):
                for u in range(U):
                    pe.wait_ge(arrived[u % PLACES],
                               (i * (U // PLACES) + u // PLACES + 1 + before[u % PLACES]) * 16)
                    if by_scalar(u):
                        pe.wait_ge(selected_too, i * len(made) + made.index(u) + 1)
                    else:
                        pe.wait_ge(selected, i * len(own) + own.index(u) + 1)
                    pe.wait_ge(added, i * U + u + 1)
                    for b in range(PIECES):
                        last = nc.tensor.matmul(ps[:, (u % RING) * BANKS + b, 0:W], select[:, u, :],
                                                got[:, u % PLACES, b * W:b * W + W], start=True, stop=True)
                    last.then_inc(multiplied, 1)
                    for w in late(u):
                        for job in jobs:
                            if not last_turn or job.turns == TURNS_OF_CHUNKS:
                                job.tensor(pe, i, w)

            with pe.Fori(0, TURNS_OF_CHUNKS - 1) as i:
                turn(i, False)
            turn(TURNS_OF_CHUNKS - 1, True)

        @block.scalar
        def _(act):
            def put(i, q):
                nc.scalar.copy(index[:, q * Q:q * Q + Q], rows[:, bass.ds(i * U + q * Q, Q)]).then_inc(indexed, 1)

            def make(i, u):
                act.wait_ge(multiplied, i * U + u + 1)
                nc.scalar.nop(nofuse=True)
                nc.scalar.activation(far[:, made.index(u), :], k.iota[:, 0:P], ACT.Abs,
                                     bias=o.minus_local[:, bass.ds(i * U + u, 1)]).then_inc(measured, 1)
                act.wait_ge(measured, i * len(made) + made.index(u) + 1)
                nc.scalar.nop(nofuse=True)
                nc.scalar.activation(select[:, u, :], far[:, made.index(u), :], ACT.Relu, bias=k.one[:, :],
                                     scale=-1.0).then_inc(selected_too, 1)

            def turn(i, last_turn):
                for u in range(U):
                    if by_scalar((u + LEAD) % U) and (u < LEAD or not last_turn):
                        make(i + (u + LEAD) // U, (u + LEAD) % U)
                    if u % Q == 2 and not last_turn:
                        act.wait_ge(multiplied, i * U + u - 2 + Q + U)
                        nc.scalar.nop(nofuse=True)
                        put(i + 1, u // Q)
                    for job in jobs:
                        if not last_turn or job.turns == TURNS_OF_CHUNKS:
                            job.scalar(act, i, u)

            for q in range(4):
                put(0, q)
            for u in made:
                if u < LEAD:
                    make(0, u)
            with act.Fori(0, TURNS_OF_CHUNKS - 1) as i:
                turn(i, False)
            turn(TURNS_OF_CHUNKS - 1, True)

        @block.vector
        def _(dve):
            if zero:
                nc.vector.memset(acc[:, :, :], 0.0).then_inc(added, RING)
            else:
                nc.vector.sem_inc(added, RING)

            def make(n, u):
                dve.wait_ge(multiplied, n + 1)
                if factors is None:
                    nc.vector.tensor_scalar(select[:, u, :], k.iota[:, 0:P], o.local[:, bass.ds(n, 1)],
                                            None, ALU.is_equal).then_inc(selected, 1)
                else:
                    nc.vector.tensor_scalar(select[:, u, :], k.iota[:, 0:P], o.local[:, bass.ds(n, 1)],
                                            factors[:, bass.ds(n, 1)], ALU.is_equal, ALU.mult).then_inc(selected, 1)

            def turn(i, last_turn):
                tiles = chunk_tiles(nc, o, DVE, i * U, U)
                for u in range(U):
                    if not by_scalar((u + LEAD) % U) and (u < LEAD or not last_turn):
                        make(i * U + u + LEAD, (u + LEAD) % U)
                    for job in jobs:
                        if not last_turn or job.turns == TURNS_OF_CHUNKS:
                            job.vector(dve, i, u)
                    for w in late(u):
                        dve.wait_ge(multiplied, i * U + w + 1 + U)
                        dve.wait_ge(added, i * U + w + RING)
                        row = acc[:, bass.ds(tiles[w], 1), 0:width]
                        part = ps[:, (w % RING) * BANKS:(w % RING + 1) * BANKS, 0:W]
                        nc.vector.tensor_tensor(row.rearrange("p a (b w) -> p (a b) w", w=W),
                                                row.rearrange("p a (b w) -> p (a b) w", w=W), part,
                                                ALU.add).then_inc(added, 1)
                for job in jobs:
                    if not last_turn or job.turns == TURNS_OF_CHUNKS:
                        job.vector_close(dve, i)

            for u in own:
                if u < LEAD:
                    make(u, u)
            with dve.Fori(0, TURNS_OF_CHUNKS - 1) as i:
                turn(i, False)
            turn(TURNS_OF_CHUNKS - 1, True)



def piece(first, width, terms, bias=None, target=None):
    return first, width, terms, bias, target


def table_stage(nc, k, tag, pieces, tables, width, scale=None):
    M = len(pieces)
    feeds = []
    for p in pieces:
        for turned, _ in p[2]:
            if not any(turned is f for f in feeds):
                feeds.append(turned)
    with Stage(nc, tag) as c:
        fed = c.sb("fed", [P, J, len(feeds), P])
        (copied,) = c.sems("copied")
        rows = c.sb("rows", [P, J, width])
        ps = c.psum("ps", [P, J, 512])
        stored = c.sems(*(f"stored{j}" for j in range(J)))
        multiplied, drained = c.sems("multiplied", "drained")
        block = c.block()

        @block.tensor
        def _(pe):
            nc.tensor.sem_inc(multiplied, M * J)
            with pe.Fori(0, TURNS) as i:
                for m in range(M * J):
                    j, (first, w, terms, bias, target) = m // M, pieces[m % M]
                    if m % M == 0:
                        pe.wait_ge(copied, (i * J + j + 1) * len(feeds))
                    pe.wait_ge(drained, i * (M * J) + m + 1)
                    for n, (turned, weights) in enumerate(terms):
                        (q,) = (q for q, f in enumerate(feeds) if f is turned)
                        last = nc.tensor.matmul(ps[:, m % J, 0:w], fed[:, j, q, :], weights,
                                                start=(n == 0), stop=(n == len(terms) - 1))
                    last.then_inc(multiplied, 1)

        def feed(engine, copy):
            with engine.Fori(0, TURNS) as i:
                for j in range(J):
                    engine.wait_ge(multiplied, i * (M * J) + M * j + M)
                    for q, turned in enumerate(feeds):
                        copy(fed[:, j, q, :], turned[:, bass.ds((i * J + j) * P, P)]).then_inc(copied, 1)

        def drain_turn(engine, i, first_turn):
            for m in range(M * J):
                j, (first, w, terms, bias, target) = m // M, pieces[m % M]
                if m % M == 0 and not first_turn:
                    engine.wait_ge(stored[j], i * 16 * len(tables))
                engine.wait_ge(multiplied, i * (M * J) + m + 1 + M * J)
                if scale is not None:
                    nc.scalar.nop(nofuse=True)
                to = rows[:, j, first:first + w] if target is None else \
                    target[:, bass.ds(i * J + j, 1), 0:w].rearrange("p a f -> p (a f)")
                if scale is not None:
                    last = nc.scalar.activation(to, ps[:, m % J, 0:w], ACT.Copy, scale=scale[:, bass.ds(i * J + j, 1)])
                elif bias is None:
                    last = nc.vector.tensor_copy(to, ps[:, m % J, 0:w])
                else:
                    last = nc.vector.tensor_tensor(to, ps[:, m % J, 0:w], bias, ALU.add)
                last.then_inc(drained, 1)

        def drain(engine):
            engine.sem_inc(drained, J)
            drain_turn(engine, 0, True)
            with engine.Fori(1, TURNS) as i:
                drain_turn(engine, i, False)

        if scale is not None:
            @block.scalar
            def _(act):
                drain(act)

            @block.vector
            def _(dve):
                feed(dve, nc.vector.tensor_copy)
        else:
            @block.vector
            def _(dve):
                drain(dve)

            @block.scalar
            def _(act):
                feed(act, nc.scalar.copy)

        @block.sync
        def _(sp):
            with sp.Fori(0, TURNS) as i:
                for j in range(J):
                    sp.wait_ge(drained, i * (M * J) + M * j + M + J)
                    for table, first, w in tables:
                        sp.dma_start(table[bass.ds((i * J + j) * P, P), :],
                                     rows[:, j, first:first + w]).then_inc(stored[j], 16)
            for j in range(J):
                sp.wait_ge(stored[j], 16 * TURNS * len(tables))


def combine_stage(nc, k, tag, acc, width, terms, bias, mean):
    PIECES = -(-width // 512)
    W = width // PIECES
    M = PIECES
    with Stage(nc, tag) as c:
        ps = c.psum("ps", [P, J, 512])
        fed = c.sb("fed", [P, J, len(terms), P])
        multiplied, drained, biased, relued, copied = c.sems("multiplied", "drained", "biased", "relued", "copied")
        block = c.block()

        @block.gpsimd
        def _(gp):
            with gp.Fori(0, TURNS) as i:
                for j in range(J):
                    gp.wait_ge(multiplied, i * (M * J) + M * j + M)
                    for q, (turned, _) in enumerate(terms):
                        nc.gpsimd.tensor_copy(fed[:, j, q, :], turned[:, bass.ds((i * J + j) * P, P)]).then_inc(copied, 1)

        @block.tensor
        def _(pe):
            nc.tensor.sem_inc(multiplied, M * J)
            with pe.Fori(0, TURNS) as i:
                for m in range(M * J):
                    j, b = divmod(m, M)
                    if b == 0:
                        pe.wait_ge(copied, (i * J + j + 1) * len(terms))
                    pe.wait_ge(drained, i * (M * J) + m + 1)
                    for n, (_, weights) in enumerate(terms):
                        last = nc.tensor.matmul(ps[:, m % J, 0:W], fed[:, j, n, :], weights[:, b * W:b * W + W],
                                                start=(n == 0), stop=(n == len(terms) - 1))
                    last.then_inc(multiplied, 1)

        @block.vector
        def _(dve):
            nc.vector.sem_inc(drained, J)
            with dve.Fori(0, TURNS) as i:
                for m in range(M * J):
                    j, b = divmod(m, M)
                    part = acc[:, bass.ds(i * J + j, 1), b * W:b * W + W].rearrange("p a f -> p (a f)")
                    dve.wait_ge(multiplied, i * (M * J) + m + 1 + M * J)
                    nc.vector.scalar_tensor_tensor(part, part, k.dinv[:, bass.ds(i * J + j, 1)], ps[:, m % J, 0:W],
                                                   ALU.mult, ALU.add).then_inc(drained, 1)
                    dve.wait_ge(drained, i * (M * J) + m + 1 + J)
                    nc.vector.tensor_tensor(part, part, bias[:, b * W:b * W + W], ALU.add).then_inc(biased, 1)
            if mean:
                F = width // K
                for n in range(1, K):
                    dve.wait_ge(relued, TURNS if n == 1 else TURNS)
                    if n > 1:
                        dve.wait_ge(biased, TURNS * M * J + 1)
                    nc.vector.tensor_tensor(acc[:, :, 0:F], acc[:, :, 0:F], acc[:, :, n * F:n * F + F],
                                            ALU.add).then_inc(biased, 1)

        @block.scalar
        def _(act):
            with act.Fori(0, TURNS) as i:
                for j in range(J):
                    act.wait_ge(biased, i * (M * J) + M * j + M)
                    nc.scalar.nop(nofuse=True)
                    part = acc[:, bass.ds(i * J + j, 1), 0:width]
                    last = nc.scalar.activation(part, part, ACT.Relu, scale=1.0 / K if mean else 1.0)
                last.then_inc(relued, 1)


def turn_stage(nc, k, tag, source, target, blocks=1, scale=None, relu=False):
    M = blocks
    with Stage(nc, tag) as c:
        fed = c.sb("fed", [P, J, M * P])
        ps = c.psum("ps", [P, J, 512])
        turned, copied, made = c.sems("turned", "copied", "made")
        block = c.block()

        @block.vector
        def _(dve):
            with dve.Fori(0, TURNS) as i:
                for j in range(J):
                    dve.wait_ge(turned, i * (M * J) + M * j + M)
                    part = source[:, bass.ds(i * J + j, 1), 0:M * P].rearrange("p a f -> p (a f)")
                    if scale is None:
                        last = nc.vector.tensor_copy(fed[:, j, :], part)
                    else:
                        last = nc.vector.tensor_scalar(fed[:, j, :], part, scale[:, bass.ds(i * J + j, 1)], None, ALU.mult)
                    last.then_inc(made, 1)

        @block.tensor
        def _(pe):
            nc.tensor.sem_inc(turned, M * J)
            with pe.Fori(0, TURNS) as i:
                for m in range(M * J):
                    j, b = divmod(m, M)
                    if b == 0:
                        pe.wait_ge(made, i * J + j + 1)
                    pe.wait_ge(copied, i * (M * J) + m + 1)
                    nc.tensor.transpose(ps[:, m % J, 0:P], fed[:, j, b * P:b * P + P], k.ident[:, :]).then_inc(turned, 1)

        @block.scalar
        def _(act):
            nc.scalar.sem_inc(copied, J)
            with act.Fori(0, TURNS) as i:
                for m in range(M * J):
                    j, b = divmod(m, M)
                    act.wait_ge(turned, i * (M * J) + m + 1 + M * J)
                    nc.scalar.nop(nofuse=True)
                    nc.scalar.activation(target[:, b, bass.ds((i * J + j) * P, P)], ps[:, m % J, 0:P],
                                         ACT.Relu if relu else ACT.Copy).then_inc(copied, 1)


def turn_back_stage(nc, k, tag, source):
    with Stage(nc, tag) as c:
        fed = c.sb("fed", [P, J, P])
        ps = c.psum("ps", [P, J, 512])
        turned, added, copied = c.sems("turned", "added", "copied")
        block = c.block()

        @block.scalar
        def _(act):
            with act.Fori(0, TURNS) as i:
                for j in range(J):
                    act.wait_ge(turned, i * J + j + 1)
                    nc.scalar.copy(fed[:, j, :], source[:, bass.ds((i * J + j) * P, P)]).then_inc(copied, 1)

        @block.tensor
        def _(pe):
            nc.tensor.sem_inc(turned, J)
            with pe.Fori(0, TURNS) as i:
                for j in range(J):
                    pe.wait_ge(copied, i * J + j + 1)
                    pe.wait_ge(added, i * J + j + 1)
                    nc.tensor.transpose(ps[:, j, 0:P], fed[:, j, :], k.ident[:, :]).then_inc(turned, 1)

        @block.vector
        def _(dve):
            nc.vector.sem_inc(added, J)
            with dve.Fori(0, TURNS) as i:
                for j in range(J):
                    part = k.xcur[:, bass.ds(i * J + j, 1), :].rearrange("p a f -> p (a f)")
                    dve.wait_ge(turned, i * J + j + 1 + J)
                    nc.vector.tensor_tensor(part, part, ps[:, j, 0:P], ALU.add).then_inc(added, 1)


def layer_norm_stage(nc, k, tag, addend=None, scale=None, bias=None):
    with Stage(nc, tag) as c:
        stats = c.sb("stats", [P, NT, 6])
        mean = c.sb("mean", [P, NT, 2])
        root = c.sb("root", [P, NT])
        step, rooting, rooted = c.sems("step", "rooting", "rooted")
        block = c.block()

        @block.vector
        def _(dve):
            done = 0

            def then(inst):
                nonlocal done
                done += 1
                inst.then_inc(step, 1)
                dve.wait_ge(step, done)

            if addend is not None:
                if scale is not None:
                    then(nc.vector.tensor_tensor(addend, addend, scale[:, :, None].to_broadcast([P, NT, D]), ALU.mult))
                then(nc.vector.tensor_tensor(k.xcur[:, :, :], k.xcur[:, :, :], addend, ALU.add))
            if bias is not None:
                then(nc.vector.tensor_tensor(k.xcur[:, :, :], k.xcur[:, :, :],
                                             bias[:, None, :].to_broadcast([P, NT, D]), ALU.add))
            for t in range(NT):
                last = nc.vector.bn_stats(stats[:, t, :], k.xcur[:, t, :])
            then(last)
            for t in range(NT):
                last = nc.vector.bn_aggr(mean[:, t, :], stats[:, t, :])
            then(last)
            nc.vector.tensor_scalar(root[:, :], mean[:, :, 1], EPS, None, ALU.add).then_inc(rooting, 1)
            dve.wait_ge(rooted, 1)
            then(nc.vector.reciprocal(root[:, :], root[:, :]))
            then(nc.vector.tensor_tensor(k.xcur[:, :, :], k.xcur[:, :, :],
                                         mean[:, :, 0:1].to_broadcast([P, NT, D]), ALU.subtract))
            then(nc.vector.tensor_tensor(k.xcur[:, :, :], k.xcur[:, :, :],
                                         root[:, :, None].to_broadcast([P, NT, D]), ALU.mult))

        @block.scalar
        def _(act):
            act.wait_ge(rooting, 1)
            nc.scalar.activation(root[:, :], root[:, :], ACT.Sqrt).then_inc(rooted, 1)


def batch_norm_stage(nc, k, tag, h, blocks, gamma, beta):
    with Stage(nc, tag) as c:
        mean = c.sb("mean", [P, blocks])
        var = c.sb("var", [P, blocks])
        root = c.sb("root", [P, blocks])
        spare = c.sb("squares", [P, NP])
        params = c.sb("params", [P, 2, blocks])
        loaded, step, centred, rooted, scaled, done_act = c.sems(
            "loaded", "step", "centred", "rooted", "scaled", "done_act")
        block = c.block()

        @block.sync
        def _(sp):
            with nc.allow_non_contiguous_dma(reason="one value per partition"):
                for n, a in enumerate((gamma, beta)):
                    sp.dma_start(params[:, n, :], a.rearrange("(b p) -> p b", p=P)).then_inc(loaded, 16)

        @block.vector
        def _(dve):
            done = 0

            def then(inst):
                nonlocal done
                done += 1
                inst.then_inc(step, 1)
                dve.wait_ge(step, done)

            then(nc.vector.tensor_reduce(mean[:, :], h[:, :, 0:N], AX.X, ALU.add))
            nc.vector.tensor_scalar(mean[:, :], mean[:, :], -1.0 / N, None, ALU.mult).then_inc(centred, 1)
            dve.wait_ge(centred, 1)
            dve.wait_ge(rooted, 1)
            then(nc.vector.reciprocal(root[:, :], root[:, :]))
            dve.wait_ge(loaded, 32)
            then(nc.vector.tensor_tensor(root[:, :], root[:, :], params[:, 0, :], ALU.mult))
            then(nc.vector.tensor_tensor(mean[:, :], mean[:, :], root[:, :], ALU.mult))
            nc.vector.tensor_tensor(mean[:, :], mean[:, :], params[:, 1, :], ALU.add).then_inc(scaled, 1)

        @block.scalar
        def _(act):
            act.wait_ge(centred, 1)
            for b in range(blocks):
                if b:
                    act.wait_ge(done_act, b)
                nc.scalar.activation(spare[:, 0:N], h[:, b, 0:N], ACT.Square, bias=mean[:, b:b + 1],
                                     accum_out=var[:, b:b + 1]).then_inc(done_act, 1)
            act.wait_ge(done_act, blocks)
            nc.scalar.activation(var[:, :], var[:, :], ACT.Copy, scale=1.0 / N, bias=EPS).then_inc(done_act, 1)
            act.wait_ge(done_act, blocks + 1)
            nc.scalar.activation(root[:, :], var[:, :], ACT.Sqrt).then_inc(rooted, 1)
            act.wait_ge(scaled, 1)
            for b in range(blocks):
                nc.scalar.activation(h[:, b, :], h[:, b, :], ACT.Relu, bias=mean[:, b:b + 1], scale=root[:, b:b + 1])


def feature_stage(nc, k, tag, out, terms, bias):
    W = 400
    PARTS = NP // W
    B = out.shape[1]
    with Stage(nc, tag) as c:
        ps = c.psum("ps", [P, 8, 512])
        multiplied, drained = c.sems("multiplied", "drained")
        block = c.block()

        @block.tensor
        def _(pe):
            for b in range(B):
                for n in range(PARTS):
                    if b:
                        pe.wait_ge(drained, (b - 1) * PARTS + n + 1)
                    for t, (weights, turned) in enumerate(terms):
                        last = nc.tensor.matmul(ps[:, n, 0:W], weights[:, b * P:b * P + P], turned[:, n * W:n * W + W],
                                                start=(t == 0), stop=(t == len(terms) - 1))
                    last.then_inc(multiplied, 1)

        @block.scalar
        def _(act):
            for b in range(B):
                for n in range(PARTS):
                    act.wait_ge(multiplied, b * PARTS + n + 1)
                    nc.scalar.activation(out[:, b, n * W:n * W + W], ps[:, n, 0:W], ACT.Relu,
                                         bias=bias[:, b:b + 1]).then_inc(drained, 1)


def load_weights_stage(nc, k, tag, loads):
    with Stage(nc, tag) as c:
        (loaded,) = c.sems("loaded")
        block = c.block()

        @block.sync
        def _(sp):
            with nc.allow_non_contiguous_dma(reason="weights and biases, small"):
                for to, source in loads:
                    sp.dma_start(to, source).then_inc(loaded, 16)
            if loads:
                sp.wait_ge(loaded, 16 * len(loads))


def setup(nc, c):
    k = Chip()

    def sb(name, shape, dt=F32):
        return c.enter_context(nc.sbuf_tensor(name, shape, dt))

    k.xcur = sb("xcur", [P, NT, D])
    k.xT = sb("xT", [P, NP])
    k.iota = sb("iota", [P, C])
    k.iota16 = sb("iota16", [P, C], FP16)
    k.diff = sb("diff", [P, P])
    k.ident = sb("ident", [P, P])
    k.one = sb("one", [P, 1])
    k.count = sb("count", [P, NT, S2])
    k.factor = sb("factor", [P, NT, S2])
    k.dinv = sb("dinv", [P, NT])
    k.dinv_loop = sb("dinv_loop", [P, NT])
    k.arrived = [nc.alloc_semaphore(f"gathered{u}") for u in range(U)]
    k.arrivals = [0] * U
    k.orders = []
    for key in (0, 1):
        o = Chip()
        o.key = key
        o.first = R * key
        o.row = sb(f"row{key}", [P, C], I32)
        o.local = sb(f"local{key}", [P, C])
        if key:
            o.other = sb(f"other{key}", [P, C], I32)
            o.minus_local = sb(f"minus_local{key}", [P, C])
        o.type = sb(f"type{key}", [P, C])
        o.coef = sb(f"coef{key}", [P, C])
        o.tile_of_chunk = sb(f"tile_of_chunk{key}", [P, C], I32)
        k.orders.append(o)
    return k


def sort_inputs(c, o):
    (o.local_in, o.minus_local_in, o.high_in, o.low_in, o.group_in, o.slot_in, o.chunk_in) = (
        c.sb(name, [P, EC]) for name in ("local_in", "minus_local_in", "high_in", "low_in", "group_in",
                                         "slot_in", "chunk_in"))


def sort_by_dst(nc, k):
    o = k.orders[1]
    with Stage(nc, "sort1") as c:
        sort_inputs(c, o)
        rank_stage(nc, k, o)
        job = Permute(nc, c, k, o)
        job.start_stage()
        run_job_stage(nc, "permute1", job)
        job.end_stage()
    degree_stage(nc, k)



def arma_layer(nc, k, A, dram):
    by_dst = k.orders[1]

    with Stage(nc, "arma1") as c:
        ax = c.sb("ax", [P, NT, D])
        out1T = c.sb("out1T", [P, K * HID // P, NP])
        axT = c.sb("axT", [P, 1, NP])
        init_w = c.sb("init_w", [P, K, HID])
        root_w = c.sb("root_w", [P, K, HID])
        w = c.sb("w", [P, K, HID // P, HID])
        bias = c.sb("bias", [P, K * HID // P])
        loads = [
            (init_w[:, :, :], A["L0_gnn_init_w1"].rearrange("k f g -> f k g")),
            (root_w[:, :, :], A["L0_gnn_root_w1"][0].rearrange("k f g -> f k g")),
            (w[:, :, :, :].rearrange("p k b h -> p (k b) h"),
             A["L0_gnn_w1"][0].rearrange("k (b p) h -> p (k b) h", p=P)),
            (bias[:, :], A["L0_gnn_b1"][0].rearrange("k o (b p) -> p (k o b)", p=P))]
        scaled_x_stage(nc, k, dram["x_scaled"])
        with Stage(nc, "sort0") as d:
            sort = Permute(nc, d, k, k.orders[0])
            sort.start_stage()
            edge_sum_stage(nc, k, "sum_x", by_dst, by_dst.other, dram["x_scaled"][:, :], D, ax, jobs=[sort],
                           zero=True, loads=loads, scalar_makes=2)
            sort.end_stage()
        factor_stage(nc, k)
        turn_stage(nc, k, "turn_ax", ax, axT, scale=k.dinv)
        feature_stage(nc, k, "arma1_out", out1T,
                      [(init_w[:, :, :].rearrange("p k g -> p (k g)"), axT[:, 0, :]),
                       (root_w[:, :, :].rearrange("p k g -> p (k g)"), k.xT[:, :])], bias)
        table_stage(nc, k, "arma1_table",
                    [piece(s * HID, HID, [(out1T[:, s * 2 + b, :], w[:, s, b, :]) for b in range(HID // P)])
                     for s in range(K)], [(dram["arma1"], 0, K * HID)], K * HID, scale=k.dinv)

    with Stage(nc, "arma2") as c2:
        hT = c2.sb("hT", [P, HID // P, NP])
        with Stage(nc, "arma1_end") as c:
            acc = c.sb("acc", [P, NT, K * HID])
            root_w = c.sb("root_w", [P, K, HID])
            bias = c.sb("bias", [P, K * HID])
            loads = [
                (root_w[:, :, :], A["L0_gnn_root_w1"][1].rearrange("k f g -> f k g")),
                (bias[:, :], A["L0_gnn_b1"][1].rearrange("k o g -> o (k g)").to_broadcast([P, K * HID]))]
            edge_sum_stage(nc, k, "sum_arma1", by_dst, by_dst.other, dram["arma1"][:, :], K * HID, acc,
                           zero=True, loads=loads)
            combine_stage(nc, k, "arma1_combine", acc, K * HID,
                          [(k.xT[:, :], root_w[:, :, :].rearrange("p k g -> p (k g)"))], bias, mean=True)
            turn_stage(nc, k, "turn_h", acc, hT, blocks=HID // P)
        batch_norm_stage(nc, k, "norm_h", hT, HID // P, A["L0_gnn_gamma1"], A["L0_gnn_beta1"])

        G = HID // P
        init_w = c2.sb("init_w", [P, G, K, D])
        root_w = c2.sb("root_w", [P, 2, G, K, D])
        w = c2.sb("w", [P, K, D])
        bias = c2.sb("bias", [P, 2, K * D])
        acc = c2.sb("acc", [P, NT, K * D])
        load_weights_stage(nc, k, "arma2_load", [
            *((init_w[:, b, :, :], A["L0_gnn_init_w2"][:, b * P:b * P + P, :].rearrange("k f g -> f k g"))
              for b in range(G)),
            *((root_w[:, t, b, :, :], A["L0_gnn_root_w2"][t, :, b * P:b * P + P, :].rearrange("k f g -> f k g"))
              for t in (0, 1) for b in range(G)),
            (w[:, :, :], A["L0_gnn_w2"][0].rearrange("k f g -> f k g")),
            *((bias[:, t, :], A["L0_gnn_b2"][t].rearrange("k o g -> o (k g)").to_broadcast([P, K * D]))
              for t in (0, 1))])

        def flat(weights):
            return weights.rearrange("p k g -> p (k g)")

        roots = [[(hT[:, b, :], flat(root_w[:, t, b, :, :])) for b in range(G)] for t in (0, 1)]
        table_stage(nc, k, "arma2_table0",
                    [piece(0, K * D, [(hT[:, b, :], flat(init_w[:, b, :, :])) for b in range(G)])],
                    [(dram["arma2"], 0, K * D)], K * D, scale=k.dinv)
        edge_sum_stage(nc, k, "sum_arma2", by_dst, by_dst.other, dram["arma2"][:, :], K * D, acc, zero=True)
        combine_stage(nc, k, "arma2_combine0", acc, K * D, roots[0], bias[:, 0, :], mean=False)
        with Stage(nc, "arma2_mid") as c:
            outT = c.sb("outT", [P, K, NP])
            turn_stage(nc, k, "turn_out", acc, outT, blocks=K)
            table_stage(nc, k, "arma2_table1",
                        [piece(s * D, D, [(outT[:, s, :], w[:, s, :])]) for s in range(K)],
                        [(dram["arma2"], 0, K * D)], K * D, scale=k.dinv)
        edge_sum_stage(nc, k, "sum_arma3", by_dst, by_dst.other, dram["arma2"][:, :], K * D, acc, zero=True)
        combine_stage(nc, k, "arma2_combine1", acc, K * D, roots[1], bias[:, 1, :], mean=True)
        h2T = c2.sb("h2T", [P, 1, NP])
        turn_stage(nc, k, "turn_h2", acc, h2T)
        batch_norm_stage(nc, k, "norm_h2", h2T, 1, A["L0_gnn_gamma2"], A["L0_gnn_beta2"])
        turn_back_stage(nc, k, "arma_back", h2T[:, 0, :])
    layer_norm_stage(nc, k, "norm0")
    turn_stage(nc, k, "turn0", k.xcur, k.xT[:, None, :])


def scaled_x_stage(nc, k, table):
    with Stage(nc, "scaled_x") as c:
        rows = c.sb("rows", [P, NT, D])
        ps = c.psum("ps", [P, J, 512])
        made, stored, turned, copied = c.sems("made", "stored", "turned", "copied")
        block = c.block()

        @block.vector
        def _(dve):
            nc.vector.tensor_tensor(rows[:, :, :], k.xcur[:, :, :], k.dinv[:, :, None].to_broadcast([P, NT, D]),
                                    ALU.mult).then_inc(made, 1)

        @block.sync
        def _(sp):
            sp.wait_ge(made, 1)
            sp.dma_start(table.rearrange("(t p) f -> p t f", p=P), rows[:, :, :]).then_inc(stored, 16)
            sp.wait_ge(stored, 16)
    turn_stage(nc, k, "turn_x", k.xcur, k.xT[:, None, :])


def sum_with_factors(nc, k, tag, order, *args, **more):
    with Stage(nc, f"factors{order.key}") as c:
        job = EdgeFactors(nc, c, k, order)
        job.start_stage()
        edge_sum_stage(nc, k, tag, *args, **more, jobs=[job])


def gcn_layer(nc, k, A, dram):
    xT = k.xT[:, :]
    by_dst = k.orders[1]
    with Stage(nc, "gcn") as c:
        w = c.sb("w", [P, D])
        bias = c.sb("bias", [P, D])
        acc = c.sb("acc", [P, NT, D])
        load_weights_stage(nc, k, "gcn_load", [
            (w[:, :], A["L1_gnn_W"]), (bias[:, :], A["L1_gnn_b"][None, :].to_broadcast([P, D]))])
        table_stage(nc, k, "gcn_table", [piece(0, D, [(xT, w[:, :])]),
                                         piece(0, D, [(xT, w[:, :])], target=acc)],
                    [(dram["narrow"], 0, D)], D, scale=k.dinv_loop)
        sum_with_factors(nc, k, "sum_gcn", k.orders[0], by_dst, by_dst.other, dram["narrow"][:, :], D, acc)
        layer_norm_stage(nc, k, "norm1", acc[:, :, :], scale=k.dinv_loop, bias=bias)
    turn_stage(nc, k, "turn1", k.xcur, k.xT[:, None, :])


def rgcn_layer(nc, k, A, dram):
    xT = k.xT[:, :]
    S = S2 + 1
    with Stage(nc, "rgcn") as c:
        acc = c.sb("acc", [P, NT, D])
        for layer in (0, 1):
            with Stage(nc, f"rgcn{layer}") as d:
                w = d.sb("w", [P, S, D])
                bias = d.sb("bias", [P, S, D])
                load_weights_stage(nc, k, f"rgcn_load{layer}", [
                    (w[:, :, :], A["L2_gnn_rgcn_weights"][layer].rearrange("s f g -> f s g")),
                    (bias[:, :, :].rearrange("p s g -> p (s g)"),
                     A["L2_gnn_rgcn_biases"][layer:layer + 1].rearrange("o s g -> o (s g)").to_broadcast([P, S * D]))])
                pieces = []
                for s in range(0, S2, 4):
                    n = min(4, S2 - s)
                    pieces.append(piece(s * D, n * D, [(xT, w[:, s:s + n, :].rearrange("p s g -> p (s g)"))],
                                        bias=bias[:, s:s + n, :].rearrange("p s g -> p (s g)")))
                pieces.append(piece(0, D, [(xT, w[:, S2, :])], bias=bias[:, S2, :], target=acc))
                table_stage(nc, k, f"rgcn_table{layer}", pieces,
                            [(dram["by_src"], 0, R * D), (dram["by_dst"], R * D, R * D)], S2 * D)
            root_scale_stage(nc, k, f"root{layer}", acc)
            for o, name in zip(k.orders, ("by_src", "by_dst")):
                args = (o, o.row, dram[name].rearrange("n (r f) -> (n r) f", f=D), D, acc, o.coef)
                if layer == 0 and name == "by_src":
                    sum_with_factors(nc, k, f"sum_rgcn{layer}_{name}", k.orders[1], *args)
                else:
                    edge_sum_stage(nc, k, f"sum_rgcn{layer}_{name}", *args)
            if layer == 0:
                turn_stage(nc, k, "turn_rgcn", acc, k.xT[:, None, :], relu=True)
        layer_norm_stage(nc, k, "norm2", acc[:, :, :])
    turn_stage(nc, k, "turn2", k.xcur, k.xT[:, None, :])


def root_scale_stage(nc, k, tag, acc):
    with Stage(nc, tag) as c:
        block = c.block()

        @block.vector
        def _(dve):
            nc.vector.tensor_tensor(acc[:, :, :], acc[:, :, :], k.factor[:, :, 0:1].to_broadcast([P, NT, D]), ALU.mult)


def neighbour_layer(nc, k, A, dram):
    xT = k.xT[:, :]
    by_dst = k.orders[1]
    with Stage(nc, "neighbour") as c:
        w = c.sb("w", [P, 2, D])
        wT = c.sb("wT", [P, 2, D])
        bias = c.sb("bias", [P, 2, D])
        acc = c.sb("acc", [P, NT, D])
        load_weights_stage(nc, k, "neighbour_load", [
            (w[:, 0, :], A["L3_gnn_W_neigh"]), (w[:, 1, :], A["L3_gnn_W_self"]),
            (bias[:, 0, :], A["L3_gnn_b_neigh"][None, :].to_broadcast([P, D])),
            (bias[:, 1, :], A["L3_gnn_b_self"][None, :].to_broadcast([P, D]))])
        with Stage(nc, "neighbour_turn") as d:
            ps = d.psum("ps", [P, 2, 512])
            (turned,) = d.sems("turned")
            block = d.block()

            @block.tensor
            def _(pe):
                for n in (0, 1):
                    last = nc.tensor.transpose(ps[:, n, 0:D], w[:, n, :], k.ident[:, :])
                last.then_inc(turned, 1)

            @block.vector
            def _(dve):
                nc.vector.tensor_tensor(bias[:, 0, :], bias[:, 0, :], bias[:, 1, :], ALU.add)
                dve.wait_ge(turned, 1)
                nc.vector.tensor_copy(wT[:, :, :], ps[:, :, 0:D])
        table_stage(nc, k, "neighbour_table", [piece(0, D, [(xT, wT[:, 0, :])]),
                                               piece(0, D, [(xT, wT[:, 1, :])], bias=bias[:, 0, :], target=acc)],
                    [(dram["narrow"], 0, D)], D)
        edge_sum_stage(nc, k, "sum_neighbour", by_dst, by_dst.other, dram["narrow"][:, :], D, acc)
        layer_norm_stage(nc, k, "norm3", acc[:, :, :])


def store_stage(nc, k, out):
    with Stage(nc, "store") as c:
        (stored,) = c.sems("stored")
        block = c.block()

        @block.sync
        def _(sp):
            sp.dma_start(out[0:(NT - 1) * P, :].rearrange("(t p) f -> p t f", p=P),
                         k.xcur[:, 0:NT - 1, :]).then_inc(stored, 16)
            sp.dma_start(out[(NT - 1) * P:N, :], k.xcur[0:LAST, NT - 1, :]).then_inc(stored, 16)
            sp.wait_ge(stored, 32)


def gnn_kernel(nc, A, out):
    dram = {name: nc.dram_tensor(name, (NP, width), F32, kind="Internal").ap()
            for name, width in (("x_scaled", D), ("arma1", K * HID), ("arma2", K * D), ("narrow", D),
                                ("by_src", R * D), ("by_dst", R * D))}
    with ExitStack() as c:
        k = setup(nc, c)
        with Stage(nc, "graph") as g:
            sort_inputs(g, k.orders[0])
            with Stage(nc, "lists") as h:
                k.edges = h.sb("edges", [P, 3, EC], I32)
                load_stage(nc, k, A)
                sort_by_dst(nc, k)
                rank_stage(nc, k, k.orders[0])
            arma_layer(nc, k, A, dram)
        gcn_layer(nc, k, A, dram)
        rgcn_layer(nc, k, A, dram)
        neighbour_layer(nc, k, A, dram)
        store_stage(nc, k, out)


NAMES = ["x", "src", "dst", "edge_type_9",
         "L0_gnn_init_w1", "L0_gnn_w1", "L0_gnn_root_w1", "L0_gnn_b1",
         "L0_gnn_init_w2", "L0_gnn_w2", "L0_gnn_root_w2", "L0_gnn_b2",
         "L0_gnn_gamma1", "L0_gnn_beta1", "L0_gnn_gamma2", "L0_gnn_beta2",
         "L1_gnn_W", "L1_gnn_b", "L2_gnn_rgcn_weights", "L2_gnn_rgcn_biases",
         "L3_gnn_W_neigh", "L3_gnn_b_neigh", "L3_gnn_W_self", "L3_gnn_b_self"]


def kernel(**inputs):
    import numpy as np
    import concourse.bacc as bacc
    from concourse.bass_utils import run_bass_kernel_spmd

    nc = bacc.Bacc("TRN2", target_bir_lowering=False, num_devices=1)
    arrays, args = {}, {}
    for name in NAMES:
        a = np.ascontiguousarray(inputs[name])
        arrays[f"in_{name}"] = a
        args[name] = nc.dram_tensor(f"in_{name}", a.shape, mybir.dt.from_np(a.dtype), kind="ExternalInput").ap()
    out = nc.dram_tensor("out_0", (N, D), F32, kind="ExternalOutput").ap()
    gnn_kernel(nc, args, out)
    return run_bass_kernel_spmd(nc, [arrays], core_ids=[0]).results[0]["out_0"]
```

```python
import concourse.bass as bass
from concourse import mybir
from contextlib import ExitStack

F32, BF16, FP16, I32 = mybir.dt.float32, mybir.dt.bfloat16, mybir.dt.float16, mybir.dt.int32
PE, DVE = mybir.EngineType.PE, mybir.EngineType.DVE
ALU, ACT, AX = mybir.AluOpType, mybir.ActivationFunctionType, mybir.AxisListType

P = 128
N = 3125
E = 50000
D = 128
R = 9
K = 3
HID = 256
EPS = 1e-5
NT = -(-N // P)
NP = NT * P
LAST = N - (NT - 1) * P
EP = 125
EC = E // EP
U = 16
C = -(-(E // P + NT + 1) // U) * U
S2 = 2 * R
PARTS = 3
J = 5
TURNS = NT // J
TURNS_OF_CHUNKS = C // U
LAG = 2
LEAD = 8


class Chip:
    pass


class Stage(ExitStack):

    def __init__(self, nc, tag):
        super().__init__()
        self.nc, self.tag = nc, tag

    def sb(self, name, shape, dt=F32):
        return self.enter_context(self.nc.sbuf_tensor(f"{name}_{self.tag}", shape, dt))

    def psum(self, name, shape, dt=F32):
        return self.enter_context(self.nc.psum_tensor(f"{name}_{self.tag}", shape, dt))

    def sems(self, *names):
        sems = [self.nc.alloc_semaphore(f"{n}_{self.tag}") for n in names]
        self.callback(self.give_back, sems)
        return sems

    def give_back(self, sems):
        for s in sems:
            self.nc.sync.sem_clear(s)
            self.nc.release_semaphore(s)

    def block(self):
        return self.enter_context(self.nc.Block())



def load_stage(nc, k, A):
    with Stage(nc, "load") as c:
        loaded, zeroed, made = c.sems("loaded", "zeroed", "made")
        block = c.block()

        @block.sync
        def _(sp):
            sp.wait_ge(zeroed, 1)
            sp.dma_start(k.xcur[:, 0:NT - 1, :],
                         A["x"][0:(NT - 1) * P, :].rearrange("(t p) f -> p t f", p=P)).then_inc(loaded, 16)
            sp.dma_start(k.xcur[0:LAST, NT - 1, :], A["x"][(NT - 1) * P:N, :]).then_inc(loaded, 16)
            sp.wait_ge(loaded, 16 * 5)

        @block.scalar
        def _(act):
            for i, name in enumerate(("src", "dst", "edge_type_9")):
                act.dma_start(k.edges[0:EP, i, :], A[name].rearrange("(p c) -> p c", p=EP)).then_inc(loaded, 16)

        @block.vector
        def _(dve):
            nc.vector.memset(k.xcur[:, :, :], 0.0).then_inc(zeroed, 1)
            nc.vector.memset(k.one[:, :], 1.0)

        @block.gpsimd
        def _(gp):
            nc.gpsimd.iota(k.iota[:, :], [[1, C]], base=0, channel_multiplier=0,
                           allow_small_or_imprecise_dtypes=True)
            nc.gpsimd.iota(k.iota16[:, :], [[1, C]], base=0, channel_multiplier=0,
                           allow_small_or_imprecise_dtypes=True)
            nc.gpsimd.iota(k.diff[:, :], [[1, P]], base=0, channel_multiplier=-1,
                           allow_small_or_imprecise_dtypes=True).then_inc(made, 1)
            gp.wait_ge(made, 1)
            nc.gpsimd.tensor_scalar(k.ident[:, :], k.diff[:, :], 0.0, None, ALU.is_equal)
            nc.gpsimd.tensor_scalar(k.ident16[:, :], k.diff[:, :], 0.0, None, ALU.is_equal)



def rank_stage(nc, k, o):
    other = 1 - o.key
    B = J
    W = EC
    BLOCKS = NT
    with Stage(nc, f"rank{o.key}") as c:
        sb = c.sb
        ps = c.psum("ps", [P, 8, 512])
        last_chunk = sb("chunks_up_to_tile", [NT, 2, NT], F32)
        after = sb("chunk_is_after_tile", [NT, C], BF16)
        ints = sb("ints", [P, 4, EC], I32)
        tile_of = sb("tile_of", [P, EC], F32)
        one_hot = sb("tile_one_hot", [P, NT, EC], BF16)
        ones = sb("ones_bf", [P, P], BF16)
        triangle = sb("triangle", [P, P], BF16)
        total = sb("column_total", [P, NT * EC], F32)
        upto = sb("edges_up_to", [P, NT * EC], F32)
        cum = sb("cum", [P, NT + 1], F32)
        size = sb("size", [P, NT], F32)
        sizei = sb("sizei", [P, NT], I32)
        first = sb("first_chunk", [P, NT + 1], F32)
        shift = sb("shift", [P, NT], F32)
        pos = sb("pos", [P, EC], F32)
        step, hot, counted, kept, placed, compared, summed = c.sems(
            "step", "hot", "counted", "kept", "placed", "compared", "summed")
        block = c.block()
        flat = one_hot[:, :, :].rearrange("p b c -> p (b c)")

        @block.vector
        def _(dve):
            done = 0

            def then(inst):
                nonlocal done
                done += 1
                inst.then_inc(step, 1)
                dve.wait_ge(step, done)

            key = k.edges[0:EP, o.key, :]
            e = slice(0, EP)
            nc.vector.tensor_single_scalar(ints[e, 0, :], key, 7, ALU.arith_shift_right)
            then(nc.vector.tensor_single_scalar(ints[e, 1, :], key, P - 1, ALU.bitwise_and))
            nc.vector.tensor_copy(o.local_in[e, :], ints[e, 1, :])
            then(nc.vector.tensor_scalar(pos[e, :], k.edges[e, other, :], float(R), None, ALU.mult))
            then(nc.vector.tensor_tensor(pos[e, :], pos[e, :], k.edges[e, 2, :], ALU.add))
            then(nc.vector.tensor_scalar(pos[e, :], pos[e, :], float(P), 1.0, ALU.mult, ALU.add))
            then(nc.vector.tensor_tensor(ints[e, 2, :], pos[e, :], o.local_in[e, :], ALU.add))
            nc.vector.tensor_single_scalar(ints[e, 3, :], ints[e, 2, :], 11, ALU.arith_shift_right)
            then(nc.vector.tensor_single_scalar(ints[e, 2, :], ints[e, 2, :], 2047, ALU.bitwise_and))
            nc.vector.tensor_copy(o.high_in[e, :], ints[e, 3, :])
            nc.vector.tensor_copy(o.low_in[e, :], ints[e, 2, :])
            then(nc.vector.tensor_copy(tile_of[e, :], ints[e, 0, :]))
            nc.vector.tensor_scalar(o.group_in[e, :], tile_of[e, :], float(R), None, ALU.mult)
            nc.vector.memset(ones[:, :], 1.0)
            nc.vector.tensor_scalar(triangle[:, :], k.diff[:, :], 0.0, 1.0, ALU.is_gt, ALU.subtract)
            for b in range(0, NT, B):
                nc.vector.tensor_tensor(one_hot[e, b:b + B, :],
                                        tile_of[e, None, :].to_broadcast([EP, B, EC]),
                                        k.iota[e, b:b + B, None].to_broadcast([EP, B, EC]),
                                        ALU.is_equal).then_inc(hot, 1)
            dve.wait_ge(hot, 1)
            nc.vector.tensor_tensor(o.group_in[e, :], o.group_in[e, :], k.edges[e, 2, :], ALU.add)
            nc.vector.sem_inc(placed, B)
            dve.wait_ge(kept, B + BLOCKS)
            then(nc.vector.tensor_tensor_scan(upto[:, :], total[:, :], total[:, :], 0.0, ALU.add, ALU.max))
            nc.vector.memset(cum[:, 0:1], 0.0)
            nc.vector.memset(first[:, 0:1], 0.0)
            then(nc.vector.tensor_copy(cum[:, 1:NT + 1],
                                       upto[:, :].rearrange("p (b c) -> p b c", c=EC)[:, :, EC - 1]))
            then(nc.vector.tensor_tensor(size[:, :], cum[:, 1:NT + 1], cum[:, 0:NT], ALU.subtract))
            then(nc.vector.tensor_scalar(sizei[:, :], size[:, :], float(P - 1), None, ALU.add))
            then(nc.vector.tensor_single_scalar(sizei[:, :], sizei[:, :], 7, ALU.arith_shift_right))
            then(nc.vector.tensor_copy(size[:, :], sizei[:, :]))
            then(nc.vector.tensor_tensor_scan(first[:, 1:NT + 1], size[:, :], size[:, :], 0.0, ALU.add, ALU.max))
            then(nc.vector.scalar_tensor_tensor(shift[:, :], first[:, 0:NT], float(P), cum[:, 0:NT],
                                                ALU.mult, ALU.subtract))
            then(nc.vector.tensor_tensor(last_chunk[:, 0, :], first[0:NT, 1:NT + 1], k.ident[0:NT, 0:NT], ALU.mult))
            then(nc.vector.tensor_reduce(last_chunk[:, 1, 0:1], last_chunk[:, 0, :], AX.X, ALU.add))
            nc.vector.tensor_scalar(after[:, :], k.iota[0:NT, 0:C], last_chunk[:, 1, 0:1], None,
                                    ALU.is_ge).then_inc(compared, 1)
            with dve.Fori(0, BLOCKS // B) as i:
                for b in range(B):
                    dve.wait_ge(counted, i * B + b + 1 + BLOCKS)
                    nc.vector.scalar_tensor_tensor(
                        upto[0:EP, bass.ds((i * B + b) * W, W)], ps[0:EP, 3 + b, 0:W],
                        shift[0:EP, bass.ds(i * B + b, 1)], upto[0:EP, bass.ds((i * B + b) * W, W)],
                        ALU.add, ALU.add).then_inc(placed, 1)
            dve.wait_ge(placed, B + BLOCKS)
            then(nc.vector.tensor_tensor(total[e, :], upto[e, :], flat[e, :], ALU.mult))
            then(nc.vector.tensor_reduce(pos[e, :], total[e, :].rearrange("p (b c) -> p c b", c=EC),
                                         AX.X, ALU.add))
            then(nc.vector.tensor_copy(ints[e, 0, :], pos[e, :]))
            nc.vector.tensor_single_scalar(ints[e, 1, :], ints[e, 0, :], P - 1, ALU.bitwise_and)
            then(nc.vector.tensor_single_scalar(ints[e, 2, :], ints[e, 0, :], 7, ALU.arith_shift_right))
            nc.vector.tensor_copy(o.slot_in[e, :], ints[e, 1, :])
            nc.vector.tensor_copy(o.chunk_in[e, :], ints[e, 2, :])
            dve.wait_ge(summed, 1)
            nc.vector.tensor_scalar_min(o.tile_of_chunk[:, :], ps[:, 0, 0:C], float(NT - 1))

        @block.tensor
        def _(pe):
            with pe.Fori(0, BLOCKS // B) as i:
                pe.wait_ge(hot, i + 1)
                for b in range(B):
                    pe.wait_ge(kept, i * B + b + 1)
                    nc.tensor.matmul(ps[:, b, 0:W], ones[0:EP, :], flat[0:EP, bass.ds((i * B + b) * W, W)],
                                     start=True, stop=True).then_inc(counted, 1)
            pe.wait_ge(kept, B + BLOCKS)
            with pe.Fori(0, BLOCKS // B) as i:
                for b in range(B):
                    pe.wait_ge(placed, i * B + b + 1)
                    nc.tensor.matmul(ps[0:EP, 3 + b, 0:W], triangle[0:EP, 0:EP],
                                     flat[0:EP, bass.ds((i * B + b) * W, W)],
                                     start=True, stop=True).then_inc(counted, 1)
            pe.wait_ge(compared, 1)
            nc.tensor.matmul(ps[:, 0, 0:C], ones[0:NT, :], after[:, :], start=True, stop=True).then_inc(summed, 1)

        @block.scalar
        def _(act):
            nc.scalar.sem_inc(kept, B)
            with act.Fori(0, BLOCKS // B) as i:
                for b in range(B):
                    act.wait_ge(counted, i * B + b + 1)
                    nc.scalar.nop(nofuse=True)
                    nc.scalar.copy(total[:, bass.ds((i * B + b) * W, W)], ps[:, b, 0:W]).then_inc(kept, 1)


class Job:

    def __init__(self, turns):
        self.turns = turns

    CLOSE = U - 1

    def at(self, u):
        return (u,)

    def tensor_at(self, u):
        return late(u)

    def vector_close(self, dve, i):
        pass


def run_job_stage(nc, tag, job):
    with Stage(nc, tag) as c:
        block = c.block()

        @block.vector
        def _(dve):
            with dve.Fori(0, job.turns) as i:
                for u in range(U):
                    job.vector(dve, i, u)

        @block.scalar
        def _(act):
            with act.Fori(0, job.turns) as i:
                for u in range(U):
                    job.scalar(act, i, u)

        @block.tensor
        def _(pe):
            with pe.Fori(0, job.turns) as i:
                for u in range(U):
                    job.tensor(pe, i, u)


class Permute(Job):

    G = NT * R
    V = 8

    def __init__(self, nc, c, k, o):
        super().__init__(EC // U)
        self.nc, self.k, self.o = nc, k, o
        self.ps = c.psum("ps", [P, 3, 512])
        self.zero = c.sb("zero", [1, 512], FP16)
        self.chunk = c.sb("chunk_one_hot", [P, self.V, C], FP16)
        self.slot = c.sb("slot_one_hot", [P, self.V, 2, P], FP16)
        self.group = c.sb("group_one_hot", [P, self.V, self.G], FP16)
        self.place = c.sb("place_one_hot", [P, self.V, P], FP16)
        self.local = c.sb("local_one_hot", [P, self.V, P], FP16)
        self.zeroed, self.column, self.placed, self.weighted, self.moved = c.sems(
            "zeroed", "column", "placed", "weighted", "moved")

    def start_stage(self):
        nc = self.nc
        with Stage(nc, f"permute_start{self.o.key}") as c:
            block = c.block()

            @block.vector
            def _(dve):
                nc.vector.memset(self.zero[:, :], 0.0).then_inc(self.zeroed, 1)

            @block.tensor
            def _(pe):
                pe.wait_ge(self.zeroed, 1)
                for b, w in ((0, C), (1, C), (2, self.G)):
                    last = nc.tensor.matmul(self.ps[:, b, 0:w], self.zero[0:1, 0:P], self.zero[0:1, 0:w],
                                            start=True, stop=False)
                last.then_inc(self.moved, self.V)

    def vector(self, dve, i, u):
        nc, k, o, e = self.nc, self.k, self.o, slice(0, EP)
        n, v = i * U + u, u % self.V
        col = bass.ds(n, 1)
        dve.wait_ge(self.moved, n + 1)
        nc.vector.tensor_scalar(self.place[e, v, :], k.iota16[e, 0:P], o.slot_in[e, col], None,
                                ALU.is_equal).then_inc(self.placed, 1)
        nc.vector.tensor_scalar(self.chunk[e, v, :], k.iota16[e, 0:C], o.chunk_in[e, col], None, ALU.is_equal)
        nc.vector.tensor_scalar(self.local[e, v, :], k.iota16[e, 0:P], o.local_in[e, col], None, ALU.is_equal)
        nc.vector.tensor_scalar(self.group[e, v, :], k.iota16[e, 0:self.G], o.group_in[e, col], None,
                                ALU.is_equal).then_inc(self.column, 1)

    def scalar(self, act, i, u):
        nc, k, o, e = self.nc, self.k, self.o, slice(0, EP)
        n, v = i * U + u, u % self.V
        act.wait_ge(self.placed, n + 1)
        nc.scalar.nop(nofuse=True)
        for half, code in enumerate((o.high_in, o.low_in)):
            last = nc.scalar.activation(self.slot[e, v, half, :], self.place[e, v, :], ACT.Copy,
                                        scale=code[e, bass.ds(n, 1)])
        last.then_inc(self.weighted, 1)

    def tensor(self, pe, i, u):
        nc, e = self.nc, slice(0, EP)
        n, v = i * U + u, u % self.V
        pe.wait_ge(self.column, n + 1)
        nc.tensor.matmul(self.ps[:, 2, 0:self.G], self.local[e, v, :], self.group[e, v, :],
                         start=False, stop=False)
        pe.wait_ge(self.weighted, n + 1)
        nc.tensor.matmul(self.ps[:, 0, 0:C], self.slot[e, v, 0, :], self.chunk[e, v, :], start=False, stop=False)
        nc.tensor.matmul(self.ps[:, 1, 0:C], self.slot[e, v, 1, :], self.chunk[e, v, :],
                         start=False, stop=False).then_inc(self.moved, 1)

    def end_stage(self):
        nc, k, o, ps, G = self.nc, self.k, self.o, self.ps, self.G
        with Stage(nc, f"permute_end{o.key}") as c:
            codes = c.sb("codes", [P, C])
            codei = c.sb("codei", [P, 2, C], I32)
            filled = c.sb("filled", [P, C])
            other = c.sb("other", [P, C])
            otheri = c.sb("otheri", [P, C], I32)
            over = c.sb("over", [P, C])
            closed, step = c.sems("closed", "step")
            block = c.block()

            @block.tensor
            def _(pe):
                for b, w in ((0, C), (1, C), (2, G)):
                    last = nc.tensor.matmul(ps[:, b, 0:w], self.zero[0:1, 0:P], self.zero[0:1, 0:w],
                                            start=False, stop=True)
                last.then_inc(closed, 1)

            @block.vector
            def _(dve):
                dve.wait_ge(closed, 1)
                done = 0

                def then(inst):
                    nonlocal done
                    done += 1
                    inst.then_inc(step, 1)
                    dve.wait_ge(step, done)

                nc.vector.tensor_copy(k.count[:, :, o.first:o.first + R],
                                      ps[:, 2, 0:G].rearrange("p (t r) -> p t r", r=R))
                then(nc.vector.tensor_scalar(codes[:, :], ps[:, 0, 0:C], 2048.0, None, ALU.mult))
                then(nc.vector.tensor_tensor(codes[:, :], codes[:, :], ps[:, 1, 0:C], ALU.add))
                nc.vector.tensor_scalar(filled[:, :], codes[:, :], 0.0, None, ALU.is_gt)
                then(nc.vector.tensor_scalar(codei[:, 0, :], codes[:, :], -1.0, 0.0, ALU.add, ALU.max))
                then(nc.vector.tensor_single_scalar(codei[:, 1, :], codei[:, 0, :], P - 1, ALU.bitwise_and))
                then(nc.vector.tensor_single_scalar(o.row[:, :], codei[:, 0, :], 7, ALU.arith_shift_right))
                then(nc.vector.tensor_scalar(codes[:, :], codei[:, 1, :], 1.0, None, ALU.add))
                then(nc.vector.tensor_tensor(codes[:, :], codes[:, :], filled[:, :], ALU.mult))
                if o.key:
                    nc.vector.tensor_scalar(o.minus_local[:, :], codes[:, :], -1.0, 1.0, ALU.mult, ALU.add)
                then(nc.vector.tensor_scalar(o.local[:, :], codes[:, :], -1.0, None, ALU.add))
                then(nc.vector.tensor_scalar(otheri[:, :], o.row[:, :], 1.0 / R, None, ALU.mult))
                then(nc.vector.tensor_copy(other[:, :], otheri[:, :]))
                then(nc.vector.tensor_copy(codes[:, :], o.row[:, :]))
                then(nc.vector.scalar_tensor_tensor(codes[:, :], other[:, :], -float(R), codes[:, :],
                                                    ALU.mult, ALU.add))
                then(nc.vector.tensor_scalar(over[:, :], codes[:, :], 0.0, None, ALU.is_lt))
                then(nc.vector.tensor_tensor(other[:, :], other[:, :], over[:, :], ALU.subtract))
                then(nc.vector.scalar_tensor_tensor(codes[:, :], over[:, :], float(R), codes[:, :],
                                                    ALU.mult, ALU.add))
                then(nc.vector.tensor_scalar(over[:, :], codes[:, :], float(R), None, ALU.is_ge))
                if o.key:
                    then(nc.vector.tensor_tensor(o.other[:, :], other[:, :], over[:, :], ALU.add))
                then(nc.vector.scalar_tensor_tensor(o.type[:, :], over[:, :], -float(R), codes[:, :],
                                                    ALU.mult, ALU.add))



def chunk_tiles(nc, o, engine, first, n):
    return nc.values_load_multi_w_load_instructions(
        o.tile_of_chunk[0:1, bass.ds(first, n)], engines=(engine,), min_val=0, max_val=NT - 1,
        skip_runtime_bounds_check_because="the sort writes tiles below NT")[1]


def degree_stage(nc, k):
    with Stage(nc, "degree") as c:
        deg = c.sb("degree", [P, NT])
        has = c.sb("has_edges", [P, NT])
        roots = c.sb("roots", [P, 2, NT])
        step, rooted, rooting = c.sems("step", "rooted", "rooting")
        block = c.block()

        @block.vector
        def _(dve):
            nc.vector.tensor_reduce(deg[:, :], k.count[:, :, R:S2], AX.X, ALU.add).then_inc(step, 1)
            dve.wait_ge(step, 1)
            nc.vector.tensor_scalar(has[:, :], deg[:, :], 0.0, None, ALU.is_gt)
            nc.vector.tensor_scalar_max(roots[:, 0, :], deg[:, :], 1.0)
            nc.vector.tensor_scalar(roots[:, 1, :], deg[:, :], 1.0, None, ALU.add).then_inc(rooting, 1)
            dve.wait_ge(rooted, 1)
            nc.vector.reciprocal(k.dinv_loop[:, :], roots[:, 1, :])
            nc.vector.reciprocal(roots[:, 0, :], roots[:, 0, :]).then_inc(step, 1)
            dve.wait_ge(step, 2)
            nc.vector.tensor_tensor(k.dinv[:, :], roots[:, 0, :], has[:, :], ALU.mult)

        @block.scalar
        def _(act):
            act.wait_ge(rooting, 1)
            nc.scalar.activation(roots[:, :, :], roots[:, :, :], ACT.Sqrt).then_inc(rooted, 1)


def factor_stage(nc, k):
    with Stage(nc, "factor") as c:
        half = c.sb("two_over_count", [P, NT, S2])
        rest = c.sb("rest", [P, NT, S2])
        (step,) = c.sems("step")
        block = c.block()

        @block.vector
        def _(dve):
            done = 0

            def then(inst):
                nonlocal done
                done += 1
                inst.then_inc(step, 1)
                dve.wait_ge(step, done)

            then(nc.vector.tensor_scalar_max(half[:, :, :], k.count[:, :, :], 1.0))
            then(nc.vector.reciprocal(half[:, :, :], half[:, :, :]))
            then(nc.vector.tensor_scalar(half[:, :, :], half[:, :, :], 2.0, None, ALU.mult))
            order = [r + R * inv for r in range(R) for inv in (0, 1)]
            then(nc.vector.tensor_copy(k.factor[:, :, order[-1]], half[:, :, order[-1]]))
            for s, after in zip(order[-2::-1], order[:0:-1]):
                then(nc.vector.tensor_tensor(k.factor[:, :, s], half[:, :, s], k.factor[:, :, after], ALU.mult))
            then(nc.vector.tensor_copy(rest[:, :, :], k.factor[:, :, :]))
            for part in range(PARTS):
                for first in (0, R):
                    last = nc.vector.tensor_copy(k.parts[:, :, first // R, part, :], rest[:, :, first:first + R])
                then(last)
                for first in (0, R):
                    last = nc.vector.tensor_tensor(rest[:, :, first:first + R], rest[:, :, first:first + R],
                                                   k.parts[:, :, first // R, part, :], ALU.subtract)
                then(last)


def late(u):
    return range(max(u - LAG, 0), u + 1) if u == U - 1 else range(u - LAG, u - LAG + 1) if u >= LAG else ()


class EdgeFactors(Job):

    STEPS = U // 2
    V = 4
    CLOSE = U - 2

    def __init__(self, nc, c, k, o):
        super().__init__(C // U)
        self.nc, self.k, self.o = nc, k, o
        self.pick = c.sb(f"pick{o.key}", [P, self.V, 2, P], BF16)
        self.turned = c.sb(f"turned{o.key}", [P, self.V, 2, P], BF16)
        self.type_hot = c.sb(f"type_one_hot{o.key}", [P, C, R])
        self.got = c.sb(f"got{o.key}", [P, U, PARTS * R])
        self.ps_turn = c.psum(f"ps_turn{o.key}", [P, 2, 1024], BF16)
        self.ps_got = c.psum(f"ps_got{o.key}", [P, 512])
        self.picked, self.flipped, self.copied, self.found, self.taken, self.step = c.sems(
            *(f"{n}{o.key}" for n in ("picked", "flipped", "copied", "found", "taken", "step")))

    def at(self, u):
        return [s for s in range(self.STEPS) if (3 * s + 1) // 2 == u]

    def tensor_at(self, u):
        return self.at(u - LAG) if u >= LAG else ()

    def start_stage(self):
        nc, k, o, V = self.nc, self.k, self.o, self.V
        with Stage(nc, f"factor_start{o.key}") as c:
            block = c.block()

            @block.vector
            def _(dve):
                nc.vector.tensor_tensor(self.type_hot[:, :, :], o.type[:, :, None].to_broadcast([P, C, R]),
                                        k.iota[:, None, 0:R].to_broadcast([P, C, R]),
                                        ALU.is_equal).then_inc(self.step, 1)
                nc.vector.sem_inc(self.taken, 1)

            @block.tensor
            def _(pe):
                nc.tensor.sem_inc(self.flipped, V)
                nc.tensor.sem_inc(self.found, V)

            @block.scalar
            def _(act):
                nc.scalar.sem_inc(self.copied, 2)

    def vector(self, dve, i, s):
        nc, k, o, V = self.nc, self.k, self.o, self.V
        n = i * self.STEPS + s
        dve.wait_ge(self.flipped, n + 1)
        for h in (0, 1):
            last = nc.vector.tensor_scalar(self.pick[:, s % V, h, :], k.iota[:, 0:P],
                                           o.local[:, bass.ds(n * 2 + h, 1)], None, ALU.is_equal)
        last.then_inc(self.picked, 1)

    def vector_close(self, dve, i):
        nc, o, V = self.nc, self.o, self.V
        dve.wait_ge(self.found, i * self.STEPS + self.STEPS + V)
        dve.wait_ge(self.step, i + 1)
        for part in range(PARTS):
            some = slice(part * R, part * R + R)
            found = self.ps_got[:, 0:U * PARTS * R].rearrange("p (v r) -> p v r", r=PARTS * R)
            last = nc.vector.tensor_tensor(self.got[:, :, some], found[:, :, some],
                                           self.type_hot[:, bass.ds(i * U, U), :], ALU.mult)
        last.then_inc(self.taken, 1)
        dve.wait_ge(self.taken, i + 2)
        nc.vector.tensor_reduce(o.coef[:, bass.ds(i * U, U)], self.got[:, :, :], AX.X,
                                ALU.add).then_inc(self.step, 1)

    def tensor(self, pe, i, s):
        nc, k, o, V = self.nc, self.k, self.o, self.V
        if s % V == 0:
            self.tiles = (self.tiles if s else []) + list(chunk_tiles(nc, o, PE, i * U + s * 2, V * 2))
        n = i * self.STEPS + s
        pe.wait_ge(self.picked, n + 1)
        pe.wait_ge(self.copied, n + 1)
        for h in (0, 1):
            last = nc.tensor.transpose(self.ps_turn[:, s % 2, h * P:h * P + P], self.pick[:, s % V, h, :],
                                       k.ident16[:, :])
        last.then_inc(self.flipped, 1)
        for w in (s - 1, s) if s == self.STEPS - 1 else (s - 1,) if s else ():
            if w == 0:
                pe.wait_ge(self.taken, i + 1)
            pe.wait_ge(self.copied, i * self.STEPS + w + 1 + 2)
            for h in (0, 1):
                g = PARTS * R * (2 * w + h)
                last = nc.tensor.matmul(self.ps_got[:, g:g + PARTS * R], self.turned[:, w % V, h, :],
                                        k.parts[:, bass.ds(self.tiles[2 * w + h], 1), o.key, :, :].rearrange(
                                            "p a q r -> p (a q r)"),
                                        start=True, stop=True)
            last.then_inc(self.found, 1)

    def scalar(self, act, i, s):
        nc, V = self.nc, self.V
        n = i * self.STEPS + s
        act.wait_ge(self.flipped, n + 1 + V)
        act.wait_ge(self.found, n + 1)
        nc.scalar.copy(self.turned[:, s % V, :, :].rearrange("p h f -> p (h f)"),
                       self.ps_turn[:, s % 2, 0:2 * P]).then_inc(self.copied, 1)



def edge_sum_stage(nc, k, tag, o, rows, table, width, acc, factors=None, jobs=(),
                   zero=False, scaled_by=None, loads=(), scalar_makes=0):
    def by_scalar(u):
        return scalar_makes and u % scalar_makes == scalar_makes - 1

    BANKS = 1 if width <= 512 else 2
    PIECES = BANKS
    W = width // PIECES
    HALF = NT // 2
    RING = 4
    PLACES = U if BANKS == 1 else U // 2
    Q = U // 4
    with Stage(nc, tag) as c:
        got = c.sb("gathered", [P, PLACES, width])
        select = c.sb("select", [P, U, P])
        index = c.sb("index", [P, U], I32)
        ps = c.psum("ps", [P, RING * BANKS, 512])
        arrived, before = k.arrived, list(k.arrivals)
        for p in range(PLACES):
            k.arrivals[p] += C // PLACES
        far = c.sb("distance", [P, U // scalar_makes, P], FP16) if scalar_makes else None
        indexed, selected, multiplied, added, loaded, measured, selected_too, begun, zeroed_too = c.sems(
            "indexed", "selected", "multiplied", "added", "loaded", "measured", "selected_too", "begun",
            "zeroed_too")
        block = c.block()
        made = [u for u in range(U) if by_scalar(u)]
        own = [u for u in range(U) if not by_scalar(u)]

        if loads:
            @block.sync
            def _(sp):
                with nc.allow_non_contiguous_dma(reason="weights and biases, small"):
                    for to, source in loads:
                        sp.dma_start(to, source).then_inc(loaded, 16)
                sp.wait_ge(loaded, 16 * len(loads))

        @block.gpsimd
        def _(gp):
            with gp.Fori(0, C // U) as i:
                for u in range(U):
                    if u % Q == 0:
                        gp.wait_ge(indexed, i * 4 + u // Q + 1)
                        gp.wait_ge(multiplied, i * U + u + Q + U - PLACES)
                        nc.gpsimd.nop(nofuse=True)
                    nc.gpsimd.indirect_dma_start(
                        got[:, u % PLACES, :], None, table,
                        bass.IndirectOffsetOnAxis(ap=index[:, u:u + 1], axis=0)).then_inc(arrived[u % PLACES], 16)

        @block.tensor
        def _(pe):
            nc.tensor.sem_inc(multiplied, U)
            def turn(i, last_turn):
                for u in range(U):
                    pe.wait_ge(arrived[u % PLACES],
                               (i * (U // PLACES) + u // PLACES + 1 + before[u % PLACES]) * 16)
                    if by_scalar(u):
                        pe.wait_ge(selected_too, i * len(made) + made.index(u) + 1)
                    else:
                        pe.wait_ge(selected, i * len(own) + own.index(u) + 1)
                    pe.wait_ge(added, i * U + u + 1)
                    for b in range(PIECES):
                        last = nc.tensor.matmul(ps[:, (u % RING) * BANKS + b, 0:W], select[:, u, :],
                                                got[:, u % PLACES, b * W:b * W + W], start=True, stop=True)
                    last.then_inc(multiplied, 1)
                    for job in jobs:
                        if not last_turn or job.turns == TURNS_OF_CHUNKS:
                            for w in job.tensor_at(u):
                                job.tensor(pe, i, w)

            with pe.Fori(0, TURNS_OF_CHUNKS - 1) as i:
                turn(i, False)
            turn(TURNS_OF_CHUNKS - 1, True)

        @block.scalar
        def _(act):
            def put(i, q):
                nc.scalar.copy(index[:, q * Q:q * Q + Q], rows[:, bass.ds(i * U + q * Q, Q)]).then_inc(indexed, 1)

            def make(i, u):
                act.wait_ge(multiplied, i * U + u + 1)
                nc.scalar.nop(nofuse=True)
                nc.scalar.activation(far[:, made.index(u), :], k.iota[:, 0:P], ACT.Abs,
                                     bias=o.minus_local[:, bass.ds(i * U + u, 1)]).then_inc(measured, 1)
                act.wait_ge(measured, i * len(made) + made.index(u) + 1)
                nc.scalar.nop(nofuse=True)
                nc.scalar.activation(select[:, u, :], far[:, made.index(u), :], ACT.Relu, bias=k.one[:, :],
                                     scale=-1.0).then_inc(selected_too, 1)

            def turn(i, last_turn):
                for u in range(U):
                    if by_scalar((u + LEAD) % U) and (u < LEAD or not last_turn):
                        make(i + (u + LEAD) // U, (u + LEAD) % U)
                    if u % Q == 2 and not last_turn:
                        act.wait_ge(multiplied, i * U + u - 2 + Q + U)
                        nc.scalar.nop(nofuse=True)
                        put(i + 1, u // Q)
                    for job in jobs:
                        if not last_turn or job.turns == TURNS_OF_CHUNKS:
                            for w in job.at(u):
                                job.scalar(act, i, w)

            for q in range(4):
                put(0, q)
            if zero:
                rest = acc[:, HALF:NT, :].rearrange("p t f -> p (t f)")
                nc.scalar.activation(rest, k.one[:, :].to_broadcast([P, (NT - HALF) * width]), ACT.Copy,
                                     scale=0.0).then_inc(zeroed_too, 1)
            for u in made:
                if u < LEAD:
                    make(0, u)
            with act.Fori(0, TURNS_OF_CHUNKS - 1) as i:
                turn(i, False)
            turn(TURNS_OF_CHUNKS - 1, True)

        @block.vector
        def _(dve):
            nc.vector.sem_inc(added, RING)

            def make(n, u):
                dve.wait_ge(multiplied, n + 1)
                if factors is None:
                    nc.vector.tensor_scalar(select[:, u, :], k.iota[:, 0:P], o.local[:, bass.ds(n, 1)],
                                            None, ALU.is_equal).then_inc(selected, 1)
                else:
                    nc.vector.tensor_scalar(select[:, u, :], k.iota[:, 0:P], o.local[:, bass.ds(n, 1)],
                                            factors[:, bass.ds(n, 1)], ALU.is_equal, ALU.mult).then_inc(selected, 1)

            def turn(i, last_turn):
                tiles = chunk_tiles(nc, o, DVE, i * U, U)
                for u in range(U):
                    if not by_scalar((u + LEAD) % U) and (u < LEAD or not last_turn):
                        make(i * U + u + LEAD, (u + LEAD) % U)
                    for job in jobs:
                        if not last_turn or job.turns == TURNS_OF_CHUNKS:
                            for w in job.at(u):
                                job.vector(dve, i, w)
                    for w in late(u):
                        dve.wait_ge(multiplied, i * U + w + 1 + U)
                        dve.wait_ge(added, i * U + w + RING)
                        row = acc[:, bass.ds(tiles[w], 1), 0:width]
                        part = ps[:, (w % RING) * BANKS:(w % RING + 1) * BANKS, 0:W]
                        nc.vector.tensor_tensor(row.rearrange("p a (b w) -> p (a b) w", w=W),
                                                row.rearrange("p a (b w) -> p (a b) w", w=W), part,
                                                ALU.add).then_inc(added, 1)
                    for job in jobs:
                        if u == job.CLOSE and (not last_turn or job.turns == TURNS_OF_CHUNKS):
                            job.vector_close(dve, i)

            for u in own:
                if u < LEAD:
                    make(u, u)
            if zero:
                nc.vector.memset(acc[:, 0:HALF, :], 0.0).then_inc(begun, 1)
                dve.wait_ge(begun, 1)
                dve.wait_ge(zeroed_too, 1)
            if scaled_by is not None:
                nc.vector.tensor_tensor(acc[:, :, :], acc[:, :, :], scaled_by.to_broadcast([P, NT, width]),
                                        ALU.mult).then_inc(begun, 1)
                dve.wait_ge(begun, 1)
            with dve.Fori(0, TURNS_OF_CHUNKS - 1) as i:
                turn(i, False)
            turn(TURNS_OF_CHUNKS - 1, True)



def piece(first, width, terms, bias=None, target=None):
    return first, width, terms, bias, target


def table_stage(nc, k, tag, pieces, tables, width, scale=None):
    M = len(pieces)
    feeds = []
    for p in pieces:
        for turned, _ in p[2]:
            if not any(turned is f for f in feeds):
                feeds.append(turned)
    with Stage(nc, tag) as c:
        fed = c.sb("fed", [P, J, len(feeds), P])
        (copied,) = c.sems("copied")
        rows = c.sb("rows", [P, J, width])
        ps = c.psum("ps", [P, J, 512])
        stored = c.sems(*(f"stored{j}" for j in range(J)))
        multiplied, drained = c.sems("multiplied", "drained")
        block = c.block()

        @block.tensor
        def _(pe):
            nc.tensor.sem_inc(multiplied, M * J)
            with pe.Fori(0, TURNS) as i:
                for m in range(M * J):
                    j, (first, w, terms, bias, target) = m // M, pieces[m % M]
                    if m % M == 0:
                        pe.wait_ge(copied, (i * J + j + 1) * len(feeds))
                    pe.wait_ge(drained, i * (M * J) + m + 1)
                    for n, (turned, weights) in enumerate(terms):
                        (q,) = (q for q, f in enumerate(feeds) if f is turned)
                        last = nc.tensor.matmul(ps[:, m % J, 0:w], fed[:, j, q, :], weights,
                                                start=(n == 0), stop=(n == len(terms) - 1))
                    last.then_inc(multiplied, 1)

        def feed(engine, copy):
            with engine.Fori(0, TURNS) as i:
                for j in range(J):
                    engine.wait_ge(multiplied, i * (M * J) + M * j + M)
                    for q, turned in enumerate(feeds):
                        copy(fed[:, j, q, :], turned[:, bass.ds((i * J + j) * P, P)]).then_inc(copied, 1)

        def drain_turn(engine, i, first_turn):
            for m in range(M * J):
                j, (first, w, terms, bias, target) = m // M, pieces[m % M]
                if m % M == 0 and not first_turn:
                    engine.wait_ge(stored[j], i * 16 * len(tables))
                engine.wait_ge(multiplied, i * (M * J) + m + 1 + M * J)
                if scale is not None:
                    nc.scalar.nop(nofuse=True)
                to = rows[:, j, first:first + w] if target is None else \
                    target[:, bass.ds(i * J + j, 1), 0:w].rearrange("p a f -> p (a f)")
                if scale is not None:
                    last = nc.scalar.activation(to, ps[:, m % J, 0:w], ACT.Copy, scale=scale[:, bass.ds(i * J + j, 1)])
                elif bias is None:
                    last = nc.vector.tensor_copy(to, ps[:, m % J, 0:w])
                else:
                    last = nc.vector.tensor_tensor(to, ps[:, m % J, 0:w], bias, ALU.add)
                last.then_inc(drained, 1)

        def drain(engine):
            engine.sem_inc(drained, J)
            drain_turn(engine, 0, True)
            with engine.Fori(1, TURNS) as i:
                drain_turn(engine, i, False)

        if scale is not None:
            @block.scalar
            def _(act):
                drain(act)

            @block.vector
            def _(dve):
                feed(dve, nc.vector.tensor_copy)
        else:
            @block.vector
            def _(dve):
                drain(dve)

            @block.scalar
            def _(act):
                feed(act, nc.scalar.copy)

        @block.sync
        def _(sp):
            with sp.Fori(0, TURNS) as i:
                for j in range(J):
                    sp.wait_ge(drained, i * (M * J) + M * j + M + J)
                    for table, first, w in tables:
                        sp.dma_start(table[bass.ds((i * J + j) * P, P), :],
                                     rows[:, j, first:first + w]).then_inc(stored[j], 16)
            for j in range(J):
                sp.wait_ge(stored[j], 16 * TURNS * len(tables))


def combine_stage(nc, k, tag, acc, width, terms, bias, mean):
    PIECES = -(-width // 512)
    W = width // PIECES
    M = PIECES
    with Stage(nc, tag) as c:
        ps = c.psum("ps", [P, J, 512])
        fed = c.sb("fed", [P, J, len(terms), P])
        multiplied, drained, biased, relued, copied = c.sems("multiplied", "drained", "biased", "relued", "copied")
        block = c.block()

        @block.gpsimd
        def _(gp):
            with gp.Fori(0, TURNS) as i:
                for j in range(J):
                    gp.wait_ge(multiplied, i * (M * J) + M * j + M)
                    for q, (turned, _) in enumerate(terms):
                        nc.gpsimd.tensor_copy(fed[:, j, q, :], turned[:, bass.ds((i * J + j) * P, P)]).then_inc(copied, 1)

        @block.tensor
        def _(pe):
            nc.tensor.sem_inc(multiplied, M * J)
            with pe.Fori(0, TURNS) as i:
                for m in range(M * J):
                    j, b = divmod(m, M)
                    if b == 0:
                        pe.wait_ge(copied, (i * J + j + 1) * len(terms))
                    pe.wait_ge(drained, i * (M * J) + m + 1)
                    for n, (_, weights) in enumerate(terms):
                        last = nc.tensor.matmul(ps[:, m % J, 0:W], fed[:, j, n, :], weights[:, b * W:b * W + W],
                                                start=(n == 0), stop=(n == len(terms) - 1))
                    last.then_inc(multiplied, 1)

        @block.vector
        def _(dve):
            nc.vector.sem_inc(drained, J)
            with dve.Fori(0, TURNS) as i:
                for m in range(M * J):
                    j, b = divmod(m, M)
                    part = acc[:, bass.ds(i * J + j, 1), b * W:b * W + W].rearrange("p a f -> p (a f)")
                    dve.wait_ge(multiplied, i * (M * J) + m + 1 + M * J)
                    nc.vector.scalar_tensor_tensor(part, part, k.dinv[:, bass.ds(i * J + j, 1)], ps[:, m % J, 0:W],
                                                   ALU.mult, ALU.add).then_inc(drained, 1)
                    dve.wait_ge(drained, i * (M * J) + m + 1 + J)
                    nc.vector.tensor_tensor(part, part, bias[:, b * W:b * W + W], ALU.add).then_inc(biased, 1)
            if mean:
                F = width // K
                dve.wait_ge(relued, TURNS)
                for n in range(1, K):
                    if n > 1:
                        dve.wait_ge(biased, TURNS * M * J + 1)
                    nc.vector.tensor_tensor(acc[:, :, 0:F], acc[:, :, 0:F], acc[:, :, n * F:n * F + F],
                                            ALU.add).then_inc(biased, 1)

        @block.scalar
        def _(act):
            with act.Fori(0, TURNS) as i:
                for j in range(J):
                    act.wait_ge(biased, i * (M * J) + M * j + M)
                    nc.scalar.nop(nofuse=True)
                    part = acc[:, bass.ds(i * J + j, 1), 0:width]
                    last = nc.scalar.activation(part, part, ACT.Relu, scale=1.0 / K if mean else 1.0)
                last.then_inc(relued, 1)


def turn_stage(nc, k, tag, source, target, blocks=1, scale=None, relu=False):
    M = blocks
    with Stage(nc, tag) as c:
        fed = c.sb("fed", [P, J, M * P])
        ps = c.psum("ps", [P, J, 512])
        turned, copied, made = c.sems("turned", "copied", "made")
        block = c.block()

        @block.vector
        def _(dve):
            with dve.Fori(0, TURNS) as i:
                for j in range(J):
                    dve.wait_ge(turned, i * (M * J) + M * j + M)
                    part = source[:, bass.ds(i * J + j, 1), 0:M * P].rearrange("p a f -> p (a f)")
                    if scale is None:
                        last = nc.vector.tensor_copy(fed[:, j, :], part)
                    else:
                        last = nc.vector.tensor_scalar(fed[:, j, :], part, scale[:, bass.ds(i * J + j, 1)], None, ALU.mult)
                    last.then_inc(made, 1)

        @block.tensor
        def _(pe):
            nc.tensor.sem_inc(turned, M * J)
            with pe.Fori(0, TURNS) as i:
                for m in range(M * J):
                    j, b = divmod(m, M)
                    if b == 0:
                        pe.wait_ge(made, i * J + j + 1)
                    pe.wait_ge(copied, i * (M * J) + m + 1)
                    nc.tensor.transpose(ps[:, m % J, 0:P], fed[:, j, b * P:b * P + P], k.ident[:, :]).then_inc(turned, 1)

        @block.scalar
        def _(act):
            nc.scalar.sem_inc(copied, J)
            with act.Fori(0, TURNS) as i:
                for m in range(M * J):
                    j, b = divmod(m, M)
                    act.wait_ge(turned, i * (M * J) + m + 1 + M * J)
                    nc.scalar.nop(nofuse=True)
                    nc.scalar.activation(target[:, b, bass.ds((i * J + j) * P, P)], ps[:, m % J, 0:P],
                                         ACT.Relu if relu else ACT.Copy).then_inc(copied, 1)


def turn_back_stage(nc, k, tag, source):
    with Stage(nc, tag) as c:
        fed = c.sb("fed", [P, J, P])
        ps = c.psum("ps", [P, J, 512])
        turned, added, copied = c.sems("turned", "added", "copied")
        block = c.block()

        @block.scalar
        def _(act):
            with act.Fori(0, TURNS) as i:
                for j in range(J):
                    act.wait_ge(turned, i * J + j + 1)
                    nc.scalar.copy(fed[:, j, :], source[:, bass.ds((i * J + j) * P, P)]).then_inc(copied, 1)

        @block.tensor
        def _(pe):
            nc.tensor.sem_inc(turned, J)
            with pe.Fori(0, TURNS) as i:
                for j in range(J):
                    pe.wait_ge(copied, i * J + j + 1)
                    pe.wait_ge(added, i * J + j + 1)
                    nc.tensor.transpose(ps[:, j, 0:P], fed[:, j, :], k.ident[:, :]).then_inc(turned, 1)

        @block.vector
        def _(dve):
            nc.vector.sem_inc(added, J)
            with dve.Fori(0, TURNS) as i:
                for j in range(J):
                    part = k.xcur[:, bass.ds(i * J + j, 1), :].rearrange("p a f -> p (a f)")
                    dve.wait_ge(turned, i * J + j + 1 + J)
                    nc.vector.tensor_tensor(part, part, ps[:, j, 0:P], ALU.add).then_inc(added, 1)


def layer_norm_stage(nc, k, tag, addend=None, scale=None, bias=None):
    with Stage(nc, tag) as c:
        stats = c.sb("stats", [P, NT, 6])
        mean = c.sb("mean", [P, NT, 2])
        root = c.sb("root", [P, NT])
        step, rooting, rooted = c.sems("step", "rooting", "rooted")
        block = c.block()

        @block.vector
        def _(dve):
            done = 0

            def then(inst):
                nonlocal done
                done += 1
                inst.then_inc(step, 1)
                dve.wait_ge(step, done)

            if addend is not None:
                if scale is not None:
                    then(nc.vector.tensor_tensor(addend, addend, scale[:, :, None].to_broadcast([P, NT, D]), ALU.mult))
                then(nc.vector.tensor_tensor(k.xcur[:, :, :], k.xcur[:, :, :], addend, ALU.add))
            if bias is not None:
                then(nc.vector.tensor_tensor(k.xcur[:, :, :], k.xcur[:, :, :],
                                             bias[:, None, :].to_broadcast([P, NT, D]), ALU.add))
            for t in range(NT):
                last = nc.vector.bn_stats(stats[:, t, :], k.xcur[:, t, :])
            then(last)
            for t in range(NT):
                last = nc.vector.bn_aggr(mean[:, t, :], stats[:, t, :])
            then(last)
            nc.vector.tensor_scalar(root[:, :], mean[:, :, 1], EPS, None, ALU.add).then_inc(rooting, 1)
            dve.wait_ge(rooted, 1)
            then(nc.vector.reciprocal(root[:, :], root[:, :]))
            then(nc.vector.tensor_tensor(k.xcur[:, :, :], k.xcur[:, :, :],
                                         mean[:, :, 0:1].to_broadcast([P, NT, D]), ALU.subtract))
            then(nc.vector.tensor_tensor(k.xcur[:, :, :], k.xcur[:, :, :],
                                         root[:, :, None].to_broadcast([P, NT, D]), ALU.mult))

        @block.scalar
        def _(act):
            act.wait_ge(rooting, 1)
            nc.scalar.activation(root[:, :], root[:, :], ACT.Sqrt).then_inc(rooted, 1)


def batch_norm_stage(nc, k, tag, h, blocks, gamma, beta):
    with Stage(nc, tag) as c:
        mean = c.sb("mean", [P, blocks])
        var = c.sb("var", [P, blocks])
        root = c.sb("root", [P, blocks])
        spare = c.sb("squares", [P, NP])
        params = c.sb("params", [P, 2, blocks])
        loaded, step, centred, rooted, scaled, done_act = c.sems(
            "loaded", "step", "centred", "rooted", "scaled", "done_act")
        block = c.block()

        @block.sync
        def _(sp):
            with nc.allow_non_contiguous_dma(reason="one value per partition"):
                for n, a in enumerate((gamma, beta)):
                    sp.dma_start(params[:, n, :], a.rearrange("(b p) -> p b", p=P)).then_inc(loaded, 16)

        @block.vector
        def _(dve):
            done = 0

            def then(inst):
                nonlocal done
                done += 1
                inst.then_inc(step, 1)
                dve.wait_ge(step, done)

            then(nc.vector.tensor_reduce(mean[:, :], h[:, :, 0:N], AX.X, ALU.add))
            nc.vector.tensor_scalar(mean[:, :], mean[:, :], -1.0 / N, None, ALU.mult).then_inc(centred, 1)
            dve.wait_ge(centred, 1)
            dve.wait_ge(rooted, 1)
            then(nc.vector.reciprocal(root[:, :], root[:, :]))
            dve.wait_ge(loaded, 32)
            then(nc.vector.tensor_tensor(root[:, :], root[:, :], params[:, 0, :], ALU.mult))
            then(nc.vector.tensor_tensor(mean[:, :], mean[:, :], root[:, :], ALU.mult))
            nc.vector.tensor_tensor(mean[:, :], mean[:, :], params[:, 1, :], ALU.add).then_inc(scaled, 1)

        @block.scalar
        def _(act):
            act.wait_ge(centred, 1)
            for b in range(blocks):
                if b:
                    act.wait_ge(done_act, b)
                nc.scalar.activation(spare[:, 0:N], h[:, b, 0:N], ACT.Square, bias=mean[:, b:b + 1],
                                     accum_out=var[:, b:b + 1]).then_inc(done_act, 1)
            act.wait_ge(done_act, blocks)
            nc.scalar.activation(var[:, :], var[:, :], ACT.Copy, scale=1.0 / N, bias=EPS).then_inc(done_act, 1)
            act.wait_ge(done_act, blocks + 1)
            nc.scalar.activation(root[:, :], var[:, :], ACT.Sqrt).then_inc(rooted, 1)
            act.wait_ge(scaled, 1)
            for b in range(blocks):
                nc.scalar.activation(h[:, b, :], h[:, b, :], ACT.Relu, bias=mean[:, b:b + 1], scale=root[:, b:b + 1])


def feature_stage(nc, k, tag, out, terms, bias):
    W = 400
    PARTS = NP // W
    B = out.shape[1]
    with Stage(nc, tag) as c:
        ps = c.psum("ps", [P, 8, 512])
        multiplied, drained = c.sems("multiplied", "drained")
        block = c.block()

        @block.tensor
        def _(pe):
            for b in range(B):
                for n in range(PARTS):
                    if b:
                        pe.wait_ge(drained, (b - 1) * PARTS + n + 1)
                    for t, (weights, turned) in enumerate(terms):
                        last = nc.tensor.matmul(ps[:, n, 0:W], weights[:, b * P:b * P + P], turned[:, n * W:n * W + W],
                                                start=(t == 0), stop=(t == len(terms) - 1))
                    last.then_inc(multiplied, 1)

        @block.scalar
        def _(act):
            for b in range(B):
                for n in range(PARTS):
                    act.wait_ge(multiplied, b * PARTS + n + 1)
                    nc.scalar.activation(out[:, b, n * W:n * W + W], ps[:, n, 0:W], ACT.Relu,
                                         bias=bias[:, b:b + 1]).then_inc(drained, 1)


def load_weights_stage(nc, k, tag, loads):
    with Stage(nc, tag) as c:
        (loaded,) = c.sems("loaded")
        block = c.block()

        @block.sync
        def _(sp):
            with nc.allow_non_contiguous_dma(reason="weights and biases, small"):
                for to, source in loads:
                    sp.dma_start(to, source).then_inc(loaded, 16)
            if loads:
                sp.wait_ge(loaded, 16 * len(loads))


def setup(nc, c):
    k = Chip()

    def sb(name, shape, dt=F32):
        return c.enter_context(nc.sbuf_tensor(name, shape, dt))

    k.xcur = sb("xcur", [P, NT, D])
    k.xT = sb("xT", [P, NP])
    k.iota = sb("iota", [P, C])
    k.iota16 = sb("iota16", [P, C], FP16)
    k.diff = sb("diff", [P, P])
    k.ident = sb("ident", [P, P])
    k.ident16 = sb("ident16", [P, P], BF16)
    k.one = sb("one", [P, 1])
    k.count = sb("count", [P, NT, S2])
    k.factor = sb("factor", [P, NT, S2])
    k.parts = sb("factor_parts", [P, NT, 2, PARTS, R], BF16)
    k.dinv = sb("dinv", [P, NT])
    k.dinv_loop = sb("dinv_loop", [P, NT])
    k.arrived = [nc.alloc_semaphore(f"gathered{u}") for u in range(U)]
    k.arrivals = [0] * U
    k.orders = []
    for key in (0, 1):
        o = Chip()
        o.key = key
        o.first = R * key
        o.row = sb(f"row{key}", [P, C], I32)
        o.local = sb(f"local{key}", [P, C])
        if key:
            o.other = sb(f"other{key}", [P, C], I32)
            o.minus_local = sb(f"minus_local{key}", [P, C])
        o.type = sb(f"type{key}", [P, C])
        o.coef = sb(f"coef{key}", [P, C])
        o.tile_of_chunk = sb(f"tile_of_chunk{key}", [P, C], I32)
        k.orders.append(o)
    return k


def sort_inputs(c, o):
    (o.local_in, o.high_in, o.low_in, o.group_in, o.slot_in, o.chunk_in) = (
        c.sb(name, [P, EC]) for name in ("local_in", "high_in", "low_in", "group_in", "slot_in", "chunk_in"))


def sort_by_dst(nc, k):
    o = k.orders[1]
    with Stage(nc, "sort1") as c:
        sort_inputs(c, o)
        rank_stage(nc, k, o)
        job = Permute(nc, c, k, o)
        job.start_stage()
        run_job_stage(nc, "permute1", job)
        job.end_stage()
    degree_stage(nc, k)



def arma_layer(nc, k, A, dram):
    by_dst = k.orders[1]

    with Stage(nc, "arma1") as c:
        ax = c.sb("ax", [P, NT, D])
        init_w = c.sb("init_w", [P, K, HID])
        root_w = c.sb("root_w", [P, K, HID])
        w = c.sb("w", [P, K, HID // P, HID])
        bias = c.sb("bias", [P, K * HID // P])
        loads = [
            (init_w[:, :, :], A["L0_gnn_init_w1"].rearrange("k f g -> f k g")),
            (root_w[:, :, :], A["L0_gnn_root_w1"][0].rearrange("k f g -> f k g")),
            (w[:, :, :, :].rearrange("p k b h -> p (k b) h"),
             A["L0_gnn_w1"][0].rearrange("k (b p) h -> p (k b) h", p=P)),
            (bias[:, :], A["L0_gnn_b1"][0].rearrange("k o (b p) -> p (k o b)", p=P))]
        scaled_x_stage(nc, k, dram["x_scaled"])
        with Stage(nc, "sort0") as d:
            sort = Permute(nc, d, k, k.orders[0])
            sort.start_stage()
            edge_sum_stage(nc, k, "sum_x", by_dst, by_dst.other, dram["x_scaled"][:, :], D, ax, jobs=[sort],
                           zero=True, loads=loads, scalar_makes=2)
            sort.end_stage()
        out1T = c.sb("out1T", [P, K * HID // P, NP])
        axT = c.sb("axT", [P, 1, NP])
        factor_stage(nc, k)
        turn_stage(nc, k, "turn_ax", ax, axT, scale=k.dinv)
        feature_stage(nc, k, "arma1_out", out1T,
                      [(init_w[:, :, :].rearrange("p k g -> p (k g)"), axT[:, 0, :]),
                       (root_w[:, :, :].rearrange("p k g -> p (k g)"), k.xT[:, :])], bias)
        table_stage(nc, k, "arma1_table",
                    [piece(s * HID, HID, [(out1T[:, s * 2 + b, :], w[:, s, b, :]) for b in range(HID // P)])
                     for s in range(K)], [(dram["arma1"], 0, K * HID)], K * HID, scale=k.dinv)

    with Stage(nc, "arma2") as c2:
        hT = c2.sb("hT", [P, HID // P, NP])
        with Stage(nc, "arma1_end") as c:
            acc = c.sb("acc", [P, NT, K * HID])
            root_w = c.sb("root_w", [P, K, HID])
            bias = c.sb("bias", [P, K * HID])
            loads = [
                (root_w[:, :, :], A["L0_gnn_root_w1"][1].rearrange("k f g -> f k g")),
                (bias[:, :], A["L0_gnn_b1"][1].rearrange("k o g -> o (k g)").to_broadcast([P, K * HID]))]
            edge_sum_stage(nc, k, "sum_arma1", by_dst, by_dst.other, dram["arma1"][:, :], K * HID, acc,
                           zero=True, loads=loads)
            combine_stage(nc, k, "arma1_combine", acc, K * HID,
                          [(k.xT[:, :], root_w[:, :, :].rearrange("p k g -> p (k g)"))], bias, mean=True)
            turn_stage(nc, k, "turn_h", acc, hT, blocks=HID // P)
        batch_norm_stage(nc, k, "norm_h", hT, HID // P, A["L0_gnn_gamma1"], A["L0_gnn_beta1"])

        G = HID // P
        init_w = c2.sb("init_w", [P, G, K, D])
        root_w = c2.sb("root_w", [P, 2, G, K, D])
        w = c2.sb("w", [P, K, D])
        bias = c2.sb("bias", [P, 2, K * D])
        acc = c2.sb("acc", [P, NT, K * D])
        load_weights_stage(nc, k, "arma2_load", [
            *((init_w[:, b, :, :], A["L0_gnn_init_w2"][:, b * P:b * P + P, :].rearrange("k f g -> f k g"))
              for b in range(G)),
            *((root_w[:, t, b, :, :], A["L0_gnn_root_w2"][t, :, b * P:b * P + P, :].rearrange("k f g -> f k g"))
              for t in (0, 1) for b in range(G)),
            (w[:, :, :], A["L0_gnn_w2"][0].rearrange("k f g -> f k g")),
            *((bias[:, t, :], A["L0_gnn_b2"][t].rearrange("k o g -> o (k g)").to_broadcast([P, K * D]))
              for t in (0, 1))])

        def flat(weights):
            return weights.rearrange("p k g -> p (k g)")

        roots = [[(hT[:, b, :], flat(root_w[:, t, b, :, :])) for b in range(G)] for t in (0, 1)]
        table_stage(nc, k, "arma2_table0",
                    [piece(0, K * D, [(hT[:, b, :], flat(init_w[:, b, :, :])) for b in range(G)])],
                    [(dram["arma2"], 0, K * D)], K * D, scale=k.dinv)
        edge_sum_stage(nc, k, "sum_arma2", by_dst, by_dst.other, dram["arma2"][:, :], K * D, acc, zero=True)
        combine_stage(nc, k, "arma2_combine0", acc, K * D, roots[0], bias[:, 0, :], mean=False)
        with Stage(nc, "arma2_mid") as c:
            outT = c.sb("outT", [P, K, NP])
            turn_stage(nc, k, "turn_out", acc, outT, blocks=K)
            table_stage(nc, k, "arma2_table1",
                        [piece(s * D, D, [(outT[:, s, :], w[:, s, :])]) for s in range(K)],
                        [(dram["arma2"], 0, K * D)], K * D, scale=k.dinv)
        edge_sum_stage(nc, k, "sum_arma3", by_dst, by_dst.other, dram["arma2"][:, :], K * D, acc, zero=True)
        combine_stage(nc, k, "arma2_combine1", acc, K * D, roots[1], bias[:, 1, :], mean=True)
        h2T = c2.sb("h2T", [P, 1, NP])
        turn_stage(nc, k, "turn_h2", acc, h2T)
        batch_norm_stage(nc, k, "norm_h2", h2T, 1, A["L0_gnn_gamma2"], A["L0_gnn_beta2"])
        turn_back_stage(nc, k, "arma_back", h2T[:, 0, :])
    layer_norm_stage(nc, k, "norm0")
    turn_stage(nc, k, "turn0", k.xcur, k.xT[:, None, :])


def scaled_x_stage(nc, k, table):
    with Stage(nc, "scaled_x") as c:
        rows = c.sb("rows", [P, NT, D])
        ps = c.psum("ps", [P, J, 512])
        made, stored, turned, copied = c.sems("made", "stored", "turned", "copied")
        block = c.block()

        @block.vector
        def _(dve):
            nc.vector.tensor_tensor(rows[:, :, :], k.xcur[:, :, :], k.dinv[:, :, None].to_broadcast([P, NT, D]),
                                    ALU.mult).then_inc(made, 1)

        @block.sync
        def _(sp):
            sp.wait_ge(made, 1)
            sp.dma_start(table.rearrange("(t p) f -> p t f", p=P), rows[:, :, :]).then_inc(stored, 16)
            sp.wait_ge(stored, 16)
    turn_stage(nc, k, "turn_x", k.xcur, k.xT[:, None, :])


def sum_with_factors(nc, k, tag, order, *args, **more):
    with Stage(nc, f"factors{order.key}") as c:
        job = EdgeFactors(nc, c, k, order)
        job.start_stage()
        edge_sum_stage(nc, k, tag, *args, **more, jobs=[job])


def gcn_layer(nc, k, A, dram):
    xT = k.xT[:, :]
    by_dst = k.orders[1]
    with Stage(nc, "gcn") as c:
        w = c.sb("w", [P, D])
        bias = c.sb("bias", [P, D])
        acc = c.sb("acc", [P, NT, D])
        load_weights_stage(nc, k, "gcn_load", [
            (w[:, :], A["L1_gnn_W"]), (bias[:, :], A["L1_gnn_b"][None, :].to_broadcast([P, D]))])
        table_stage(nc, k, "gcn_table", [piece(0, D, [(xT, w[:, :])]),
                                         piece(0, D, [(xT, w[:, :])], target=acc)],
                    [(dram["narrow"], 0, D)], D, scale=k.dinv_loop)
        sum_with_factors(nc, k, "sum_gcn", k.orders[0], by_dst, by_dst.other, dram["narrow"][:, :], D, acc)
        layer_norm_stage(nc, k, "norm1", acc[:, :, :], scale=k.dinv_loop, bias=bias)
    turn_stage(nc, k, "turn1", k.xcur, k.xT[:, None, :])


def rgcn_layer(nc, k, A, dram):
    xT = k.xT[:, :]
    S = S2 + 1
    with Stage(nc, "rgcn") as c:
        acc = c.sb("acc", [P, NT, D])
        for layer in (0, 1):
            with Stage(nc, f"rgcn{layer}") as d:
                w = d.sb("w", [P, S, D])
                bias = d.sb("bias", [P, S, D])
                load_weights_stage(nc, k, f"rgcn_load{layer}", [
                    (w[:, :, :], A["L2_gnn_rgcn_weights"][layer].rearrange("s f g -> f s g")),
                    (bias[:, :, :].rearrange("p s g -> p (s g)"),
                     A["L2_gnn_rgcn_biases"][layer:layer + 1].rearrange("o s g -> o (s g)").to_broadcast([P, S * D]))])
                pieces = []
                for s in range(0, S2, 4):
                    n = min(4, S2 - s)
                    pieces.append(piece(s * D, n * D, [(xT, w[:, s:s + n, :].rearrange("p s g -> p (s g)"))],
                                        bias=bias[:, s:s + n, :].rearrange("p s g -> p (s g)")))
                pieces.append(piece(0, D, [(xT, w[:, S2, :])], bias=bias[:, S2, :], target=acc))
                table_stage(nc, k, f"rgcn_table{layer}", pieces,
                            [(dram["by_src"], 0, R * D), (dram["by_dst"], R * D, R * D)], S2 * D)
            scaled_by = k.factor[:, :, 0:1]
            for o, name in zip(k.orders, ("by_src", "by_dst")):
                args = (o, o.row, dram[name].rearrange("n (r f) -> (n r) f", f=D), D, acc, o.coef)
                if layer == 0 and name == "by_src":
                    sum_with_factors(nc, k, f"sum_rgcn{layer}_{name}", k.orders[1], *args, scaled_by=scaled_by)
                else:
                    edge_sum_stage(nc, k, f"sum_rgcn{layer}_{name}", *args, scaled_by=scaled_by)
                scaled_by = None
            if layer == 0:
                turn_stage(nc, k, "turn_rgcn", acc, k.xT[:, None, :], relu=True)
        layer_norm_stage(nc, k, "norm2", acc[:, :, :])
    turn_stage(nc, k, "turn2", k.xcur, k.xT[:, None, :])


def neighbour_layer(nc, k, A, dram):
    xT = k.xT[:, :]
    by_dst = k.orders[1]
    with Stage(nc, "neighbour") as c:
        w = c.sb("w", [P, 2, D])
        wT = c.sb("wT", [P, 2, D])
        bias = c.sb("bias", [P, 2, D])
        acc = c.sb("acc", [P, NT, D])
        load_weights_stage(nc, k, "neighbour_load", [
            (w[:, 0, :], A["L3_gnn_W_neigh"]), (w[:, 1, :], A["L3_gnn_W_self"]),
            (bias[:, 0, :], A["L3_gnn_b_neigh"][None, :].to_broadcast([P, D])),
            (bias[:, 1, :], A["L3_gnn_b_self"][None, :].to_broadcast([P, D]))])
        with Stage(nc, "neighbour_turn") as d:
            ps = d.psum("ps", [P, 2, 512])
            (turned,) = d.sems("turned")
            block = d.block()

            @block.tensor
            def _(pe):
                for n in (0, 1):
                    last = nc.tensor.transpose(ps[:, n, 0:D], w[:, n, :], k.ident[:, :])
                last.then_inc(turned, 1)

            @block.vector
            def _(dve):
                nc.vector.tensor_tensor(bias[:, 0, :], bias[:, 0, :], bias[:, 1, :], ALU.add)
                dve.wait_ge(turned, 1)
                nc.vector.tensor_copy(wT[:, :, :], ps[:, :, 0:D])
        table_stage(nc, k, "neighbour_table", [piece(0, D, [(xT, wT[:, 0, :])]),
                                               piece(0, D, [(xT, wT[:, 1, :])], bias=bias[:, 0, :], target=acc)],
                    [(dram["narrow"], 0, D)], D)
        edge_sum_stage(nc, k, "sum_neighbour", by_dst, by_dst.other, dram["narrow"][:, :], D, acc)
        layer_norm_stage(nc, k, "norm3", acc[:, :, :])


def store_stage(nc, k, out):
    with Stage(nc, "store") as c:
        (stored,) = c.sems("stored")
        block = c.block()

        @block.sync
        def _(sp):
            sp.dma_start(out[0:(NT - 1) * P, :].rearrange("(t p) f -> p t f", p=P),
                         k.xcur[:, 0:NT - 1, :]).then_inc(stored, 16)
            sp.dma_start(out[(NT - 1) * P:N, :], k.xcur[0:LAST, NT - 1, :]).then_inc(stored, 16)
            sp.wait_ge(stored, 32)


def gnn_kernel(nc, A, out):
    dram = {name: nc.dram_tensor(name, (NP, width), F32, kind="Internal").ap()
            for name, width in (("x_scaled", D), ("arma1", K * HID), ("arma2", K * D), ("narrow", D),
                                ("by_src", R * D), ("by_dst", R * D))}
    with ExitStack() as c:
        k = setup(nc, c)
        with Stage(nc, "graph") as g:
            sort_inputs(g, k.orders[0])
            with Stage(nc, "lists") as h:
                k.edges = h.sb("edges", [P, 3, EC], I32)
                load_stage(nc, k, A)
                sort_by_dst(nc, k)
                rank_stage(nc, k, k.orders[0])
            arma_layer(nc, k, A, dram)
        gcn_layer(nc, k, A, dram)
        rgcn_layer(nc, k, A, dram)
        neighbour_layer(nc, k, A, dram)
        store_stage(nc, k, out)


NAMES = ["x", "src", "dst", "edge_type_9",
         "L0_gnn_init_w1", "L0_gnn_w1", "L0_gnn_root_w1", "L0_gnn_b1",
         "L0_gnn_init_w2", "L0_gnn_w2", "L0_gnn_root_w2", "L0_gnn_b2",
         "L0_gnn_gamma1", "L0_gnn_beta1", "L0_gnn_gamma2", "L0_gnn_beta2",
         "L1_gnn_W", "L1_gnn_b", "L2_gnn_rgcn_weights", "L2_gnn_rgcn_biases",
         "L3_gnn_W_neigh", "L3_gnn_b_neigh", "L3_gnn_W_self", "L3_gnn_b_self"]


def kernel(**inputs):
    import numpy as np
    import concourse.bacc as bacc
    from concourse.bass_utils import run_bass_kernel_spmd

    nc = bacc.Bacc("TRN2", target_bir_lowering=False, num_devices=1)
    arrays, args = {}, {}
    for name in NAMES:
        a = np.ascontiguousarray(inputs[name])
        arrays[f"in_{name}"] = a
        args[name] = nc.dram_tensor(f"in_{name}", a.shape, mybir.dt.from_np(a.dtype), kind="ExternalInput").ap()
    out = nc.dram_tensor("out_0", (N, D), F32, kind="ExternalOutput").ap()
    gnn_kernel(nc, args, out)
    return run_bass_kernel_spmd(nc, [arrays], core_ids=[0]).results[0]["out_0"]
```
